# Optimizing a Trainium2 kernel written in Bass

```python
import numpy as np
import jax
import jax.numpy as jnp

def _softmax(x, axis=-1):
    return jax.nn.softmax(x, axis=axis)

def _gelu(x):
    return jax.nn.gelu(x, approximate=True)

def _silu(x):
    return jax.nn.silu(x)

def _sigmoid(x):
    return jax.nn.sigmoid(x)

def _layernorm(x, axis=-1, eps=1e-05):
    m = jnp.mean(x, axis=axis, keepdims=True)
    v = jnp.var(x, axis=axis, keepdims=True)
    return (x - m) / jnp.sqrt(v + eps)

def _scatter_add(tgt, idx, src, axis=0):
    return tgt.at[idx].add(src)

def _segment_sum(src, seg, n):
    return jax.ops.segment_sum(src, seg, n)
kernel_name = 'mk_gnn_preln_d2_gnn_r64_934a79'

def setup_inputs(seed: int=0):
    np.random.seed(seed)
    _w = jnp.asarray

    def _rec_inputs():
        import jax
        import jax.numpy as jnp
        _gk = jax.random.key(seed)
        x = 0.0001712 + 1 * jax.random.normal(jax.random.fold_in(_gk, 1), (100000, 16), jnp.float32)
        src = jax.random.randint(jax.random.fold_in(_gk, 2), (50000,), 0, 100000, jnp.int32)
        dst = jax.random.randint(jax.random.fold_in(_gk, 3), (50000,), 0, 100000, jnp.int32)
        _o = jnp.argsort(dst, stable=True)
        src = src[_o]
        dst = dst[_o]
        edge_attr_16 = -0.00010739 + 0.99994 * jax.random.normal(jax.random.fold_in(_gk, 12), (50000, 16), jnp.float32)
        edge_type_90 = jax.random.randint(jax.random.fold_in(_gk, 14), (50000,), 0, 90, jnp.int32)
        edge_weight = jax.random.uniform(jax.random.fold_in(_gk, 15), (50000,), jnp.float32, 0.0, 0.999998)
        return (x, src, dst, edge_attr_16, edge_type_90, edge_weight)
    x, src, dst, edge_attr_16, edge_type_90, edge_weight = _rec_inputs()

    def _L0_gnn_setup():
        import jax, jax.numpy as jnp
        import numpy as np
        N_NODES = 50000
        N_EDGES = 12500
        IN_CH = 16
        HIDDEN = [128, 128, 128]
        OUT_CH = 16
        SELF_LOOP_W = 2.0

        def _glorot(key, fan_in, fan_out):
            s = jnp.sqrt(6.0 / (fan_in + fan_out))
            return jax.random.uniform(key, (fan_in, fan_out), jnp.float32, -s, s)

        def _gcn_norm(edge_index, edge_attr, n):
            src = jnp.concatenate([edge_index[0], jnp.arange(n, dtype=edge_index.dtype)])
            dst = jnp.concatenate([edge_index[1], jnp.arange(n, dtype=edge_index.dtype)])
            w = jnp.concatenate([edge_attr, jnp.full((n,), SELF_LOOP_W, edge_attr.dtype)])
            deg = jax.ops.segment_sum(w, dst, num_segments=n)
            dinv = jnp.where(deg > 0, jax.lax.rsqrt(jnp.where(deg > 0, deg, 1.0)), 0.0)
            norm = dinv[src] * w * dinv[dst]
            return (src, dst, norm)

        def _gcn_conv(x, src, dst, norm, w, b, n):
            h = x @ w
            msg = norm[:, None] * h[src]
            return jax.ops.segment_sum(msg, dst, num_segments=n) + b
        key = jax.random.key(seed)
        ks = jax.random.split(key, 12)
        x = jax.random.normal(ks[0], (N_NODES, IN_CH), jnp.float32)
        edge_index = jax.random.randint(ks[1], (2, N_EDGES), 0, N_NODES, jnp.int64)
        edge_attr = jax.random.uniform(ks[2], (N_EDGES,), jnp.float32)
        dims = [IN_CH] + HIDDEN + [OUT_CH]
        inp = {'x': x, 'edge_index': edge_index, 'edge_attr': edge_attr}
        for i in range(4):
            inp[f'w{i}'] = _glorot(ks[3 + i], dims[i], dims[i + 1])
            inp[f'b{i}'] = jnp.zeros((dims[i + 1],), jnp.float32)
        return inp
    _L0_gnn_all = _L0_gnn_setup()
    _L0_gnn_in = {k: v for k, v in _L0_gnn_all.items() if k in ('w0', 'b0', 'w1', 'b1', 'w2', 'b2', 'w3', 'b3')}
    del _L0_gnn_all

    def _L1_gnn_setup():
        import jax, jax.numpy as jnp
        import numpy as np
        N, E, IN, OUT, R, B = (50000, 12500, 16, 16, 90, 30)
        key = jax.random.key(seed)
        ks = jax.random.split(key, 9)
        h = jax.random.normal(ks[0], (N, IN), dtype=jnp.float32)
        he = jax.random.normal(ks[1], (E, IN), dtype=jnp.float32)
        Ws = jax.random.normal(ks[2], (OUT, IN), dtype=jnp.float32) * 0.1
        Wa = jax.random.normal(ks[3], (1, 3 * OUT), dtype=jnp.float32) * 0.1
        weight = jax.random.normal(ks[4], (B, IN, OUT), dtype=jnp.float32) * 0.1
        w_comp = jax.random.normal(ks[5], (R, B), dtype=jnp.float32) * 0.1
        src = jax.random.randint(ks[6], (E,), 0, N)
        dst = jax.random.randint(ks[7], (E,), 0, N)
        rel_type = jax.random.randint(ks[8], (E,), 0, R)
        return {'h': h, 'he': he, 'Ws': Ws, 'Wa': Wa, 'weight': weight, 'w_comp': w_comp, 'src': src, 'dst': dst, 'rel_type': rel_type}
    _L1_gnn_all = _L1_gnn_setup()
    _L1_gnn_in = {k: v for k, v in _L1_gnn_all.items() if k in ('Ws', 'Wa', 'weight', 'w_comp')}
    del _L1_gnn_all
    return {'x': x, 'src': src, 'dst': dst, 'edge_attr_16': edge_attr_16, 'edge_type_90': edge_type_90, 'edge_weight': edge_weight, 'L0_gnn_w0': _L0_gnn_in['w0'], 'L0_gnn_b0': _L0_gnn_in['b0'], 'L0_gnn_w1': _L0_gnn_in['w1'], 'L0_gnn_b1': _L0_gnn_in['b1'], 'L0_gnn_w2': _L0_gnn_in['w2'], 'L0_gnn_b2': _L0_gnn_in['b2'], 'L0_gnn_w3': _L0_gnn_in['w3'], 'L0_gnn_b3': _L0_gnn_in['b3'], 'L1_gnn_Ws': _L1_gnn_in['Ws'], 'L1_gnn_Wa': _L1_gnn_in['Wa'], 'L1_gnn_weight': _L1_gnn_in['weight'], 'L1_gnn_w_comp': _L1_gnn_in['w_comp']}

def reference(x, src, dst, edge_attr_16, edge_type_90, edge_weight, L0_gnn_w0, L0_gnn_b0, L0_gnn_w1, L0_gnn_b1, L0_gnn_w2, L0_gnn_b2, L0_gnn_w3, L0_gnn_b3, L1_gnn_Ws, L1_gnn_Wa, L1_gnn_weight, L1_gnn_w_comp):
    import jax
    import jax.numpy as jnp

    def _L0_gnn_ref(x, edge_index, edge_attr, w0, b0, w1, b1, w2, b2, w3, b3):
        import jax, jax.numpy as jnp
        import numpy as np
        N_NODES = 50000
        N_EDGES = 12500
        IN_CH = 16
        HIDDEN = [128, 128, 128]
        OUT_CH = 16
        SELF_LOOP_W = 2.0

        def _glorot(key, fan_in, fan_out):
            s = jnp.sqrt(6.0 / (fan_in + fan_out))
            return jax.random.uniform(key, (fan_in, fan_out), jnp.float32, -s, s)

        def _gcn_norm(edge_index, edge_attr, n):
            src = jnp.concatenate([edge_index[0], jnp.arange(n, dtype=edge_index.dtype)])
            dst = jnp.concatenate([edge_index[1], jnp.arange(n, dtype=edge_index.dtype)])
            w = jnp.concatenate([edge_attr, jnp.full((n,), SELF_LOOP_W, edge_attr.dtype)])
            deg = jax.ops.segment_sum(w, dst, num_segments=n)
            dinv = jnp.where(deg > 0, jax.lax.rsqrt(jnp.where(deg > 0, deg, 1.0)), 0.0)
            norm = dinv[src] * w * dinv[dst]
            return (src, dst, norm)

        def _gcn_conv(x, src, dst, norm, w, b, n):
            h = x @ w
            msg = norm[:, None] * h[src]
            return jax.ops.segment_sum(msg, dst, num_segments=n) + b
        n = x.shape[0]
        src, dst, norm = _gcn_norm(edge_index, edge_attr, n)
        ws = [(w0, b0), (w1, b1), (w2, b2), (w3, b3)]
        for i, (w, b) in enumerate(ws):
            x = _gcn_conv(x, src, dst, norm, w, b, n)
            if i < len(ws) - 1:
                x = jax.nn.relu(x)
        return x

    def _L1_gnn_ref(h, he, Ws, Wa, weight, w_comp, src, dst, rel_type):
        import jax, jax.numpy as jnp
        import numpy as np
        N, E, IN, OUT, R, B = (50000, 12500, 16, 16, 90, 30)
        n_nodes, in_dim = h.shape
        num_bases, _, out_dim = weight.shape
        num_rels = w_comp.shape[0]
        V = weight.reshape(in_dim, num_bases, out_dim)
        W_rel = jnp.matmul(w_comp, V).reshape(num_rels, in_dim, out_dim)
        h_src = h[src]
        z_src = h_src @ Ws.T
        z_dst = h[dst] @ Ws.T
        z_e = he @ Ws.T
        e = jnp.concatenate([z_src, z_e, z_dst], axis=1) @ Wa.T
        msg = jnp.einsum('ei,eio->eo', h_src, W_rel[rel_type]) * e
        h_out = jax.ops.segment_sum(msg, dst, num_segments=n_nodes)
        return h_out
    edge_index = jnp.stack([src, dst])
    h = jnp.maximum(_layernorm(x, axis=-1), 0.0)
    x = x + _L0_gnn_ref(h, edge_index, edge_weight, L0_gnn_w0, L0_gnn_b0, L0_gnn_w1, L0_gnn_b1, L0_gnn_w2, L0_gnn_b2, L0_gnn_w3, L0_gnn_b3)
    h = jnp.maximum(_layernorm(x, axis=-1), 0.0)
    x = x + _L1_gnn_ref(h, edge_attr_16, L1_gnn_Ws, L1_gnn_Wa, L1_gnn_weight, L1_gnn_w_comp, src, dst, edge_type_90)
    return x

_drawn_inputs = setup_inputs


def setup_inputs(seed=0):
    import zlib

    import numpy as np

    out = dict(_drawn_inputs(seed))
    spreads = {'L0_gnn_b0': (0.0, 0.1),
     'L0_gnn_b1': (0.0, 0.1),
     'L0_gnn_b2': (0.0, 0.1),
     'L0_gnn_b3': (0.0, 0.1)}
    factors = {'edge_weight': 2.792}
    for name, (base, spread) in spreads.items():
        noise = np.random.default_rng([zlib.crc32(name.encode()), seed]).standard_normal(out[name].shape)
        drawn = base * np.exp(spread * noise) if base else spread * noise
        out[name] = jnp.asarray(drawn.astype(out[name].dtype))
    for name, factor in factors.items():
        out[name] = (out[name] * factor).astype(out[name].dtype)
    return out
```

```python
from contextlib import ExitStack

import numpy as np
import concourse.bass as bass
from concourse import mybir

F32 = mybir.dt.float32
I32 = mybir.dt.int32
ALU = mybir.AluOpType
ACT = mybir.ActivationFunctionType
AX = mybir.AxisListType

P = 128
N = 100000
E = 50000
C = 16
H = 128
R = 90
B = 30
COLS = 5
BN = P * COLS
NB = 158
NP = NB * BN
WN = 160
WB = BN // WN
WP = WN // COLS
WQ = 5
NWIN = WQ * P
BC = COLS * C
FULL = N // BN
REST = (N - FULL * BN) // COLS
EP = 125
ET = E // EP
EG = 8
NCH = ET // EG
LAST = E - P
SKIP = 1 << 21
HEAD = 6


class Step:

    def __init__(self, i, c=0):
        self.i, self.c = (i + c // 2, c % 2) if isinstance(i, int) else (i, c)
        if isinstance(i, int):
            self.i, self.c = (2 * i + c) // 2, (2 * i + c) % 2
        self.static = isinstance(i, int)

    @property
    def n(self):
        return self.i * 2 + self.c

    @property
    def par(self):
        return self.c % 2

    @property
    def round(self):
        return self.i + self.c // 2

    def back(self, k):
        return Step(self.i, self.c - k)

    def has(self, count):
        return not self.static or 0 <= self.n < count


def run_steps(eng, step, count, drain=0):
    pairs = count // 2
    for t in range(HEAD):
        step(Step(0, t))
    with eng.Fori(HEAD // 2, pairs) as i:
        step(Step(i, 0))
        step(Step(i, 1))
    for t in range(2 * pairs, count + drain):
        step(Step(0, t))


def hold(eng, sem, value):
    eng.wait_ge(sem, value)
    eng.nop(nofuse=True)


class Chain:

    def __init__(self, eng, sem, n=0):
        self.eng, self.sem, self.n = eng, sem, n

    def __call__(self, ins):
        self.n += 1
        ins.then_inc(self.sem, 1)
        self.eng.wait_ge(self.sem, self.n)


def build(nc, x, src, dst, edge_attr, edge_type, edge_weight, w0, b0, w1, b1, w2, b2, w3, b3,
          Ws, Wa, weight, w_comp, out):
    top = ExitStack()
    with top:
        def sb(name, shape, dt=F32, ctx=top):
            return ctx.enter_context(nc.sbuf_tensor(name, shape, dt))

        def ps(name, shape, ctx):
            return ctx.enter_context(nc.psum_tensor(name, shape, F32))

        def sem(name):
            return top.enter_context(nc.semaphore(name))

        yn_tab = nc.dram_tensor("y_narrow", (NP, C), F32).ap()
        y1_tab = nc.dram_tensor("y1", (NP, H), F32).ap()
        y2_tab = nc.dram_tensor("y2", (NP, H), F32).ap()
        msg_a = nc.dram_tensor("msg_a", (E, C), F32).ap()
        msg_b = nc.dram_tensor("msg_b", (E, C), F32).ap()
        deg_tab = nc.dram_tensor("deg", (NP, 1), F32).ap()
        dot_tab = nc.dram_tensor("dst_dot", (NP, 1), F32).ap()
        sum_tab = nc.dram_tensor("sum_narrow", (NP, C), F32).ap()
        u_tab = nc.dram_tensor("own_wide", (NP, H), F32).ap()
        rel_tab = nc.dram_tensor("rel_w", (C * R, C), F32).ap()

        X = sb("X", [P, NB * BC])
        Y = sb("Y", [P, NB * BC])
        ident = sb("ident", [P, P])
        nodes = sb("nodes", [P, WN])
        ones = sb("ones", [P, P])
        dst_win = sb("dst_win", [P, NWIN])
        w_win = sb("w_win", [P, NWIN])
        src_win = sb("src_win", [P, NWIN], I32)
        start16 = sb("start16", [P, WQ], I32)
        covered = sb("covered", [P, 1])
        covered_i = sb("covered_i", [P, 1], I32)
        part = sb("part", [P, 1])
        dinv = sb("dinv", [P, NB * COLS])
        W1 = sb("W1", [H, H])
        W2 = sb("W2", [H, H])
        W3 = sb("W3", [H, C])
        bias1 = sb("bias1", [P, H])
        bias2 = sb("bias2", [P, H])
        bias3 = sb("bias3", [P, C])
        W0x = sb("W0x", [BC + 1, COLS * H])
        v_rel = sb("v_rel", [P, 3 * C])
        src_edge = sb("src_edge", [EP, ET], I32)
        type_edge = sb("type_edge", [EP, ET])
        Wr = sb("Wr", [R, C * C])

        def blocks(tab, width):
            return tab.rearrange("(b p c) f -> p b (c f)", p=P, c=COLS)

        xv = blocks(x[0:FULL * BN, :], C)
        xr = x[FULL * BN:N, :].rearrange("(p c) f -> p (c f)", c=COLS)
        ov = blocks(out[0:FULL * BN, :], C)
        orr = out[FULL * BN:N, :].rearrange("(p c) f -> p (c f)", c=COLS)
        Xb = X[:, :].rearrange("p (b g) -> p b g", g=BC)
        Yb = Y[:, :].rearrange("p (b g) -> p b g", g=BC)

        with ExitStack() as ph:
            def t(name, shape, dt=F32):
                return sb("su_" + name, shape, dt, ph)
            nodes_i = t("nodes_i", [P, WN], I32)
            part_i = t("part_i", [P, 1], I32)
            first_i = t("first_i", [P, WQ], I32)
            first = t("first", [P, WQ])
            base_i = t("base_i", [P, NWIN], I32)
            base = t("base", [P, NWIN])
            head_i = t("head_i", [1, ET], I32)
            head = t("head", [1, ET])
            below = t("below", [P, ET])
            cnt = t("cnt", [P, WQ])
            row_i = t("row_i", [P, WQ], I32)
            row = t("row", [P, WQ])
            runs = t("runs", [P, WQ, EP], I32)
            runs_f = t("runs_f", [P, WQ, EP])
            begin = t("begin", [P, WQ])
            begin_i = t("begin_i", [P, WQ], I32)
            lanes_s = t("lanes_s", [P, WQ, P], I32)
            lanes_d = t("lanes_d", [P, WQ, P], I32)
            lanes_w = t("lanes_w", [P, WQ, P])
            lanes_sf = t("lanes_sf", [P, WQ, P])
            lanes_df = t("lanes_df", [P, WQ, P])
            valid = t("valid", [P, NWIN])
            tmp = t("tmp", [P, NWIN])
            total = t("total", [P, 1])
            type_i = t("type_i", [EP, ET], I32)
            bases = t("bases", [B, C * C])
            comp = t("comp", [B, R])
            comp_r = t("comp_r", [R, B])
            rel_mix = t("rel_mix", [R, C * C])
            rel_in = t("rel_in", [R, C * C])
            wa = t("wa", [C, 3])
            wa_b = t("wa_b", [C, 3, P])
            ws = t("ws", [C, C])
            p_head = ps("p_head", [P, 512], ph)
            p_win = ps("p_win", [P, 2, 512], ph)
            p_misc = ps("p_misc", [P, 512], ph)

            s_load = sem("su_loaded")
            s_heads = sem("su_heads_loaded")
            s_relw = sem("su_relation_inputs_loaded")
            s_iota = sem("su_iota")
            s_d = sem("su_dve")
            s_id = sem("su_identity_ready")
            s_hf = sem("su_heads_float")
            s_hb = sem("su_heads_broadcast")
            s_row = sem("su_rows_ready")
            s_runs = sem("su_runs_gathered")
            s_beg = sem("su_begins_ready")
            s_lanes = sem("su_lanes_gathered")
            s_lf = sem("su_lanes_float")
            s_tr = sem("su_windows_turned")
            s_tc = sem("su_windows_copied")
            s_tot = sem("su_valid_counted")
            s_sum = sem("su_valid_summed")
            s_rm = sem("su_relation_matrix")
            s_rst = sem("su_relation_stored")
            s_rld = sem("su_relation_loaded")
            s_rc = sem("su_relation_copied")
            s_cT = sem("su_comp_turned")

            dst_rows = dst.rearrange("(t p) -> t p", p=EP)
            with nc.Block() as block:
                @block.sync
                def _(sp):
                    sp.dma_start(head_i[:, :], dst.rearrange("(t p) -> p t", p=EP)[0:1, :],
                                 allow_slow_non_contiguous=True).then_inc(s_heads, 16)
                    sp.dma_start(bases[:, :].rearrange("b (i o) -> b i o", i=C),
                                 weight.rearrange("b i o -> (b i o)").rearrange("(i b o) -> b i o", i=C, b=B)
                                 ).then_inc(s_relw, 16)
                    sp.dma_start(comp_r[:, :], w_comp).then_inc(s_relw, 16)
                    sp.dma_start(wa[:, :], Wa.rearrange("a (k o) -> o (a k)", k=3),
                                 allow_slow_non_contiguous=True).then_inc(s_relw, 16)
                    sp.dma_start(ws[:, :], Ws).then_inc(s_relw, 16)
                    sp.dma_start(src_edge[:, :], src.rearrange("(p t) -> p t", t=ET)).then_inc(s_load, 16)
                    sp.dma_start(type_i[:, :], edge_type.rearrange("(p t) -> p t", t=ET)).then_inc(s_load, 16)
                    sp.dma_start(W1[:, :], w1).then_inc(s_load, 16)
                    sp.dma_start(W2[:, :], w2).then_inc(s_load, 16)
                    sp.dma_start(W3[:, :], w3).then_inc(s_load, 16)
                    for tile, vec in ((bias1, b1), (bias2, b2), (bias3, b3)):
                        sp.dma_start(tile[:, :], vec.rearrange("(a f) -> a f", a=1).broadcast_to([P, vec.shape[0]])
                                     ).then_inc(s_load, 16)
                    sp.wait_ge(s_iota, 4)
                    for c in range(COLS):
                        sp.dma_start(W0x[c * C:(c + 1) * C, c * H:(c + 1) * H], w0).then_inc(s_load, 16)
                        sp.dma_start(W0x[BC:BC + 1, c * H:(c + 1) * H],
                                     b0.rearrange("(a f) -> a f", a=1)).then_inc(s_load, 16)
                    sp.wait_ge(s_rm, 1)
                    sp.dma_start(rel_tab.rearrange("(i r) o -> r i o", r=R),
                                 rel_mix[:, :].rearrange("r (i o) -> r i o", i=C)).then_inc(s_rst, 16)
                    sp.wait_ge(s_rst, 16)
                    sp.dma_start(rel_in[:, :], rel_tab.rearrange("(r i) o -> r (i o)", i=C)).then_inc(s_rld, 16)
                    sp.wait_ge(s_load, 16 * 20)
                    sp.wait_ge(s_rld, 16)

                @block.scalar
                def _(act):
                    act.wait_ge(s_iota, 5)
                    act.dma_start(Xb[:, 0:FULL, :], xv).then_inc(s_load, 16)
                    act.dma_start(Xb[0:REST, FULL, :], xr).then_inc(s_load, 16)
                    act.wait_ge(s_load, 16 * 20)

                @block.gpsimd
                def _(pool):
                    pool.iota(nodes_i[:, :], pattern=[[1, WN]], base=0, channel_multiplier=0).then_inc(s_iota, 1)
                    pool.iota(part_i[:, :], pattern=[[0, 1]], base=0, channel_multiplier=1).then_inc(s_iota, 1)
                    pool.iota(first_i[:, :], pattern=[[WN * P, WQ]], base=0, channel_multiplier=WN).then_inc(s_iota, 1)
                    pool.memset(W0x[:, :], 0.0).then_inc(s_iota, 1)
                    pool.memset(Xb[:, FULL:NB, :], 0.0).then_inc(s_iota, 1)
                    pool.iota(base_i[:, :], pattern=[[WN, NWIN]], base=0, channel_multiplier=0).then_inc(s_iota, 1)
                    pool.memset(ones[:, :], 1.0).then_inc(s_iota, 1)
                    pool.wait_ge(s_row, 1)
                    for q in range(WQ):
                        pool.indirect_dma_start(
                            out=runs[:, q, :], out_offset=None, in_=dst_rows,
                            in_offset=bass.IndirectOffsetOnAxis(ap=row_i[:, q:q + 1], axis=0)).then_inc(s_runs, 16)
                    pool.wait_ge(s_beg, 1)
                    for tile, vec in ((lanes_d, dst), (lanes_s, src), (lanes_w, edge_weight)):
                        for q in range(WQ):
                            pool.indirect_dma_start(
                                out=tile[:, q, :], out_offset=None, in_=vec.rearrange("(a e) -> a e", a=1),
                                in_offset=bass.IndirectOffsetOnAxis(ap=begin_i[:, q:q + 1], axis=1)
                                ).then_inc(s_lanes, 16)
                    pool.wait_ge(s_lanes, 16 * 3 * WQ)

                @block.vector
                def _(dve):
                    c = Chain(dve, s_d)
                    dve.wait_ge(s_iota, 7)
                    c(dve.tensor_copy(nodes[:, :], nodes_i[:, :]))
                    c(dve.tensor_copy(part[:, :], part_i[:, :]))
                    dve.tensor_scalar(ident[:, :], nodes[:, 0:P], part[:, 0:1], None, ALU.is_equal).then_inc(s_id, 1)
                    dve.wait_ge(s_heads, 16)
                    dve.tensor_copy(head[:, :], head_i[:, :]).then_inc(s_hf, 1)
                    c(dve.tensor_copy(first[:, :], first_i[:, :]))
                    c(dve.tensor_copy(base[:, :], base_i[:, :]))
                    dve.wait_ge(s_hb, 1)
                    for q in range(WQ):
                        c(dve.tensor_scalar(below[:, :], p_head[:, 0:ET], first[:, q:q + 1], None, ALU.is_lt))
                        c(dve.tensor_reduce(cnt[:, q:q + 1], below[:, :], AX.X, ALU.add))
                    c(dve.tensor_scalar(row[:, :], cnt[:, :], -1.0, 0.0, ALU.add, ALU.max))
                    dve.tensor_copy(row_i[:, :], row[:, :]).then_inc(s_row, 1)
                    dve.wait_ge(s_runs, 16 * WQ)
                    c(dve.tensor_copy(runs_f[:, :, :], runs[:, :, :]))
                    for q in range(WQ):
                        c(dve.tensor_scalar(below[:, 0:EP], runs_f[:, q, :], first[:, q:q + 1], None, ALU.is_lt))
                        c(dve.tensor_reduce(cnt[:, q:q + 1], below[:, 0:EP], AX.X, ALU.add))
                    c(dve.scalar_tensor_tensor(out=begin[:, :], in0=row[:, :], scalar=float(EP), in1=cnt[:, :],
                                               op0=ALU.mult, op1=ALU.add))
                    c(dve.tensor_scalar(begin[:, :], begin[:, :], float(LAST), None, ALU.min))
                    dve.tensor_copy(begin_i[:, :], begin[:, :]).then_inc(s_beg, 1)
                    c(dve.tensor_scalar(cnt[:, :], begin[:, :], float(C), None, ALU.mult))
                    c(dve.tensor_copy(start16[:, :], cnt[:, :]))
                    dve.wait_ge(s_cT, 1)
                    dve.tensor_copy(comp[:, :], p_misc[0:B, 0:R]).then_inc(s_rc, 1)
                    dve.tensor_copy(wa_b[:, :, :], wa[:, :].rearrange("o (k a) -> o k a", a=1)
                                    .broadcast_to([C, 3, P])).then_inc(s_rc, 1)
                    dve.wait_ge(s_cT, 2)
                    dve.tensor_copy(rel_mix[:, :], p_misc[0:R, 0:C * C]).then_inc(s_rm, 1)
                    dve.tensor_copy(v_rel[:, :], p_misc[:, C * C:C * C + 3 * C]).then_inc(s_rc, 1)
                    dve.wait_ge(s_load, 16 * 20)
                    dve.tensor_copy(type_edge[:, :], type_i[:, :]).then_inc(s_rc, 1)
                    dve.wait_ge(s_lanes, 16 * 3 * WQ)
                    dve.tensor_copy(lanes_df[:, :, :], lanes_d[:, :, :]).then_inc(s_lf, 1)
                    dve.tensor_copy(lanes_sf[:, :, :], lanes_s[:, :, :]).then_inc(s_lf, 1)
                    k = 0
                    for tile in (dst_win, tmp, w_win):
                        for half in range(2):
                            k += 1
                            dve.wait_ge(s_tr, k)
                            n = min(4, WQ - 4 * half) * P
                            dve.tensor_copy(tile[:, 512 * half:512 * half + n], p_win[:, half, 0:n]).then_inc(s_tc, 1)
                    dve.wait_ge(s_tc, 6)
                    c(dve.tensor_tensor(dst_win[:, :], dst_win[:, :], base[:, :], ALU.subtract))
                    c(dve.tensor_scalar(valid[:, :], dst_win[:, :], 0.0, None, ALU.is_ge))
                    c(dve.scalar_tensor_tensor(out=valid[:, :], in0=dst_win[:, :], scalar=float(WN), in1=valid[:, :],
                                               op0=ALU.is_lt, op1=ALU.mult))
                    dve.tensor_reduce(total[:, :], valid[:, :], AX.X, ALU.add).then_inc(s_tot, 1)
                    c(dve.tensor_scalar(valid[:, :], valid[:, :], -float(SKIP), float(SKIP), ALU.mult, ALU.add))
                    c(dve.tensor_tensor(tmp[:, :], tmp[:, :], valid[:, :], ALU.add))
                    c(dve.tensor_copy(src_win[:, :], tmp[:, :]))
                    dve.wait_ge(s_sum, 1)
                    c(dve.tensor_scalar(covered[:, :], p_head[:, 0:1], float(E), None, ALU.is_equal))
                    c(dve.tensor_copy(covered_i[:, :], covered[:, :]))
                    c(dve.tensor_scalar(w_win[:, :], w_win[:, :], covered[:, 0:1], None, ALU.mult))
                    dve.wait_ge(s_rld, 16)
                    c(dve.tensor_copy(Wr[:, :].rearrange("r (o i) -> r o i", o=C),
                                      rel_in[:, :].rearrange("r (i o) -> r o i", i=C)))

                @block.tensor
                def _(pe):
                    pe.wait_ge(s_id, 1)
                    pe.wait_ge(s_hf, 1)
                    pe.matmul(p_head[:, 0:ET], ones[0:1, :], head[:, :], start=True, stop=True).then_inc(s_hb, 1)
                    pe.wait_ge(s_relw, 64)
                    pe.transpose(p_misc[0:B, 0:R], comp_r[:, :], ident[0:R, 0:R]).then_inc(s_cT, 1)
                    pe.wait_ge(s_rc, 2)
                    pe.matmul(p_misc[0:R, 0:C * C], comp[:, :], bases[:, :], start=True, stop=True)
                    for k in range(3):
                        mm = pe.matmul(p_misc[:, C * C + k * C:C * C + (k + 1) * C], wa_b[:, k, :], ws[:, :],
                                       start=True, stop=True)
                    mm.then_inc(s_cT, 1)
                    pe.wait_ge(s_lf, 2)
                    k = 0
                    for tile in (lanes_df, lanes_sf, lanes_w):
                        for half in range(2):
                            if k >= 2:
                                pe.wait_ge(s_tc, k - 1)
                            k += 1
                            for q in range(4 * half, min(4 * half + 4, WQ)):
                                mm = pe.transpose(p_win[:, half, (q % 4) * P:(q % 4 + 1) * P], tile[:, q, :], ident[:, :])
                            mm.then_inc(s_tr, 1)
                    pe.wait_ge(s_tot, 1)
                    pe.matmul(p_head[:, 0:1], ones[:, :], total[:, :], start=True, stop=True).then_inc(s_sum, 1)

        s_oh = sem("wp_onehot_ready")
        s_mm = sem("wp_block_summed")
        s_fin = sem("wp_block_finished")
        s_f = sem("wp_finish_chain")
        s_msg = sem("wp_messages_staged")
        s_lane = [sem(f"rw_lanes_gathered{u}") for u in range(2)]
        s_turned = sem("rw_turned")
        s_copied = sem("rw_copied")
        visits = {"window": 0, "staged": 0, "chain": 0, "rewindow": 0}

        def window_pass(name, tables, scale, finish, links, oh_ctx):
            width = C * len(tables) or 1
            oh = sb(name + "_oh", [P, 2, WB, WN], F32, oh_ctx)
            msgs = sb(name + "_msgs", [P, 2, WB, width], F32, oh_ctx)
            acc = ps(name + "_acc", [P, 2, 512], oh_ctx)
            before = visits["window"] * NB
            staged_before = visits["staged"] * NB
            chain_before = visits["chain"]
            visits["window"] += 1
            visits["staged"] += 1 if tables else 0
            visits["chain"] += links * NB
            with nc.Block() as block:
                @block.vector
                def _(dve):
                    def onehot(b):
                        if not b.static or b.n >= 2:
                            dve.wait_ge(s_mm, b.n + (before - 1))
                        for w in range(WB):
                            j = b.n * WB + w
                            ins = dve.tensor_scalar(oh[:, b.par, w, :], nodes[:, :], dst_win[:, bass.ds(j, 1)],
                                                    scale(j), ALU.is_equal, ALU.mult)
                        ins.then_inc(s_oh, 1)

                    def step(t):
                        if t.has(NB):
                            onehot(t)
                        b = t.back(1)
                        if b.has(NB):
                            dve.wait_ge(s_mm, b.n + (before + 1))
                            finish(dve, b, acc[:, b.par, 0:COLS * width], chain_before).then_inc(s_fin, 1)
                    run_steps(dve, step, NB, 1)

                @block.tensor
                def _(pe):
                    def step(b):
                        hold(pe, s_oh, b.n + (before + 1))
                        if tables:
                            hold(pe, s_msg, b.n + (staged_before + 1))
                        if not b.static or b.n >= 2:
                            hold(pe, s_fin, b.n + (before - 1))
                        for w in range(WB):
                            for c in range(COLS):
                                mm = pe.matmul(acc[w * WP:(w + 1) * WP, b.par, c * width:(c + 1) * width],
                                               oh[:, b.par, w, c::COLS],
                                               msgs[:, b.par, w, :] if tables else ones[:, 0:1],
                                               start=True, stop=True, tile_position=(0, w * WP))
                        mm.then_inc(s_mm, 1)
                    run_steps(pe, step, NB)

                if tables:
                    @block.scalar
                    def _(act):
                        def step(b):
                            if not b.static or b.n >= 2:
                                hold(act, s_mm, b.n + (before - 1))
                            for k, tab in enumerate(tables):
                                ins = act.copy(msgs[:, b.par, :, k * C:(k + 1) * C], tab[:, bass.ds(b.n * WB, WB), :])
                            ins.then_inc(s_msg, 1)
                        run_steps(act, step, NB)

        def edge_gather(name, tab):
            with ExitStack() as ph:
                rows = sb(name + "_rows", [EP, 2, EG, C], F32, ph)
                idx = sb(name + "_idx", [EP, 2, EG], I32, ph)
                s_ix = sem(name + "_index_ready")
                s_g = [sem(f"{name}_rows_gathered{u}") for u in range(2)]
                s_st = [sem(f"{name}_rows_stored{u}") for u in range(2)]
                with nc.Block() as block:
                    @block.gpsimd
                    def _(pool):
                        def step(b):
                            if not b.static or b.n >= 2:
                                hold(pool, s_st[b.par], b.round * 16)
                            pool.tensor_copy(idx[:, b.par, :], src_edge[:, bass.ds(b.n * EG, EG)]).then_inc(s_ix, 1)
                            hold(pool, s_ix, b.n + 1)
                            for k in range(EG):
                                pool.indirect_dma_start(
                                    out=rows[:, b.par, k, :], out_offset=None, in_=tab,
                                    in_offset=bass.IndirectOffsetOnAxis(ap=idx[:, b.par, k:k + 1], axis=0)
                                    ).then_inc(s_g[b.par], 16)
                        run_steps(pool, step, NCH)

                    @block.sync
                    def _(sp):
                        def step(b):
                            sp.wait_ge(s_g[b.par], (b.round + 1) * 16 * EG)
                            sp.dma_start(msg_a.rearrange("(p t) f -> p (t f)", t=ET)[:, bass.ds(b.n * EG * C, EG * C)],
                                         rows[:, b.par, :, :].rearrange("p k f -> p (k f)")).then_inc(s_st[b.par], 16)
                        run_steps(sp, step, NCH)
                        for u in range(2):
                            sp.wait_ge(s_st[u], 16 * (NCH // 2))

        def rewindow(name, msg, win):
            with ExitStack() as ph:
                lanes = sb(name + "_lanes", [P, 2, P * C], F32, ph)
                turned = ps(name + "_turned", [P, 4, 512], ph)
                G = C // 4
                before = visits["rewindow"] * WQ * G
                lanes_before = [visits["rewindow"] * 16 * ((WQ + 1 - u) // 2) for u in range(2)]
                visits["rewindow"] += 1
                with nc.Block() as block:
                    @block.gpsimd
                    def _(pool):
                        for q in range(WQ):
                            if q >= 2:
                                pool.wait_ge(s_turned, before + G * (q - 1))
                            pool.indirect_dma_start(
                                out=lanes[:, q % 2, :], out_offset=None,
                                in_=msg.rearrange("e f -> (e f)").rearrange("(a g) -> a g", a=1),
                                in_offset=bass.IndirectOffsetOnAxis(ap=start16[:, q:q + 1], axis=1)
                                ).then_inc(s_lane[q % 2], 16)

                    @block.tensor
                    def _(pe):
                        for q in range(WQ):
                            pe.wait_ge(s_lane[q % 2], lanes_before[q % 2] + 16 * (q // 2 + 1))
                            for g in range(G):
                                n = q * G + g
                                if n >= 4:
                                    pe.wait_ge(s_copied, before + n - 3)
                                for f in range(4):
                                    mm = pe.transpose(turned[:, n % 4, f * P:(f + 1) * P],
                                                      lanes[:, q % 2, 4 * g + f::C], ident[:, :])
                                mm.then_inc(s_turned, 1)

                    @block.vector
                    def _(dve):
                        for n in range(WQ * G):
                            q, g = divmod(n, G)
                            dve.wait_ge(s_turned, before + n + 1)
                            dve.tensor_copy(win[:, q * P:(q + 1) * P, 4 * g:4 * g + 4],
                                            turned[:, n % 4, :].rearrange("p (f j) -> p j f", f=4)).then_inc(s_copied, 1)

        def layer_norm(name, store, scale_by):
            with ExitStack() as ph:
                GB = 40
                mean = sb(name + "_mean", [P, NB * COLS], F32, ph)
                var = sb(name + "_var", [P, NB * COLS], F32, ph)
                sq = sb(name + "_sq", [P, GB * BC], F32, ph)
                s_v = sem(name + "_dve")
                s_var = sem(name + "_variance_ready")
                s_sq = sem(name + "_root_ready")
                s_y = sem(name + "_rows_ready")
                s_store = sem(name + "_rows_stored")
                parts = [(k, min(k + GB, NB)) for k in range(0, NB, GB)]
                with nc.Block() as block:
                    @block.vector
                    def _(dve):
                        c = Chain(dve, s_v)
                        for k, (lo, hi) in enumerate(parts):
                            xs = X[:, lo * BC:hi * BC].rearrange("p (n f) -> p n f", f=C)
                            ys = Y[:, lo * BC:hi * BC].rearrange("p (n f) -> p n f", f=C)
                            qs = sq[:, 0:(hi - lo) * BC].rearrange("p (n f) -> p n f", f=C)
                            m = mean[:, lo * COLS:hi * COLS]
                            v = var[:, lo * COLS:hi * COLS]
                            shape = [P, (hi - lo) * COLS, C]
                            c(dve.tensor_reduce(m, xs, AX.X, ALU.add))
                            c(dve.tensor_scalar(m, m, 1.0 / C, None, ALU.mult))
                            c(dve.tensor_tensor(ys, xs, m.rearrange("p (n a) -> p n a", a=1).broadcast_to(shape),
                                                ALU.subtract))
                            c(dve.tensor_tensor(qs, ys, ys, ALU.mult))
                            c(dve.tensor_reduce(v, qs, AX.X, ALU.add))
                            dve.tensor_scalar(v, v, 1.0 / C, 1e-5, ALU.mult, ALU.add).then_inc(s_var, 1)
                            dve.wait_ge(s_sq, k + 1)
                            c(dve.reciprocal(v, v))
                            if scale_by is not None:
                                c(dve.tensor_tensor(v, v, scale_by[:, lo * COLS:hi * COLS], ALU.mult))
                            dve.scalar_tensor_tensor(out=ys, in0=ys, scalar=0.0,
                                                     in1=v.rearrange("p (n a) -> p n a", a=1).broadcast_to(shape),
                                                     op0=ALU.max, op1=ALU.mult).then_inc(s_y, 1)

                    @block.scalar
                    def _(act):
                        for k, (lo, hi) in enumerate(parts):
                            act.wait_ge(s_var, k + 1)
                            act.activation(var[:, lo * COLS:hi * COLS], var[:, lo * COLS:hi * COLS],
                                           ACT.Sqrt).then_inc(s_sq, 1)

                    @block.sync
                    def _(sp):
                        for k, (lo, hi) in enumerate(parts):
                            sp.wait_ge(s_y, k + 1)
                            sp.dma_start(blocks(store[lo * BN:hi * BN, :], C), Yb[:, lo:hi, :]).then_inc(s_store, 16)
                        sp.wait_ge(s_store, 16 * len(parts))

        def uncovered(eng):
            return eng.value_load(covered_i[0:1, 0:1], min_val=0, max_val=1) < 1

        s_in = sem("gp_inputs_loaded")
        s_before = sem("gp_target_prepared")
        s_link = sem("gp_chain")
        s_dg = sem("gp_diagonal_ready")
        s_row = sem("gp_targets_spread")
        s_same = sem("gp_index_ready")
        s_from = sem("gp_source_ready")
        s_rows = sem("gp_rows_gathered")
        s_rowmsg = sem("gp_messages_ready")
        s_comb = sem("gp_sums_ready")
        s_sum_out = sem("gp_sums_copied")
        s_add = sem("gp_sums_added")
        s_after = sem("gp_result_loaded")
        general_count = {"visits": 0, "before": 0, "after": 0, "from": 0, "rows": 0, "chain": 0}

        def general_path(name, width, target, before, after, tab=None, dots=False):
            with ExitStack() as ph:
                dst_i = sb(name + "_dst_i", [EP, ET], I32, ph)
                dst_e = sb(name + "_dst", [EP, ET], F32, ph)
                w_e = sb(name + "_w", [EP, ET], F32, ph)
                tri = sb(name + "_tri", [EP, EP], F32, ph)
                spare = sb(name + "_spare", [EP, 1], F32, ph)
                diag = sb(name + "_diag", [EP, EP], F32, ph)
                same = sb(name + "_same", [EP, EP], F32, ph)
                low = sb(name + "_low", [EP, EP], F32, ph)
                earlier = sb(name + "_earlier", [EP, 1], F32, ph)
                firsts = sb(name + "_firsts", [EP, 1], F32, ph)
                off = sb(name + "_off", [EP, 1], F32, ph)
                at_f = sb(name + "_at_f", [EP, 1], F32, ph)
                at = sb(name + "_at", [EP, 1], I32, ph)
                from_ = sb(name + "_from", [EP, 1], I32, ph)
                rows = sb(name + "_rows", [EP, width], F32, ph)
                rows_b = sb(name + "_rows_b", [EP, width], F32, ph)
                dot = sb(name + "_dot", [EP, 1], F32, ph)
                msg = sb(name + "_msg", [EP, width], F32, ph)
                comb = sb(name + "_comb", [EP, width], F32, ph)
                p_row = ps(name + "_p_row", [EP, 512], ph)
                p_comb = ps(name + "_p_comb", [EP, 512], ph)
                was = dict(general_count)
                visit = was["visits"]
                tiles = visit * ET
                K = 7
                with nc.Block() as block:
                    @block.sync
                    def _(sp):
                        with sp.If(uncovered(sp)):
                            sp.dma_start(dst_i[:, :], dst.rearrange("(p t) -> p t", t=ET)).then_inc(s_in, 16)
                            sp.dma_start(w_e[:, :], edge_weight.rearrange("(p t) -> p t", t=ET)).then_inc(s_in, 16)
                            for o, i in before:
                                sp.dma_start(o, i).then_inc(s_before, 16)
                            sp.wait_ge(s_add, 16 * (tiles + ET))
                            for o, i in after:
                                sp.dma_start(o, i).then_inc(s_after, 16)
                            if after:
                                sp.wait_ge(s_after, 16 * (was["after"] + len(after)))
                            sp.nop()

                    @block.gpsimd
                    def _(pool):
                        with pool.If(uncovered(pool)):
                            hold(pool, s_before, 16 * (was["before"] + len(before)))
                            with pool.Fori(0, ET) as t:
                                if tab is not None:
                                    pool.tensor_copy(from_[:, :], src_edge[:, bass.ds(t, 1)]).then_inc(s_from, 1)
                                    hold(pool, s_from, t + (was["from"] + 1))
                                    pool.indirect_dma_start(
                                        out=rows[:, :], out_offset=None, in_=tab,
                                        in_offset=bass.IndirectOffsetOnAxis(ap=from_[:, 0:1], axis=0)
                                        ).then_inc(s_rows, 16)
                                if dots:
                                    pool.tensor_copy(from_[:, :], dst_i[:, bass.ds(t, 1)]).then_inc(s_from, 1)
                                    hold(pool, s_from, t + (was["from"] + 1))
                                    pool.indirect_dma_start(
                                        out=dot[:, :], out_offset=None, in_=dot_tab,
                                        in_offset=bass.IndirectOffsetOnAxis(ap=from_[:, 0:1], axis=0)
                                        ).then_inc(s_rows, 16)
                                    for m, r in ((msg_a, rows), (msg_b, rows_b)):
                                        pool.dma_start(r[:, :], m.rearrange("(p t) f -> p (t f)", t=ET)
                                                       [:, bass.ds(t * C, C)]).then_inc(s_rows, 16)
                                hold(pool, s_same, t + (tiles + 1))
                                hold(pool, s_sum_out, t + (tiles + 1))
                                pool.indirect_dma_start(
                                    out=target, out_offset=bass.IndirectOffsetOnAxis(ap=at[:, 0:1], axis=0),
                                    in_=comb[:, :], in_offset=None, compute_op=ALU.add).then_inc(s_add, 16)
                                hold(pool, s_add, (t + (tiles + 1)) * 16)
                            pool.nop()

                    @block.tensor
                    def _(pe):
                        with pe.If(uncovered(pe)):
                            with pe.Fori(0, ET) as t:
                                hold(pe, s_dg, t + (tiles + 1))
                                pe.matmul(p_row[:, 0:EP], ones[0:EP, 0:EP], diag[:, :], start=True, stop=True
                                          ).then_inc(s_row, 1)
                                hold(pe, s_same, t + (tiles + 1))
                                hold(pe, s_rowmsg, t + (tiles + 1))
                                pe.matmul(p_comb[:, 0:width], same[:, :], msg[:, :], start=True, stop=True
                                          ).then_inc(s_comb, 1)
                            pe.nop()

                    @block.vector
                    def _(dve):
                        with dve.If(uncovered(dve)):
                            c = Chain(dve, s_link, was["chain"])
                            dve.wait_ge(s_in, 32 * (visit + 1))
                            c(dve.tensor_copy(dst_e[:, :], dst_i[:, :]))
                            c(dve.tensor_scalar(tri[:, :], nodes[0:EP, 0:EP], part[0:EP, 0:1], None, ALU.is_lt))
                            c(dve.tensor_scalar(spare[:, :], part[0:EP, :], float(N), None, ALU.add))
                            n0 = c.n
                            general_count["chain"] = n0 + ET * K
                            with dve.Fori(0, ET) as t:
                                def link(ins, k):
                                    ins.then_inc(s_link, 1)
                                    hold(dve, s_link, t * K + n0 + k)
                                col = dst_e[:, bass.ds(t, 1)]
                                dve.tensor_scalar(diag[:, :], ident[0:EP, 0:EP], col, None, ALU.mult).then_inc(s_dg, 1)
                                hold(dve, s_row, t + (tiles + 1))
                                link(dve.tensor_scalar(same[:, :], p_row[:, 0:EP], col, None, ALU.is_equal), 1)
                                link(dve.tensor_tensor(low[:, :], same[:, :], tri[:, :], ALU.mult), 2)
                                link(dve.tensor_reduce(earlier[:, :], low[:, :], AX.X, ALU.add), 3)
                                link(dve.tensor_scalar(firsts[:, :], earlier[:, :], 0.0, None, ALU.is_equal), 4)
                                link(dve.tensor_tensor(off[:, :], col, spare[:, :], ALU.subtract), 5)
                                link(dve.scalar_tensor_tensor(out=at_f[:, :], in0=off[:, :], scalar=firsts[:, 0:1],
                                                              in1=spare[:, :], op0=ALU.mult, op1=ALU.add), 6)
                                dve.tensor_copy(at[:, :], at_f[:, :]).then_inc(s_same, 1)
                                w_col = w_e[:, bass.ds(t, 1)]
                                if tab is not None:
                                    hold(dve, s_rows, t * 16 + (was["rows"] + 16))
                                    link(dve.tensor_scalar(rows_b[:, :], rows[:, :], w_col, None, ALU.mult), 7)
                                    dve.tensor_scalar(msg[:, :], rows_b[:, :], 0.5, None, ALU.mult).then_inc(s_rowmsg, 1)
                                elif dots:
                                    hold(dve, s_rows, t * 48 + (was["rows"] + 48))
                                    link(dve.tensor_scalar(low[:, 0:width], rows_b[:, :], dot[:, 0:1], None,
                                                           ALU.mult), 7)
                                    dve.tensor_tensor(msg[:, :], low[:, 0:width], rows[:, :], ALU.add
                                                      ).then_inc(s_rowmsg, 1)
                                else:
                                    link(dve.tensor_copy(low[:, 0:1], w_col), 7)
                                    dve.tensor_copy(msg[:, :], low[:, 0:1]).then_inc(s_rowmsg, 1)
                                hold(dve, s_comb, t + (tiles + 1))
                                dve.tensor_copy(comb[:, :], p_comb[:, 0:width]).then_inc(s_sum_out, 1)
                                hold(dve, s_add, (t + (tiles + 1)) * 16)
                            dve.nop()
            general_count["visits"] += 1
            general_count["before"] += len(before)
            general_count["after"] += len(after)
            general_count["from"] += ET if tab is not None or dots else 0
            general_count["rows"] += 16 * ET if tab is not None else 48 * ET if dots else 0

        def deg_finish(dve, b, acc, f0):
            return dve.tensor_copy(dinv[:, bass.ds(b.n * COLS, COLS)], acc)

        with ExitStack() as ph:
            window_pass("deg", [], lambda j: w_win[:, bass.ds(j, 1)], deg_finish, 0, ph)
        with ExitStack() as ph:
            nodes_of = "(b p c) a -> p b (c a)"
            deg3 = dinv[:, :].rearrange("p (b c) -> p b c", c=COLS)
            deg_rows = deg_tab.rearrange(nodes_of, p=P, c=COLS)
            general_path("gd", 1, deg_tab, [(deg_rows, deg3)], [(deg3, deg_rows)])
            pos = sb("dg_pos", [P, NB * COLS], F32, ph)
            s_c = sem("dg_dve")
            s_m = sem("dg_guarded")
            s_r = sem("dg_root")
            with nc.Block() as block:
                @block.vector
                def _(dve):
                    c = Chain(dve, s_c)
                    c(dve.tensor_scalar(dinv[:, :], dinv[:, :], 2.0, None, ALU.add))
                    c(dve.tensor_scalar(pos[:, :], dinv[:, :], 0.0, None, ALU.is_gt))
                    c(dve.tensor_tensor(dinv[:, :], dinv[:, :], pos[:, :], ALU.mult))
                    c(dve.tensor_tensor(dinv[:, :], dinv[:, :], pos[:, :], ALU.subtract))
                    dve.tensor_scalar(dinv[:, :], dinv[:, :], 1.0, None, ALU.add).then_inc(s_m, 1)
                    dve.wait_ge(s_r, 1)
                    c(dve.reciprocal(dinv[:, :], dinv[:, :]))
                    c(dve.tensor_tensor(dinv[:, :], dinv[:, :], pos[:, :], ALU.mult))

                @block.scalar
                def _(act):
                    act.wait_ge(s_m, 1)
                    act.activation(dinv[:, :], dinv[:, :], ACT.Sqrt).then_inc(s_r, 1)

        layer_norm("ln0", yn_tab, dinv)

        def dinv_b(b, shape_last):
            return dinv[:, bass.ds(b.n * COLS, COLS)].rearrange("p (c a) -> p c a", a=1).broadcast_to(
                [P, COLS, shape_last])

        general_path("g0g", C, sum_tab, [(blocks(sum_tab, C), Yb)], [(Yb, blocks(sum_tab, C))], tab=yn_tab)
        edge_gather("g0", yn_tab)
        with ExitStack() as ph:
            win = sb("win0", [P, NWIN, C], F32, ph)
            rewindow("rw0", msg_a, win)

            def finish0(dve, b, acc, f0):
                y = Y[:, bass.ds(b.n * BC, BC)]
                dve.scalar_tensor_tensor(out=y, in0=y, scalar=2.0, in1=acc, op0=ALU.mult, op1=ALU.add).then_inc(s_f, 1)
                dve.wait_ge(s_f, b.n + (f0 + 1))
                y3 = y.rearrange("p (c f) -> p c f", f=C)
                return dve.tensor_tensor(y3, y3, dinv_b(b, C), ALU.mult)
            window_pass("sum0", [win], lambda j: w_win[:, bass.ds(j, 1)], finish0, 1, ph)

        CUT = 3
        with ExitStack() as ph:
            turn_buf = sb("h1_stage", [P, 2, BC], F32, ph)
            s_stage = sem("h1_staged")
            sumT = sb("h1_sumT", [P, 2, P], F32, ph)
            rows = sb("h1_rows", [P, 2, COLS * H], F32, ph)
            p_t = ps("h1_t", [P, 512], ph)
            p_z = ps("h1_z", [P, 2, 2, 512], ph)
            s_one = sem("h1_ones_set")
            s_t = sem("h1_turned")
            s_tc = sem("h1_turned_copied")
            s_z = sem("h1_product")
            s_y = [sem("h1_rows_vector"), sem("h1_rows_scalar")]
            s_st = [sem(f"h1_rows_stored{u}") for u in range(2)]
            with nc.Block() as block:
                @block.tensor
                def _(pe):
                    def product(b):
                        pe.wait_ge(s_tc, b.n + 1)
                        if b.static and b.n < 2:
                            pass
                        else:
                            hold(pe, s_y[0], b.n - 1)
                            hold(pe, s_y[1], b.n - 1)
                        pe.matmul(p_z[:, b.par, 0, 0:CUT * H], sumT[0:BC + 1, b.par, :], W0x[:, 0:CUT * H],
                                  start=True, stop=True)
                        pe.matmul(p_z[:, b.par, 1, 0:(COLS - CUT) * H], sumT[0:BC + 1, b.par, :], W0x[:, CUT * H:],
                                  start=True, stop=True).then_inc(s_z, 1)

                    def step(t):
                        if t.has(NB):
                            if not t.static or t.n >= 1:
                                hold(pe, s_tc, t.n)
                            hold(pe, s_stage, t.n + 1)
                            pe.transpose(p_t[0:BC, 0:P], turn_buf[:, t.par, :], ident[:, :]).then_inc(s_t, 1)
                        if t.back(1).has(NB):
                            product(t.back(1))
                    run_steps(pe, step, NB, 1)

                @block.gpsimd
                def _(pool):
                    def step(b):
                        if not b.static or b.n >= 2:
                            hold(pool, s_t, b.n - 1)
                        pool.tensor_copy(turn_buf[:, b.par, :], Y[:, bass.ds(b.n * BC, BC)]).then_inc(s_stage, 1)
                    run_steps(pool, step, NB)

                @block.vector
                def _(dve):
                    dve.memset(sumT[64:P, :, :], 1.0).then_inc(s_one, 1)
                    dve.wait_ge(s_one, 1)

                    def step(t):
                        if t.has(NB):
                            dve.wait_ge(s_t, t.n + 1)
                            if not t.static or t.n >= 2:
                                dve.wait_ge(s_z, t.n - 1)
                            dve.tensor_copy(sumT[0:BC, t.par, :], p_t[0:BC, 0:P]).then_inc(s_tc, 1)
                        b = t.back(1)
                        if b.has(NB):
                            dve.wait_ge(s_z, b.n + 1)
                            if not b.static or b.n >= 2:
                                dve.wait_ge(s_st[b.par], 16 * b.round)
                            for k in range(CUT):
                                ins = dve.tensor_scalar(rows[:, b.par, k * H:(k + 1) * H],
                                                        p_z[:, b.par, 0, k * H:(k + 1) * H],
                                                        dinv[:, bass.ds(b.n * COLS + k, 1)], 0.0, ALU.mult, ALU.max)
                            ins.then_inc(s_y[0], 1)
                    run_steps(dve, step, NB, 1)

                @block.scalar
                def _(act):
                    def step(b):
                        hold(act, s_z, b.n + 1)
                        if not b.static or b.n >= 2:
                            hold(act, s_st[b.par], 16 * b.round)
                        for k in range(CUT, COLS):
                            ins = act.activation(rows[:, b.par, k * H:(k + 1) * H],
                                                 p_z[:, b.par, 1, (k - CUT) * H:(k - CUT + 1) * H],
                                                 ACT.Relu, scale=dinv[:, bass.ds(b.n * COLS + k, 1)])
                        ins.then_inc(s_y[1], 1)
                    run_steps(act, step, NB)

                @block.sync
                def _(sp):
                    def step(b):
                        hold(sp, s_y[0], b.n + 1)
                        sp.wait_ge(s_y[1], b.n + 1)
                        sp.dma_start(y1_tab[bass.ds(b.n * BN, BN), :].rearrange("(p c) f -> p (c f)", c=COLS),
                                     rows[:, b.par, :]).then_inc(s_st[b.par], 16)
                    run_steps(sp, step, NB)
                    for u in range(2):
                        sp.wait_ge(s_st[u], 16 * (NB // 2))

        def wide_layer(name, tab, Wt, bias, y_out):
            narrow = y_out is None
            with ExitStack() as ph:
                rows = sb(name + "_rows", [P, 2, WB, H], F32, ph)
                idx = sb(name + "_idx", [P, 2, WB], I32, ph)
                oh = sb(name + "_oh", [P, 2, WB, WN], F32, ph)
                own = sb(name + "_own", [P, 2, COLS * H], F32, ph)
                ownT = sb(name + "_ownT2", [P, 2, COLS * P], F32, ph)
                sumT = sb(name + "_sumT", [P, 2, COLS, P], F32, ph)
                pre = sb(name + "_pre", [P, 2, COLS * H], F32, ph)
                post = sb(name + "_post", [P, 2, COLS * H], F32, ph)
                p_agg = ps(name + "_agg", [P, 1024], ph)
                p_own = ps(name + "_ownT", [P, 1024], ph)
                p_z = ps(name + "_z", [P, 1024], ph)
                p_h = ps(name + "_h", [P, 1024], ph) if narrow else None
                s_clr = sem(name + "_rows_cleared")
                s_ix = sem(name + "_index_ready")
                s_g = [sem(f"{name}_rows_gathered{u}") for u in range(2)]
                s_own = [sem(f"{name}_own_loaded{u}") for u in range(2)]
                s_oh = sem(name + "_onehot_ready")
                s_agg = sem(name + "_windows_summed")
                s_turn = sem(name + "_own_turned")
                s_twice = sem(name + "_own_copied")
                s_T = sem(name + "_sums_ready")
                s_z = sem(name + "_product")
                s_e = sem(name + "_preactivation")
                s_post = sem(name + "_activated")
                s_st = [sem(f"{name}_stored{u}") for u in range(2)]
                s_h = sem(name + "_hidden_turned")
                s_y = sem(name + "_narrow_product")
                s_p = sem(name + "_narrow_rows")
                with nc.Block() as block:
                    @block.gpsimd
                    def _(pool):
                        pool.memset(rows[:, :, :, :], 0.0).then_inc(s_clr, 1)
                        pool.wait_ge(s_clr, 1)

                        def step(b):
                            if not b.static or b.n >= 2:
                                hold(pool, s_agg, b.n - 1)
                            pool.tensor_copy(idx[:, b.par, :], src_win[:, bass.ds(b.n * WB, WB)]).then_inc(s_ix, 1)
                            hold(pool, s_ix, b.n + 1)
                            for w in range(WB):
                                pool.indirect_dma_start(
                                    out=rows[:, b.par, w, :], out_offset=None, in_=tab,
                                    in_offset=bass.IndirectOffsetOnAxis(ap=idx[:, b.par, w:w + 1], axis=0),
                                    bounds_check=limit, oob_is_err=False).then_inc(s_g[b.par], 16)
                        limit = pool.to_reg(NP - 1)
                        run_steps(pool, step, NB)

                    @block.sync
                    def _(sp):
                        def load(b, own_tab):
                            if not b.static or b.n >= 2:
                                sp.wait_ge(s_turn, b.n - 1)
                            sp.dma_start(own[:, b.par, :], own_tab[bass.ds(b.n * BN, BN), :]
                                         .rearrange("(p c) f -> p (c f)", c=COLS)).then_inc(s_own[b.par], 16)
                        with sp.If(uncovered(sp)):
                            run_steps(sp, lambda b: load(b, u_tab), NB)
                        with sp.Else():
                            run_steps(sp, lambda b: load(b, tab), NB)

                    @block.vector
                    def _(dve):
                        def step(t):
                            b = t.back(-1)
                            if b.has(NB):
                                onehot(b)
                            if t.has(NB):
                                dve.wait_ge(s_agg, t.n + 1)
                                dve.wait_ge(s_twice, t.n + 1)
                                if not t.static or t.n >= 2:
                                    dve.wait_ge(s_z, t.n - 1)
                                for lo, hi, at in ((0, 96, 0), (96, P, 512)):
                                    ins = dve.tensor_tensor(
                                        sumT[:, t.par, :, lo:hi],
                                        p_agg[:, at:at + (hi - lo) * COLS].rearrange("f (p c) -> f c p", c=COLS),
                                        ownT[:, t.par, :].rearrange("f (c p) -> f c p", c=COLS)[:, :, lo:hi],
                                        ALU.add)
                                ins.then_inc(s_T, 1)
                            b = t.back(1)
                            if b.has(NB):
                                dve.wait_ge(s_z, b.n + 1)
                                if not b.static or b.n >= 2:
                                    dve.wait_ge(s_h if narrow else s_post, b.n - 1)
                                for c in range(COLS):
                                    ins = dve.scalar_tensor_tensor(
                                        out=pre[:, b.par, c * H:(c + 1) * H], in0=p_z[:, c * H:(c + 1) * H],
                                        scalar=dinv[:, bass.ds(b.n * COLS + c, 1)], in1=bias[:, :],
                                        op0=ALU.mult, op1=ALU.add)
                                ins.then_inc(s_e, 1)
                            b = t.back(2)
                            if narrow and b.has(NB):
                                dve.wait_ge(s_y, b.n + 1)
                                dve.tensor_tensor(
                                    Y[:, bass.ds(b.n * BC, BC)].rearrange("p (c f) -> p c f", f=C),
                                    p_h[:, BN:BN + BC].rearrange("p (c f) -> p c f", f=C),
                                    dinv_b(b, C), ALU.mult).then_inc(s_p, 1)

                        def onehot(b):
                            if not b.static or b.n >= 2:
                                dve.wait_ge(s_agg, b.n - 1)
                            for w in range(WB):
                                j = b.n * WB + w
                                ins = dve.tensor_scalar(oh[:, b.par, w, :], nodes[:, :], dst_win[:, bass.ds(j, 1)],
                                                        w_win[:, bass.ds(j, 1)], ALU.is_equal, ALU.mult)
                            ins.then_inc(s_oh, 1)
                        onehot(Step(0, 0))
                        run_steps(dve, step, NB - 2, 5)

                    @block.tensor
                    def _(pe):
                        def sums(b):
                            hold(pe, s_own[b.par], (b.round + 1) * 16)
                            if not b.static or b.n >= 1:
                                hold(pe, s_twice, b.n)
                            for c in range(COLS):
                                mm = pe.transpose(p_own[:, c * P:(c + 1) * P], own[:, b.par, c * H:(c + 1) * H],
                                                  ident[:, :])
                            mm.then_inc(s_turn, 1)
                            hold(pe, s_oh, b.n + 1)
                            hold(pe, s_g[b.par], (b.round + 1) * 16 * WB)
                            if not b.static or b.n >= 1:
                                hold(pe, s_T, b.n)
                            for w in range(WB):
                                at = w * WN if w < 3 else 512
                                mm = pe.matmul(p_agg[:, at:at + WN], rows[:, b.par, w, :], oh[:, b.par, w, :],
                                               start=True, stop=True)
                            mm.then_inc(s_agg, 1)

                        def step(t):
                            b = t.back(-1)
                            if b.has(NB):
                                sums(b)
                            if t.has(NB):
                                hold(pe, s_T, t.n + 1)
                                if not t.static or t.n >= 1:
                                    hold(pe, s_e, t.n)
                                for c in range(COLS):
                                    mm = pe.matmul(p_z[:, c * H:(c + 1) * H], sumT[:, t.par, c, :], Wt[:, :],
                                                   start=True, stop=True)
                                mm.then_inc(s_z, 1)
                            b = t.back(2)
                            if narrow and b.has(NB):
                                hold(pe, s_post, b.n + 1)
                                for c in range(COLS):
                                    mm = pe.matmul(p_h[:, BN + c * C:BN + (c + 1) * C],
                                                   post[:, b.par, c * P:(c + 1) * P], W3[:, :],
                                                   start=True, stop=True)
                                mm.then_inc(s_y, 1)
                            b = t.back(1)
                            if narrow and b.has(NB):
                                hold(pe, s_e, b.n + 1)
                                if not b.static or b.n >= 1:
                                    hold(pe, s_p, b.n)
                                for c in range(COLS):
                                    mm = pe.transpose(p_h[:, c * P:(c + 1) * P], pre[:, b.par, c * H:(c + 1) * H],
                                                      ident[:, :])
                                mm.then_inc(s_h, 1)
                        sums(Step(0, 0))
                        run_steps(pe, step, NB - 2, 5)

                    @block.scalar
                    def _(act):
                        def twice(b):
                            hold(act, s_turn, b.n + 1)
                            if not b.static or b.n >= 2:
                                hold(act, s_T, b.n - 1)
                            act.mul(ownT[:, b.par, :], p_own[:, 0:COLS * P], 2.0).then_inc(s_twice, 1)

                        def step(t):
                            b = t.back(-1)
                            if b.has(NB):
                                twice(b)
                            b = t.back(1)
                            if not b.has(NB):
                                return
                            if narrow:
                                hold(act, s_h, b.n + 1)
                                if not b.static or b.n >= 2:
                                    hold(act, s_y, b.n - 1)
                                act.activation(post[:, b.par, :], p_h[:, 0:COLS * P], ACT.Relu).then_inc(s_post, 1)
                                return
                            hold(act, s_e, b.n + 1)
                            if not b.static or b.n >= 2:
                                hold(act, s_st[b.par], 16 * b.round)
                            for c in range(COLS):
                                ins = act.activation(post[:, b.par, c * H:(c + 1) * H],
                                                     pre[:, b.par, c * H:(c + 1) * H], ACT.Relu,
                                                     scale=dinv[:, bass.ds(b.n * COLS + c, 1)])
                            ins.then_inc(s_post, 1)
                            act.wait_ge(s_post, b.n + 1)
                            act.dma_start(y_out[bass.ds(b.n * BN, BN), :].rearrange("(p c) f -> p (c f)", c=COLS),
                                          post[:, b.par, :]).then_inc(s_st[b.par], 16)
                        twice(Step(0, 0))
                        run_steps(act, step, NB - 2, 3)
                        if not narrow:
                            for u in range(2):
                                act.wait_ge(s_st[u], 16 * (NB // 2))

        general_path("g1g", H, u_tab, [(u_tab, y1_tab)], [], tab=y1_tab)
        wide_layer("l1", y1_tab, W1, bias1, y2_tab)
        general_path("g2g", H, u_tab, [(u_tab, y2_tab)], [], tab=y2_tab)
        wide_layer("l2", y2_tab, W2, bias2, None)

        s_y3 = sem("y3_stored")
        with nc.Block() as block:
            @block.sync
            def _(sp):
                sp.dma_start(blocks(yn_tab, C), Yb).then_inc(s_y3, 16)
                sp.wait_ge(s_y3, 16)
        general_path("g3g", C, sum_tab, [(blocks(sum_tab, C), Yb)], [(Yb, blocks(sum_tab, C))], tab=yn_tab)
        edge_gather("g3", yn_tab)
        with ExitStack() as ph:
            win = sb("win3", [P, NWIN, C], F32, ph)
            rewindow("rw3", msg_a, win)

            def finish3(dve, b, acc, f0):
                y = Y[:, bass.ds(b.n * BC, BC)]
                x_ = X[:, bass.ds(b.n * BC, BC)]
                y3, x3 = (a.rearrange("p (c f) -> p c f", f=C) for a in (y, x_))
                dve.scalar_tensor_tensor(out=y, in0=y, scalar=2.0, in1=acc, op0=ALU.mult, op1=ALU.add).then_inc(s_f, 1)
                dve.tensor_tensor(x3, x3, bias3[:, :].rearrange("p (a f) -> p a f", a=1).broadcast_to([P, COLS, C]),
                                  ALU.add).then_inc(s_f, 1)
                dve.wait_ge(s_f, b.n * 3 + (f0 + 1))
                dve.tensor_tensor(y3, y3, dinv_b(b, C), ALU.mult).then_inc(s_f, 1)
                dve.wait_ge(s_f, b.n * 3 + (f0 + 3))
                return dve.tensor_tensor(x_, x_, y, ALU.add)
            window_pass("sum3", [win], lambda j: w_win[:, bass.ds(j, 1)], finish3, 3, ph)

        layer_norm("ln1", yn_tab, None)
        with ExitStack() as rel:
            drow = sb("drow", [P, NB * COLS], F32, rel)
            with ExitStack() as ph:
                h = sb("rg_h", [EP, 2, EG, C], F32, ph)
                idx = sb("rg_idx", [EP, 2, EG], I32, ph)
                attr = sb("rg_attr", [EP, 2, EG, C], F32, ph)
                typ = sb("rg_type", [EP, 2, EG, R], F32, ph)
                typT = sb("rg_typeT", [R, 2, EG, EP], F32, ph)
                prod = sb("rg_prod", [EP, EG * C * C], F32, ph)
                u = sb("rg_u", [EP, 2, EG, C], F32, ph)
                ue = sb("rg_ue", [EP, 2, EG, C], F32, ph)
                dots = sb("rg_dots", [EP, EG, C], F32, ph)
                dote = sb("rg_dote", [EP, EG, C], F32, ph)
                coef = sb("rg_coef", [EP, EG], F32, ph)
                p_t = ps("rg_pt", [P, 2, 512], ph)
                p_w = ps("rg_pw", [P, EG * C * C], ph)
                dtmp = sb("rg_dtmp", [P, 20 * BC], F32, ph)
                s_ix = sem("rg_index_ready")
                s_g = [sem(f"rg_rows_gathered{k}") for k in range(2)]
                s_at = [sem(f"rg_attr_loaded{k}") for k in range(2)]
                s_st = [sem(f"rg_messages_stored{k}") for k in range(2)]
                s_ty = sem("rg_types_compared")
                s_tt = sem("rg_types_turned")
                s_tc = sem("rg_types_copied")
                s_w = sem("rg_matrices_selected")
                s_pr = sem("rg_products")
                s_u = sem("rg_rows_times_matrix")
                s_a = sem("rg_attention_chain")
                s_m = sem("rg_messages_ready")
                s_dr = sem("rg_dst_dots")
                with nc.Block() as block:
                    @block.gpsimd
                    def _(pool):
                        def step(b):
                            if not b.static or b.n >= 2:
                                hold(pool, s_m, b.n - 1)
                            pool.tensor_copy(idx[:, b.par, :], src_edge[:, bass.ds(b.n * EG, EG)]).then_inc(s_ix, 1)
                            hold(pool, s_ix, b.n + 1)
                            for k in range(EG):
                                pool.indirect_dma_start(
                                    out=h[:, b.par, k, :], out_offset=None, in_=yn_tab,
                                    in_offset=bass.IndirectOffsetOnAxis(ap=idx[:, b.par, k:k + 1], axis=0)
                                    ).then_inc(s_g[b.par], 16)
                        run_steps(pool, step, NCH)

                    @block.sync
                    def _(sp):
                        def step(t):
                            if t.has(NCH):
                                if not t.static or t.n >= 2:
                                    sp.wait_ge(s_m, t.n - 1)
                                sp.dma_start(attr[:, t.par, :, :].rearrange("p k f -> p (k f)"),
                                             edge_attr.rearrange("(p t) f -> p (t f)", t=ET)
                                             [:, bass.ds(t.n * EG * C, EG * C)]).then_inc(s_at[t.par], 16)
                            b = t.back(1)
                            if b.has(NCH):
                                for tab, buf in ((msg_a, ue), (msg_b, u)):
                                    sp.wait_ge(s_m, b.n + 1)
                                    sp.dma_start(tab.rearrange("(p t) f -> p (t f)", t=ET)
                                                 [:, bass.ds(b.n * EG * C, EG * C)],
                                                 buf[:, b.par, :, :].rearrange("p k f -> p (k f)")
                                                 ).then_inc(s_st[b.par], 16)
                        run_steps(sp, step, NCH, 1)
                        for k in range(2):
                            sp.wait_ge(s_st[k], 32 * (NCH // 2))

                    @block.vector
                    def _(dve):
                        c = Chain(dve, s_dr)
                        for lo in range(0, NB, 20):
                            hi = min(lo + 20, NB)
                            n = (hi - lo) * COLS
                            d3 = dtmp[:, 0:n * C].rearrange("p (n f) -> p n f", f=C)
                            c(dve.tensor_tensor(d3, Y[:, lo * BC:hi * BC].rearrange("p (n f) -> p n f", f=C),
                                                v_rel[:, 2 * C:3 * C].rearrange("p (a f) -> p a f", a=1)
                                                .broadcast_to([P, n, C]), ALU.mult))
                            c(dve.tensor_reduce(drow[:, lo * COLS:hi * COLS], d3, AX.X, ALU.add))

                        def types(b):
                            if not b.static or b.n >= 2:
                                dve.wait_ge(s_tt, b.n - 1)
                            dve.tensor_tensor(
                                typ[:, b.par, :, :],
                                nodes[0:EP, 0:R].rearrange("p (a r) -> p a r", a=1).broadcast_to([EP, EG, R]),
                                type_edge[:, bass.ds(b.n * EG, EG)].rearrange("p (k a) -> p k a", a=1)
                                .broadcast_to([EP, EG, R]), ALU.is_equal).then_inc(s_ty, 1)

                        def vec(k):
                            return v_rel[0:EP, k * C:(k + 1) * C].rearrange("p (a f) -> p a f", a=1).broadcast_to(
                                [EP, EG, C])

                        def step(t):
                            if t.has(NCH):
                                types(t)
                            b = t.back(1)
                            if b.has(NCH):
                                hold(dve, s_g[b.par], (b.round + 1) * 16 * EG)
                                hold(dve, s_at[b.par], (b.round + 1) * 16)
                                dve.tensor_tensor(dots[:, :, :], h[:, b.par, :, :], vec(0), ALU.mult).then_inc(s_a, 1)
                                dve.tensor_tensor(dote[:, :, :], attr[:, b.par, :, :], vec(1), ALU.mult).then_inc(s_a, 1)
                                dve.wait_ge(s_w, b.n + 1)
                                dve.tensor_tensor(
                                    prod[:, :].rearrange("p (k o i) -> p k o i", k=EG, o=C),
                                    p_w[0:EP, :].rearrange("p (k o i) -> p k o i", k=EG, o=C),
                                    h[:, b.par, :, :].rearrange("p k (a i) -> p k a i", a=1)
                                    .broadcast_to([EP, EG, C, C]), ALU.mult).then_inc(s_pr, 1)
                                dve.wait_ge(s_a, b.n * 4 + 2)
                                dve.tensor_tensor(dots[:, :, :], dots[:, :, :], dote[:, :, :], ALU.add).then_inc(s_a, 1)
                                if not b.static or b.n >= 2:
                                    hold(dve, s_st[b.par], 32 * b.round)
                                dve.wait_ge(s_pr, b.n + 1)
                                dve.tensor_reduce(u[:, b.par, :, :].rearrange("p k o -> p (k o)"),
                                                  prod[:, :].rearrange("p (g i) -> p g i", i=C),
                                                  AX.X, ALU.add).then_inc(s_u, 1)
                                dve.wait_ge(s_a, b.n * 4 + 3)
                                dve.tensor_reduce(coef[:, :], dots[:, :, :], AX.X, ALU.add).then_inc(s_a, 1)
                                dve.wait_ge(s_a, b.n * 4 + 4)
                                dve.wait_ge(s_u, b.n + 1)
                                dve.tensor_tensor(ue[:, b.par, :, :], u[:, b.par, :, :],
                                                  coef[:, :].rearrange("p (k a) -> p k a", a=1)
                                                  .broadcast_to([EP, EG, C]), ALU.mult).then_inc(s_m, 1)
                        run_steps(dve, step, NCH, 1)

                    @block.tensor
                    def _(pe):
                        def step(t):
                            if t.has(NCH):
                                hold(pe, s_ty, t.n + 1)
                                if not t.static or t.n >= 1:
                                    hold(pe, s_tc, t.n)
                                for k in range(EG):
                                    mm = pe.transpose(p_t[0:R, k // 4, (k % 4) * EP:(k % 4 + 1) * EP],
                                                      typ[:, t.par, k, :], ident[0:EP, 0:EP])
                                mm.then_inc(s_tt, 1)
                            b = t.back(1)
                            if b.has(NCH):
                                hold(pe, s_tc, b.n + 1)
                                if not b.static or b.n >= 1:
                                    hold(pe, s_pr, b.n)
                                for k in range(EG):
                                    mm = pe.matmul(p_w[0:EP, k * C * C:(k + 1) * C * C], typT[:, b.par, k, :],
                                                   Wr[:, :], start=True, stop=True)
                                mm.then_inc(s_w, 1)
                        run_steps(pe, step, NCH, 1)

                    @block.scalar
                    def _(act):
                        def step(b):
                            hold(act, s_tt, b.n + 1)
                            if not b.static or b.n >= 2:
                                hold(act, s_w, b.n - 1)
                            act.copy(typT[:, b.par, :, :].rearrange("r (g k) e -> r g (k e)", g=2),
                                     p_t[0:R, :, 0:4 * EP]).then_inc(s_tc, 1)
                        run_steps(act, step, NCH)

            drow3 = drow[:, :].rearrange("p (b c) -> p b c", c=COLS)
            general_path("grg", C, sum_tab, [(blocks(sum_tab, C), Xb), (dot_tab.rearrange(nodes_of, p=P, c=COLS), drow3)],
                         [(Xb, blocks(sum_tab, C))], dots=True)
            with ExitStack() as ph:
                win_a = sb("win_a", [P, NWIN, C], F32, ph)
                win_b = Y[:, 0:NWIN * C].rearrange("p (j f) -> p j f", f=C)
                rewindow("rwa", msg_a, win_a)
                rewindow("rwb", msg_b, win_b)
                tmp = sb("rg_tmp", [P, 2, BC], F32, ph)

                def finish_rel(dve, b, acc, f0):
                    x3 = X[:, bass.ds(b.n * BC, BC)].rearrange("p (c f) -> p c f", f=C)
                    t3 = tmp[:, b.par, :].rearrange("p (c f) -> p c f", f=C)
                    a4 = acc.rearrange("p (c k f) -> p c k f", c=COLS, k=2)
                    dve.tensor_tensor(t3, a4[:, :, 1, :],
                                      drow[:, bass.ds(b.n * COLS, COLS)].rearrange("p (c a) -> p c a", a=1)
                                      .broadcast_to([P, COLS, C]), ALU.mult).then_inc(s_f, 1)
                    dve.tensor_tensor(x3, x3, a4[:, :, 0, :], ALU.add).then_inc(s_f, 1)
                    dve.wait_ge(s_f, b.n * 2 + (f0 + 2))
                    return dve.tensor_tensor(x3, x3, t3, ALU.add)
                window_pass("sumr", [win_a, win_b], lambda j: covered[:, 0:1], finish_rel, 2, ph)

        s_out = sem("out_stored")
        with nc.Block() as block:
            @block.sync
            def _(sp):
                sp.dma_start(ov, Xb[:, 0:FULL, :]).then_inc(s_out, 16)
                sp.dma_start(orr, Xb[0:REST, FULL, :]).then_inc(s_out, 16)
                sp.wait_ge(s_out, 32)


_INS = ["x", "src", "dst", "edge_attr_16", "edge_type_90", "edge_weight", "L0_gnn_w0", "L0_gnn_b0", "L0_gnn_w1",
        "L0_gnn_b1", "L0_gnn_w2", "L0_gnn_b2", "L0_gnn_w3", "L0_gnn_b3", "L1_gnn_Ws", "L1_gnn_Wa", "L1_gnn_weight",
        "L1_gnn_w_comp"]


def kernel(**inputs):
    import concourse.bacc as bacc
    from concourse.bass_utils import run_bass_kernel_spmd as run

    nc = bacc.Bacc("TRN2", target_bir_lowering=False, num_devices=1)
    arrays, args = {}, []
    for name in _INS:
        a = np.ascontiguousarray(inputs[name])
        arrays["in_" + name] = a
        args.append(nc.dram_tensor("in_" + name, a.shape, mybir.dt.from_np(a.dtype), kind="ExternalInput").ap())
    o = nc.dram_tensor("out_0", (N, C), F32, kind="ExternalOutput").ap()
    build(nc, *args, o)
    return run(nc, [arrays], core_ids=[0]).results[0]["out_0"]
```

```python
from contextlib import ExitStack

import numpy as np
import concourse.bass as bass
from concourse import mybir

F32 = mybir.dt.float32
I32 = mybir.dt.int32
ALU = mybir.AluOpType
ACT = mybir.ActivationFunctionType
AX = mybir.AxisListType

P = 128
N = 100000
E = 50000
C = 16
H = 128
R = 90
B = 30
COLS = 5
BP = 125
BN = BP * COLS
NB = N // BN
G = 3
BC = COLS * C
NT = N + P
TAIL = P * G
NQ = -(-NB // P)
EP = 125
ET = E // EP
SKIP = 1 << 21
UNROLL = 4
HEAD = 2 * UNROLL
SPAN = ((0, 360), (150, BN), (365, BN))
HALF = 310

D0, W0_, DI, DQ = 0, G, 2 * G, 2 * G + COLS
DP, WC, KS = DQ + COLS, DQ + COLS + G, DQ + COLS + G + G * COLS
RP, RC, RT, RE, RD, KR = 0, G, G + G * COLS, 2 * G + G * COLS, 3 * G + G * COLS, 3 * G + G * COLS + COLS


class Step:

    def __init__(self, i, c=0):
        self.static = isinstance(i, int)
        self.i, self.c = divmod(UNROLL * i + c, UNROLL) if self.static else (i, c)

    @property
    def n(self):
        return self.i * UNROLL + self.c

    @property
    def par(self):
        return self.c % 2

    @property
    def slot(self):
        return self.c % UNROLL

    @property
    def round(self):
        return self.i + self.c // UNROLL

    @property
    def round2(self):
        return self.i * 2 + self.c // 2

    def back(self, k):
        return Step(self.i, self.c - k)

    def has(self):
        return not self.static or 0 <= self.n < NB

    def from_(self, k):
        return not self.static or self.n >= k


def run_steps(eng, step, ahead=0, drain=0):
    for t in range(HEAD):
        step(Step(0, t))
    with eng.Fori(HEAD // UNROLL, NB // UNROLL - (1 if ahead else 0)) as i:
        for c in range(UNROLL):
            step(Step(i, c))
    for t in range(NB - (UNROLL if ahead else 0), NB + drain):
        step(Step(0, t))


def hold(eng, sem, value):
    eng.wait_ge(sem, value)
    eng.nop(nofuse=True)


class Chain:

    def __init__(self, eng, sem, n=0):
        self.eng, self.sem, self.n = eng, sem, n

    def __call__(self, ins):
        self.n += 1
        ins.then_inc(self.sem, 1)
        self.eng.wait_ge(self.sem, self.n)


def spread(ap, parts, n, m):
    return ap.rearrange("p (n a) -> p n a", a=1).broadcast_to([parts, n, m])


def build(nc, x, src, dst, edge_attr, edge_type, edge_weight, w0, b0, w1, b1, w2, b2, w3, b3,
          Ws, Wa, weight, w_comp, out):
    top = ExitStack()
    with top:
        def sb(name, shape, dt=F32, ctx=top):
            return ctx.enter_context(nc.sbuf_tensor(name, shape, dt))

        def ps(name, shape, ctx):
            return ctx.enter_context(nc.psum_tensor(name, shape, F32))

        def sem(name):
            return top.enter_context(nc.semaphore(name))

        yn_tab = nc.dram_tensor("y_narrow", (N, C), F32).ap()
        y1_tab = nc.dram_tensor("y1", (N, H), F32).ap()
        y2_tab = nc.dram_tensor("y2", (N, H), F32).ap()
        te_tab = nc.dram_tensor("edge_dot", (E + TAIL,), F32).ap()
        dst_tab = nc.dram_tensor("dst_tailed", (E + TAIL,), I32).ap()
        src_tab = nc.dram_tensor("src_tailed", (E + TAIL,), I32).ap()
        type_tab = nc.dram_tensor("type_tailed", (E + TAIL,), I32).ap()
        w_tab = nc.dram_tensor("weight_tailed", (E + TAIL,), F32).ap()
        rel_tab = nc.dram_tensor("rel_w", (C * R, C), F32).ap()
        deg_tab = nc.dram_tensor("deg", (NT, 1), F32).ap()
        dot_tab = nc.dram_tensor("dst_dot", (N, 1), F32).ap()
        sum_tab = nc.dram_tensor("sum_narrow", (NT, C), F32).ap()
        u_tab = nc.dram_tensor("own_wide", (NT, H), F32).ap()

        X = sb("X", [BP, NB * BC])
        Y = sb("Y", [BP, NB * BC])
        ident = sb("ident", [P, P])
        nodes = sb("nodes", [P, BN])
        ones = sb("ones", [P, P])
        part = sb("part", [P, 1])
        src_slot = sb("src_slot", [P, NB, G], I32)
        scal = sb("scal", [P, NB, KS])
        scal_rel = sb("scal_rel", [P, NB, KR])
        covered = sb("covered", [P, 1])
        covered_i = sb("covered_i", [P, 1], I32)
        W1 = sb("W1", [H, H])
        W2 = sb("W2", [H, H])
        W3 = sb("W3", [H, C])
        bias1 = sb("bias1", [P, H])
        bias2 = sb("bias2", [H, 1])
        bias3 = sb("bias3", [P, C])
        W0x = sb("W0x", [BC + COLS, COLS * H])
        v_rel = sb("v_rel", [P, 3 * C])
        Wr = sb("Wr", [R, C * C])

        def blocks(tab):
            return tab.rearrange("(b p c) f -> p b (c f)", p=BP, c=COLS)

        def rows_of(tab, b):
            return tab[bass.ds(b.n * BN, BN), :].rearrange("(p c) f -> p (c f)", c=COLS)

        Xb = X[:, :].rearrange("p (b g) -> p b g", g=BC)
        Yb = Y[:, :].rearrange("p (b g) -> p b g", g=BC)
        dinv3 = scal[0:BP, :, DI:DI + COLS]
        dinv_sq = scal[0:BP, :, DQ:DQ + COLS]
        drow3 = scal_rel[0:BP, :, RD:RD + COLS]

        with ExitStack() as ph:
            def t(name, shape, dt=F32):
                return sb("su_" + name, shape, dt, ph)
            nodes_i = t("nodes_i", [P, BN], I32)
            part_i = t("part_i", [P, 1], I32)
            first = t("first", [P, NQ])
            base_i = t("base_i", [P, NB], I32)
            head_i = t("head_i", [1, ET], I32)
            head = t("head", [1, ET])
            below = t("below", [P, ET])
            cnt = t("cnt", [P, NQ])
            row_i = t("row_i", [P, NQ], I32)
            row = t("row", [P, NQ])
            runs = t("runs", [P, NQ, EP], I32)
            runs_f = t("runs_f", [P, NQ, EP])
            begin = t("begin", [P, NQ])
            begin_i = t("begin_i", [P, NQ], I32)
            lanes = [t("lanes_" + k, [P, NQ, TAIL], dt) for k, dt in
                     (("dst", I32), ("src", I32), ("type", I32), ("w", F32), ("te", F32))]
            lanes_f = [t("lanes_f_" + k, [P, NQ, TAIL]) for k in ("dst", "src", "type")]
            slots = [t("slots_" + k, [P, G, NB]) for k in ("dst", "src", "type", "w", "te")]
            d, s, typ, w, te = slots
            valid = t("valid", [P, G, NB])
            tmp = t("tmp", [P, G, NB])
            dp = t("dp", [P, G, NB])
            dp_i = t("dp_i", [P, G, NB], I32)
            dc = t("dc", [P, G, NB])
            total = t("total", [P, 1])
            tail_i = t("tail_i", [3, P], I32)
            bases = t("bases", [B, C * C])
            comp = t("comp", [B, R])
            comp_r = t("comp_r", [R, B])
            wa = t("wa", [C, 3])
            wa_b = t("wa_b", [C, 3, P])
            ws = t("ws", [C, C])
            p_head = ps("p_head", [P, 512], ph)
            p_win = ps("p_win", [P, 5, 512], ph)
            p_misc = ps("p_misc", [P, 512], ph)
            attr = Y[:, 0:ET * C]
            rel_mix = Y[0:R, ET * C:ET * C + C * C]
            te_e = Y[:, ET * C + 2 * C * C:ET * C + 2 * C * C + ET]
            rel_in = Y[0:R, ET * C + C * C:ET * C + 2 * C * C]

            s_load = sem("su_loaded")
            s_heads = sem("su_heads_loaded")
            s_relw = sem("su_relation_inputs_loaded")
            s_attr = sem("su_attributes_loaded")
            s_tail = sem("su_lists_tailed")
            s_te = sem("su_edge_dots")
            s_tes = sem("su_edge_dots_stored")
            s_iota = sem("su_iota")
            s_d = sem("su_dve")
            s_id = sem("su_identity_ready")
            s_hf = sem("su_heads_float")
            s_hb = sem("su_heads_broadcast")
            s_row = sem("su_rows_ready")
            s_runs = sem("su_runs_gathered")
            s_beg = sem("su_begins_ready")
            s_lanes = sem("su_lanes_gathered")
            s_lf = sem("su_lanes_float")
            s_tr = sem("su_slots_turned")
            s_tc = sem("su_slots_copied")
            s_tot = sem("su_valid_counted")
            s_sum = sem("su_valid_summed")
            s_rm = sem("su_relation_matrix")
            s_rst = sem("su_relation_stored")
            s_rld = sem("su_relation_loaded")
            s_rc = sem("su_relation_copied")
            s_cT = sem("su_comp_turned")

            LOADS = 7 + 2 * COLS
            TAILS = 4 * 2 + 1
            dst_rows = dst.rearrange("(t p) -> t p", p=EP)
            with nc.Block() as block:
                @block.sync
                def _(sp):
                    sp.dma_start(head_i[:, :], dst.rearrange("(t p) -> p t", p=EP)[0:1, :],
                                 allow_slow_non_contiguous=True).then_inc(s_heads, 16)
                    sp.dma_start(bases[:, :].rearrange("b (i o) -> b i o", i=C),
                                 weight.rearrange("b i o -> (b i o)").rearrange("(i b o) -> b i o", i=C, b=B)
                                 ).then_inc(s_relw, 16)
                    sp.dma_start(comp_r[:, :], w_comp).then_inc(s_relw, 16)
                    sp.dma_start(wa[:, :], Wa.rearrange("a (k o) -> o (a k)", k=3),
                                 allow_slow_non_contiguous=True).then_inc(s_relw, 16)
                    sp.dma_start(ws[:, :], Ws).then_inc(s_relw, 16)
                    sp.dma_start(attr, edge_attr.rearrange("(p t) f -> p (t f)", t=ET)).then_inc(s_attr, 16)
                    sp.dma_start(W1[:, :], w1).then_inc(s_load, 16)
                    sp.dma_start(W2[:, :], w2).then_inc(s_load, 16)
                    sp.dma_start(W3[:, :], w3).then_inc(s_load, 16)
                    for tile, vec in ((bias1, b1), (bias3, b3)):
                        sp.dma_start(tile[:, :], vec.rearrange("(a f) -> a f", a=1).broadcast_to([P, vec.shape[0]])
                                     ).then_inc(s_load, 16)
                    sp.dma_start(bias2[:, :], b2.rearrange("(f a) -> f a", a=1)).then_inc(s_load, 16)
                    sp.wait_ge(s_iota, 4)
                    for c in range(COLS):
                        sp.dma_start(W0x[c * C:(c + 1) * C, c * H:(c + 1) * H], w0).then_inc(s_load, 16)
                        sp.dma_start(W0x[BC + c:BC + c + 1, c * H:(c + 1) * H],
                                     b0.rearrange("(a f) -> a f", a=1)).then_inc(s_load, 16)
                    sp.wait_ge(s_rm, 1)
                    sp.dma_start(rel_tab.rearrange("(i r) o -> r i o", r=R),
                                 rel_mix[:, :].rearrange("r (i o) -> r i o", i=C)).then_inc(s_rst, 16)
                    sp.wait_ge(s_rst, 16)
                    sp.dma_start(rel_in[:, :], rel_tab.rearrange("(r i) o -> r (i o)", i=C)).then_inc(s_rld, 16)
                    sp.wait_ge(s_load, 16 * LOADS)
                    sp.wait_ge(s_rld, 16)

                @block.scalar
                def _(act):
                    act.wait_ge(s_iota, 3)
                    for tab, vec in ((dst_tab, dst), (src_tab, src), (type_tab, edge_type), (w_tab, edge_weight)):
                        act.dma_start(tab[0:E].rearrange("(a e) -> a e", a=16),
                                      vec.rearrange("(a e) -> a e", a=16)).then_inc(s_tail, 16)
                    for tab in (dst_tab, src_tab, type_tab):
                        act.dma_start(tab[E:E + TAIL].rearrange("(a e) -> a e", a=G), tail_i[:, :]).then_inc(s_tail, 16)
                    act.wait_ge(s_iota, 8)
                    act.dma_start(w_tab[E:E + TAIL].rearrange("(a e) -> a e", a=G), ones[0:G, :]).then_inc(s_tail, 16)
                    act.dma_start(te_tab[E:E + TAIL].rearrange("(a e) -> a e", a=G), ones[0:G, :]).then_inc(s_tail, 16)
                    act.dma_start(Xb, blocks(x)).then_inc(s_load, 16)
                    act.wait_ge(s_te, 1)
                    act.dma_start(te_tab[0:E].rearrange("(p t) -> p t", t=ET), te_e).then_inc(s_tes, 16)
                    for k in range(5):
                        act.wait_ge(s_tr, k + 1)
                        act.copy(slots[k][:, :, :].rearrange("p g b -> p (g b)"), p_win[:, k, 0:G * NB]).then_inc(s_tc, 1)
                    act.wait_ge(s_load, 16 * LOADS)
                    act.wait_ge(s_tes, 16)
                    act.wait_ge(s_tail, 16 * TAILS)

                @block.gpsimd
                def _(pool):
                    pool.iota(nodes_i[:, :], pattern=[[1, BN]], base=0, channel_multiplier=0).then_inc(s_iota, 1)
                    pool.iota(part_i[:, :], pattern=[[0, 1]], base=0, channel_multiplier=1).then_inc(s_iota, 1)
                    pool.iota(tail_i[:, :], pattern=[[0, P]], base=1 << 20, channel_multiplier=0).then_inc(s_iota, 1)
                    pool.memset(W0x[:, :], 0.0).then_inc(s_iota, 1)
                    pool.iota(base_i[:, :], pattern=[[BN, NB]], base=0, channel_multiplier=0).then_inc(s_iota, 1)
                    pool.memset(scal[:, :, DI:DI + 2 * COLS], 0.0).then_inc(s_iota, 1)
                    pool.memset(scal_rel[:, :, RD:RD + COLS], 0.0).then_inc(s_iota, 1)
                    pool.memset(ones[:, :], 1.0).then_inc(s_iota, 1)
                    pool.wait_ge(s_row, 1)
                    for q in range(NQ):
                        pool.indirect_dma_start(
                            out=runs[:, q, :], out_offset=None, in_=dst_rows,
                            in_offset=bass.IndirectOffsetOnAxis(ap=row_i[:, q:q + 1], axis=0)).then_inc(s_runs, 16)
                    hold(pool, s_tail, 16 * TAILS)
                    hold(pool, s_tes, 16)
                    pool.wait_ge(s_beg, 1)
                    for tile, tab in zip(lanes, (dst_tab, src_tab, type_tab, w_tab, te_tab)):
                        for q in range(NQ):
                            pool.indirect_dma_start(
                                out=tile[:, q, :], out_offset=None, in_=tab.rearrange("(a e) -> a e", a=1),
                                in_offset=bass.IndirectOffsetOnAxis(ap=begin_i[:, q:q + 1], axis=1)
                                ).then_inc(s_lanes, 16)
                    pool.wait_ge(s_lanes, 16 * 5 * NQ)

                @block.vector
                def _(dve):
                    c = Chain(dve, s_d)
                    dve.wait_ge(s_iota, 8)
                    c(dve.tensor_copy(nodes[:, :], nodes_i[:, :]))
                    c(dve.tensor_copy(part[:, :], part_i[:, :]))
                    dve.tensor_scalar(ident[:, :], nodes[:, 0:P], part[:, 0:1], None, ALU.is_equal).then_inc(s_id, 1)
                    dve.wait_ge(s_heads, 16)
                    dve.tensor_copy(head[:, :], head_i[:, :]).then_inc(s_hf, 1)
                    for q in range(NQ):
                        c(dve.tensor_scalar(first[:, q:q + 1], part[:, :], float(BN), float(BN * P * q), ALU.mult, ALU.add))
                    dve.wait_ge(s_hb, 1)
                    for q in range(NQ):
                        c(dve.tensor_scalar(below[:, :], p_head[:, 0:ET], first[:, q:q + 1], None, ALU.is_lt))
                        c(dve.tensor_reduce(cnt[:, q:q + 1], below[:, :], AX.X, ALU.add))
                    c(dve.tensor_scalar(row[:, :], cnt[:, :], -1.0, 0.0, ALU.add, ALU.max))
                    dve.tensor_copy(row_i[:, :], row[:, :]).then_inc(s_row, 1)
                    dve.wait_ge(s_cT, 1)
                    dve.tensor_copy(comp[:, :], p_misc[0:B, 0:R]).then_inc(s_rc, 1)
                    dve.tensor_copy(wa_b[:, :, :], spread(wa[:, :], C, 3, P)).then_inc(s_rc, 1)
                    dve.wait_ge(s_runs, 16 * NQ)
                    c(dve.tensor_copy(runs_f[:, :, :], runs[:, :, :]))
                    for q in range(NQ):
                        c(dve.tensor_scalar(below[:, 0:EP], runs_f[:, q, :], first[:, q:q + 1], None, ALU.is_lt))
                        c(dve.tensor_reduce(cnt[:, q:q + 1], below[:, 0:EP], AX.X, ALU.add))
                    c(dve.scalar_tensor_tensor(out=begin[:, :], in0=row[:, :], scalar=float(EP), in1=cnt[:, :],
                                               op0=ALU.mult, op1=ALU.add))
                    dve.tensor_copy(begin_i[:, :], begin[:, :]).then_inc(s_beg, 1)
                    dve.wait_ge(s_cT, 2)
                    dve.tensor_copy(rel_mix[:, :], p_misc[0:R, 0:C * C]).then_inc(s_rm, 1)
                    c(dve.tensor_copy(v_rel[:, :], p_misc[:, C * C:C * C + 3 * C]))
                    dve.wait_ge(s_attr, 16)
                    a3 = attr.rearrange("p (t f) -> p t f", f=C)
                    c(dve.tensor_tensor(a3, a3, v_rel[0:EP, C:2 * C].rearrange("p (a f) -> p a f", a=1)
                                        .broadcast_to([EP, ET, C]), ALU.mult))
                    dve.tensor_reduce(te_e, a3, AX.X, ALU.add).then_inc(s_te, 1)
                    dve.wait_ge(s_lanes, 16 * 5 * NQ)
                    for k in range(3):
                        dve.tensor_copy(lanes_f[k][:, :, :], lanes[k][:, :, :]).then_inc(s_lf, 1)
                    dve.wait_ge(s_tc, 5)
                    c(dve.tensor_copy(tmp[:, 0, :], base_i[:, :]))
                    c(dve.tensor_tensor(d[:, :, :], d[:, :, :], tmp[:, 0, :].rearrange("p (a b) -> p a b", a=1)
                                        .broadcast_to([P, G, NB]), ALU.subtract))
                    for g, (lo, hi) in enumerate(SPAN):
                        c(dve.tensor_scalar(valid[:, g, :], d[:, g, :], float(lo), None, ALU.is_ge))
                        c(dve.scalar_tensor_tensor(out=valid[:, g, :], in0=d[:, g, :], scalar=float(hi),
                                                   in1=valid[:, g, :], op0=ALU.is_lt, op1=ALU.mult))
                    dve.tensor_reduce(total[:, :], valid[:, :, :].rearrange("p g b -> p (g b)"), AX.X, ALU.add
                                      ).then_inc(s_tot, 1)
                    c(dve.scalar_tensor_tensor(out=d[:, :, :], in0=d[:, :, :], scalar=10000.0, in1=valid[:, :, :],
                                               op0=ALU.add, op1=ALU.mult))
                    c(dve.tensor_scalar(d[:, :, :], d[:, :, :], -10000.0, None, ALU.add))
                    c(dve.tensor_scalar(valid[:, :, :], valid[:, :, :], -float(SKIP), float(SKIP), ALU.mult, ALU.add))
                    c(dve.tensor_tensor(s[:, :, :], s[:, :, :], valid[:, :, :], ALU.add))
                    c(dve.tensor_copy(src_slot[:, :, :].rearrange("p b g -> p g b"), s[:, :, :]))
                    c(dve.tensor_scalar(dp[:, :, :], d[:, :, :], 0.2, None, ALU.mult))
                    c(dve.tensor_copy(dp_i[:, :, :], dp[:, :, :]))
                    c(dve.tensor_copy(dp[:, :, :], dp_i[:, :, :]))
                    c(dve.scalar_tensor_tensor(out=dc[:, :, :], in0=dp[:, :, :], scalar=-float(COLS), in1=d[:, :, :],
                                               op0=ALU.mult, op1=ALU.add))
                    c(dve.tensor_scalar(tmp[:, :, :], dc[:, :, :], 0.0, None, ALU.is_lt))
                    c(dve.tensor_tensor(dp[:, :, :], dp[:, :, :], tmp[:, :, :], ALU.subtract))
                    c(dve.tensor_scalar(tmp[:, :, :], dc[:, :, :], float(COLS), None, ALU.is_ge))
                    c(dve.tensor_tensor(dp[:, :, :], dp[:, :, :], tmp[:, :, :], ALU.add))
                    c(dve.scalar_tensor_tensor(out=dc[:, :, :], in0=dp[:, :, :], scalar=-float(COLS), in1=d[:, :, :],
                                               op0=ALU.mult, op1=ALU.add))
                    dve.wait_ge(s_sum, 1)
                    c(dve.tensor_scalar(covered[:, :], p_head[:, 0:1], float(E), None, ALU.is_equal))
                    c(dve.tensor_copy(covered_i[:, :], covered[:, :]))
                    c(dve.tensor_scalar(w[:, :, :], w[:, :, :], covered[:, 0:1], None, ALU.mult))
                    for dest, k, source in ((scal, D0, d), (scal, W0_, w), (scal, DP, dp),
                                            (scal_rel, RP, dp), (scal_rel, RT, typ), (scal_rel, RE, te)):
                        dve.tensor_copy(dest[:, :, k:k + G].rearrange("p b g -> p g b"), source[:, :, :]).then_inc(s_rc, 1)
                    for j in range(COLS):
                        c(dve.tensor_scalar(tmp[:, :, :], dc[:, :, :], float(j), None, ALU.is_equal))
                        c(dve.tensor_tensor(scal[:, :, WC + j:WC + G * COLS:COLS].rearrange("p b g -> p g b"),
                                            tmp[:, :, :], w[:, :, :], ALU.mult))
                        c(dve.tensor_scalar(scal_rel[:, :, RC + j:RC + G * COLS:COLS].rearrange("p b g -> p g b"),
                                            tmp[:, :, :], covered[:, 0:1], None, ALU.mult))
                    dve.wait_ge(s_rld, 16)
                    c(dve.tensor_copy(Wr[:, :].rearrange("r (o i) -> r o i", o=C),
                                      rel_in[:, :].rearrange("r (i o) -> r o i", i=C)))

                @block.tensor
                def _(pe):
                    pe.wait_ge(s_id, 1)
                    pe.wait_ge(s_hf, 1)
                    pe.matmul(p_head[:, 0:ET], ones[0:1, :], head[:, :], start=True, stop=True).then_inc(s_hb, 1)
                    pe.wait_ge(s_relw, 64)
                    pe.transpose(p_misc[0:B, 0:R], comp_r[:, :], ident[0:R, 0:R]).then_inc(s_cT, 1)
                    pe.wait_ge(s_rc, 2)
                    pe.matmul(p_misc[0:R, 0:C * C], comp[:, :], bases[:, :], start=True, stop=True)
                    for k in range(3):
                        mm = pe.matmul(p_misc[:, C * C + k * C:C * C + (k + 1) * C], wa_b[:, k, :], ws[:, :],
                                       start=True, stop=True)
                    mm.then_inc(s_cT, 1)
                    for k, tile in enumerate(lanes_f + lanes[3:]):
                        pe.wait_ge(s_lf, min(k + 1, 3))
                        for g in range(G):
                            for q in range(NQ):
                                n = min(P, NB - q * P)
                                mm = pe.transpose(p_win[:, k, g * NB + q * P:g * NB + q * P + n],
                                                  tile[0:n, q, g * P:(g + 1) * P], ident[0:n, 0:n])
                        mm.then_inc(s_tr, 1)
                    pe.wait_ge(s_tot, 1)
                    pe.matmul(p_head[:, 0:1], ones[:, :], total[:, :], start=True, stop=True).then_inc(s_sum, 1)

        def layer_norm(name, store, scale_by):
            with ExitStack() as ph:
                GB = 20
                nodes_n = GB * COLS
                mean = sb(name + "_mean", [BP, 2, nodes_n], F32, ph)
                var = sb(name + "_var", [BP, 2, nodes_n], F32, ph)
                inv = sb(name + "_inv", [BP, 2, nodes_n], F32, ph)
                sq = sb(name + "_sq", [BP, 2, GB * BC], F32, ph)
                s_v = sem(name + "_dve")
                s_cen = sem(name + "_centred")
                s_sq = sem(name + "_squared")
                s_var = sem(name + "_variance_ready")
                s_root = sem(name + "_root_ready")
                s_y = sem(name + "_rows_ready")
                s_store = sem(name + "_rows_stored")
                parts = NB // GB

                def nodes_of_part(tile, k):
                    return tile[:, k * GB * BC:(k + 1) * GB * BC].rearrange("p (n f) -> p n f", f=C)

                with nc.Block() as block:
                    @block.vector
                    def _(dve):
                        c = Chain(dve, s_v)
                        for k in range(parts + 2):
                            if k < parts:
                                m = mean[:, k % 2, :]
                                c(dve.tensor_reduce(m, nodes_of_part(X, k), AX.X, ALU.add))
                                c(dve.tensor_scalar(m, m, 1.0 / C, None, ALU.mult))
                                dve.tensor_tensor(nodes_of_part(Y, k), nodes_of_part(X, k), spread(m, BP, nodes_n, C),
                                                  ALU.subtract).then_inc(s_cen, 1)
                            b = k - 1
                            if 0 <= b < parts:
                                v = var[:, b % 2, :]
                                dve.wait_ge(s_sq, b + 1)
                                c(dve.tensor_reduce(v, sq[:, b % 2, :].rearrange("p (n f) -> p n f", f=C), AX.X, ALU.add))
                                dve.tensor_scalar(v, v, 1.0 / C, 1e-5, ALU.mult, ALU.add).then_inc(s_var, 1)
                            b = k - 2
                            if b >= 0:
                                v = inv[:, b % 2, :]
                                dve.wait_ge(s_root, b + 1)
                                c(dve.reciprocal(v, v))
                                if scale_by is not None:
                                    v3 = v.rearrange("p (b c) -> p b c", c=COLS)
                                    c(dve.tensor_tensor(v3, v3, scale_by[:, b * GB:(b + 1) * GB, :], ALU.mult))
                                dve.scalar_tensor_tensor(out=nodes_of_part(Y, b), in0=nodes_of_part(Y, b), scalar=0.0,
                                                         in1=spread(v, BP, nodes_n, C), op0=ALU.max, op1=ALU.mult
                                                         ).then_inc(s_y, 1)

                    @block.scalar
                    def _(act):
                        for k in range(parts + 1):
                            if k < parts:
                                act.wait_ge(s_cen, k + 1)
                                if k >= 2:
                                    act.wait_ge(s_var, k - 1)
                                act.activation(sq[:, k % 2, :], Y[:, k * GB * BC:(k + 1) * GB * BC], ACT.Square
                                               ).then_inc(s_sq, 1)
                            if k >= 1:
                                act.wait_ge(s_var, k)
                                if k >= 3:
                                    act.wait_ge(s_y, k - 2)
                                act.activation(inv[:, (k - 1) % 2, :], var[:, (k - 1) % 2, :], ACT.Sqrt
                                               ).then_inc(s_root, 1)

                    @block.sync
                    def _(sp):
                        for k in range(parts):
                            sp.wait_ge(s_y, k + 1)
                            sp.dma_start(blocks(store[k * GB * BN:(k + 1) * GB * BN, :]), Yb[:, k * GB:(k + 1) * GB, :]
                                         ).then_inc(s_store, 16)
                        sp.wait_ge(s_store, 16 * parts)

        def uncovered(eng):
            return eng.value_load(covered_i[0:1, 0:1], min_val=0, max_val=1) < 1

        s_in = sem("gp_inputs_loaded")
        s_before = sem("gp_target_prepared")
        s_link = sem("gp_chain")
        s_dg = sem("gp_diagonal_ready")
        s_row = sem("gp_targets_spread")
        s_same = sem("gp_index_ready")
        s_from = sem("gp_source_ready")
        s_rows = sem("gp_rows_gathered")
        s_rowmsg = sem("gp_messages_ready")
        s_comb = sem("gp_sums_ready")
        s_sum_out = sem("gp_sums_copied")
        s_add = sem("gp_sums_added")
        s_after = sem("gp_result_loaded")
        s_is_type = sem("gp_types_compared")
        s_type_turned = sem("gp_types_turned")
        s_type_copied = sem("gp_types_copied")
        s_mat = sem("gp_matrices_selected")
        general_count = {"visits": 0, "in": 0, "before": 0, "after": 0, "from": 0, "rows": 0, "chain": 0}

        def general_path(name, width, target, before, after, tab=None, dots=False):
            before = before + [(target[N:N + EP, :], X[:, 0:width])]
            with ExitStack() as ph:
                dst_i = sb(name + "_dst_i", [EP, ET], I32, ph)
                dst_e = sb(name + "_dst", [EP, ET], F32, ph)
                w_e = sb(name + "_w", [EP, ET], F32, ph)
                src_e = sb(name + "_src", [EP, ET], I32, ph)
                tri = sb(name + "_tri", [EP, EP], F32, ph)
                spare = sb(name + "_spare", [EP, 1], F32, ph)
                diag = sb(name + "_diag", [EP, EP], F32, ph)
                same = sb(name + "_same", [EP, EP], F32, ph)
                low = sb(name + "_low", [EP, EP], F32, ph)
                earlier = sb(name + "_earlier", [EP, 1], F32, ph)
                firsts = sb(name + "_firsts", [EP, 1], F32, ph)
                off = sb(name + "_off", [EP, 1], F32, ph)
                at_f = sb(name + "_at_f", [EP, 1], F32, ph)
                at = sb(name + "_at", [EP, 1], I32, ph)
                from_ = sb(name + "_from", [EP, 1], I32, ph)
                rows = sb(name + "_rows", [EP, width], F32, ph)
                scaled = sb(name + "_scaled", [EP, width], F32, ph)
                dot = sb(name + "_dot", [EP, 1], F32, ph)
                msg = sb(name + "_msg", [EP, width], F32, ph)
                comb = sb(name + "_comb", [EP, width], F32, ph)
                if dots:
                    type_i = sb(name + "_type_i", [EP, ET], I32, ph)
                    type_e = sb(name + "_type", [EP, ET], F32, ph)
                    te_e = sb(name + "_edge_dot", [EP, ET], F32, ph)
                    is_type = sb(name + "_is_type", [EP, R], F32, ph)
                    is_typeT = sb(name + "_is_typeT", [R, EP], F32, ph)
                    prod = sb(name + "_prod", [EP, C, C], F32, ph)
                    u = sb(name + "_u", [EP, C], F32, ph)
                    coef = sb(name + "_coef", [EP, 2], F32, ph)
                    p_type = ps(name + "_p_type", [P, 512], ph)
                    p_mat = ps(name + "_p_mat", [P, 512], ph)
                p_row = ps(name + "_p_row", [EP, 512], ph)
                p_comb = ps(name + "_p_comb", [EP, 512], ph)
                was = dict(general_count)
                visit = was["visits"]
                tiles = visit * ET
                per = 2 if dots else 1
                K = 13 if dots else 7
                loads = 5 if dots else 3
                with nc.Block() as block:
                    @block.sync
                    def _(sp):
                        with sp.If(uncovered(sp)):
                            sp.dma_start(dst_i[:, :], dst.rearrange("(p t) -> p t", t=ET)).then_inc(s_in, 16)
                            sp.dma_start(w_e[:, :], edge_weight.rearrange("(p t) -> p t", t=ET)).then_inc(s_in, 16)
                            sp.dma_start(src_e[:, :], src.rearrange("(p t) -> p t", t=ET)).then_inc(s_in, 16)
                            if dots:
                                sp.dma_start(type_i[:, :], edge_type.rearrange("(p t) -> p t", t=ET)).then_inc(s_in, 16)
                                sp.dma_start(te_e[:, :], te_tab[0:E].rearrange("(p t) -> p t", t=ET)).then_inc(s_in, 16)
                            for o, i in before:
                                sp.dma_start(o, i).then_inc(s_before, 16)
                            sp.wait_ge(s_add, 16 * (tiles + ET))
                            for o, i in after:
                                sp.dma_start(o, i).then_inc(s_after, 16)
                            if after:
                                sp.wait_ge(s_after, 16 * (was["after"] + len(after)))
                            sp.nop()

                    @block.gpsimd
                    def _(pool):
                        with pool.If(uncovered(pool)):
                            hold(pool, s_before, 16 * (was["before"] + len(before)))
                            hold(pool, s_in, 16 * (was["in"] + loads))
                            with pool.Fori(0, ET) as t:
                                if tab is not None:
                                    pool.tensor_copy(from_[:, :], src_e[:, bass.ds(t, 1)]).then_inc(s_from, 1)
                                    hold(pool, s_from, t * per + (was["from"] + 1))
                                    pool.indirect_dma_start(
                                        out=rows[:, :], out_offset=None, in_=tab,
                                        in_offset=bass.IndirectOffsetOnAxis(ap=from_[:, 0:1], axis=0)
                                        ).then_inc(s_rows, 16)
                                if dots:
                                    hold(pool, s_rows, t * 32 + (was["rows"] + 16))
                                    pool.tensor_copy(from_[:, :], dst_i[:, bass.ds(t, 1)]).then_inc(s_from, 1)
                                    hold(pool, s_from, t * 2 + (was["from"] + 2))
                                    pool.indirect_dma_start(
                                        out=dot[:, :], out_offset=None, in_=dot_tab,
                                        in_offset=bass.IndirectOffsetOnAxis(ap=from_[:, 0:1], axis=0)
                                        ).then_inc(s_rows, 16)
                                hold(pool, s_same, t + (tiles + 1))
                                hold(pool, s_sum_out, t + (tiles + 1))
                                pool.indirect_dma_start(
                                    out=target, out_offset=bass.IndirectOffsetOnAxis(ap=at[:, 0:1], axis=0),
                                    in_=comb[:, :], in_offset=None, compute_op=ALU.add).then_inc(s_add, 16)
                                hold(pool, s_add, (t + (tiles + 1)) * 16)
                            pool.nop()

                    @block.tensor
                    def _(pe):
                        with pe.If(uncovered(pe)):
                            with pe.Fori(0, ET) as t:
                                hold(pe, s_dg, t + (tiles + 1))
                                pe.matmul(p_row[:, 0:EP], ones[0:EP, 0:EP], diag[:, :], start=True, stop=True
                                          ).then_inc(s_row, 1)
                                if dots:
                                    hold(pe, s_is_type, t + 1)
                                    pe.transpose(p_type[0:R, 0:EP], is_type[:, :], ident[0:EP, 0:EP]
                                                 ).then_inc(s_type_turned, 1)
                                    hold(pe, s_type_copied, t + 1)
                                    pe.matmul(p_mat[0:EP, 0:C * C], is_typeT[:, :], Wr[:, :], start=True, stop=True
                                              ).then_inc(s_mat, 1)
                                hold(pe, s_same, t + (tiles + 1))
                                hold(pe, s_rowmsg, t + (tiles + 1))
                                pe.matmul(p_comb[:, 0:width], same[:, :], msg[:, :], start=True, stop=True
                                          ).then_inc(s_comb, 1)
                            pe.nop()

                    @block.vector
                    def _(dve):
                        with dve.If(uncovered(dve)):
                            c = Chain(dve, s_link, was["chain"])
                            dve.wait_ge(s_in, 16 * (was["in"] + loads))
                            c(dve.tensor_copy(dst_e[:, :], dst_i[:, :]))
                            c(dve.tensor_scalar(tri[:, :], nodes[0:EP, 0:EP], part[0:EP, 0:1], None, ALU.is_lt))
                            c(dve.tensor_scalar(spare[:, :], part[0:EP, :], float(N), None, ALU.add))
                            if dots:
                                c(dve.tensor_copy(type_e[:, :], type_i[:, :]))
                            n0 = c.n
                            general_count["chain"] = n0 + ET * K
                            with dve.Fori(0, ET) as t:
                                def link(ins, k):
                                    ins.then_inc(s_link, 1)
                                    hold(dve, s_link, t * K + n0 + k)
                                col = dst_e[:, bass.ds(t, 1)]
                                dve.tensor_scalar(diag[:, :], ident[0:EP, 0:EP], col, None, ALU.mult).then_inc(s_dg, 1)
                                hold(dve, s_row, t + (tiles + 1))
                                link(dve.tensor_scalar(same[:, :], p_row[:, 0:EP], col, None, ALU.is_equal), 1)
                                link(dve.tensor_tensor(low[:, :], same[:, :], tri[:, :], ALU.mult), 2)
                                link(dve.tensor_reduce(earlier[:, :], low[:, :], AX.X, ALU.add), 3)
                                link(dve.tensor_scalar(firsts[:, :], earlier[:, :], 0.0, None, ALU.is_equal), 4)
                                link(dve.tensor_tensor(off[:, :], col, spare[:, :], ALU.subtract), 5)
                                link(dve.scalar_tensor_tensor(out=at_f[:, :], in0=off[:, :], scalar=firsts[:, 0:1],
                                                              in1=spare[:, :], op0=ALU.mult, op1=ALU.add), 6)
                                dve.tensor_copy(at[:, :], at_f[:, :]).then_inc(s_same, 1)
                                w_col = w_e[:, bass.ds(t, 1)]
                                if dots:
                                    dve.tensor_scalar(is_type[:, :], nodes[0:EP, 0:R], type_e[:, bass.ds(t, 1)], None,
                                                      ALU.is_equal).then_inc(s_is_type, 1)
                                    hold(dve, s_type_turned, t + 1)
                                    dve.tensor_copy(is_typeT[:, :], p_type[0:R, 0:EP]).then_inc(s_type_copied, 1)
                                    hold(dve, s_rows, t * 32 + (was["rows"] + 32))
                                    hold(dve, s_mat, t + 1)
                                    link(dve.tensor_tensor(
                                        prod[:, :, :], p_mat[0:EP, 0:C * C].rearrange("p (o i) -> p o i", i=C),
                                        rows[:, :].rearrange("p (a i) -> p a i", a=1).broadcast_to([EP, C, C]),
                                        ALU.mult), 7)
                                    link(dve.tensor_reduce(u[:, :], prod[:, :, :], AX.X, ALU.add), 8)
                                    link(dve.tensor_tensor(scaled[:, :], rows[:, :], v_rel[0:EP, 0:C], ALU.mult), 9)
                                    link(dve.tensor_reduce(coef[:, 0:1], scaled[:, :], AX.X, ALU.add), 10)
                                    link(dve.tensor_tensor(coef[:, 1:2], coef[:, 0:1], te_e[:, bass.ds(t, 1)],
                                                           ALU.add), 11)
                                    link(dve.tensor_tensor(coef[:, 0:1], coef[:, 1:2], dot[:, :], ALU.add), 12)
                                    link(dve.tensor_scalar(scaled[:, :], u[:, :], coef[:, 0:1], None, ALU.mult), 13)
                                    dve.tensor_copy(msg[:, :], scaled[:, :]).then_inc(s_rowmsg, 1)
                                elif tab is not None:
                                    hold(dve, s_rows, t * 16 + (was["rows"] + 16))
                                    link(dve.tensor_scalar(scaled[:, :], rows[:, :], w_col, None, ALU.mult), 7)
                                    dve.tensor_scalar(msg[:, :], scaled[:, :], 0.5, None, ALU.mult).then_inc(s_rowmsg, 1)
                                else:
                                    link(dve.tensor_copy(low[:, 0:1], w_col), 7)
                                    dve.tensor_copy(msg[:, :], low[:, 0:1]).then_inc(s_rowmsg, 1)
                                hold(dve, s_comb, t + (tiles + 1))
                                dve.tensor_copy(comb[:, :], p_comb[:, 0:width]).then_inc(s_sum_out, 1)
                                hold(dve, s_add, (t + (tiles + 1)) * 16)
                            dve.nop()
            general_count["visits"] += 1
            general_count["before"] += len(before)
            general_count["after"] += len(after)
            general_count["in"] += loads
            general_count["from"] += per * ET if tab is not None else 0
            general_count["rows"] += 16 * per * ET if tab is not None else 0

        s_clr = sem("ring_cleared")
        cleared = {"times": 0}

        def gather_blocks(pool, tab, rows, idx, s_ix, s_g, s_used):
            cleared["times"] += 1
            pool.memset(rows[:, :, :, :], 0.0).then_inc(s_clr, 1)
            hold(pool, s_clr, cleared["times"])
            limit = pool.to_reg(N - 1)

            def index(b):
                if b.from_(UNROLL):
                    hold(pool, s_g[b.slot], b.round * 16 * G)
                pool.tensor_copy(idx[:, b.slot, :], src_slot[:, bass.ds(b.n, 1), :].rearrange("p b g -> p (b g)")
                                 ).then_inc(s_ix, 1)

            def step(t):
                if t.back(-1).has():
                    index(t.back(-1))
                if not t.has():
                    return
                hold(pool, s_ix, t.n + 1)
                if t.from_(UNROLL):
                    hold(pool, s_used, t.n - (UNROLL - 1))
                for g in range(G):
                    pool.indirect_dma_start(
                        out=rows[:, t.slot, g, :], out_offset=None, in_=tab,
                        in_offset=bass.IndirectOffsetOnAxis(ap=idx[:, t.slot, g:g + 1], axis=0),
                        bounds_check=limit, oob_is_err=False).then_inc(s_g[t.slot], 16)
            index(Step(0, 0))
            run_steps(pool, step, ahead=1)

        def scalars_of(b, lo, hi, tab=scal, parts=P):
            return tab[0:parts, bass.ds(b.n, 1), lo:hi].rearrange("p b k -> p (b k)")

        with ExitStack() as ph:
            sc = sb("dg_scalars", [P, 4, KS - DP], F32, ph)
            oh = sb("dg_oh", [P, 4, G, BP], F32, ph)
            acc = ps("dg_acc", [P, 4, 512], ph)
            s_sc = sem("dg_scalars_staged")
            s_oh = sem("dg_onehot_ready")
            s_mm = sem("dg_block_summed")
            s_fin = sem("dg_block_finished")
            with nc.Block() as block:
                @block.scalar
                def _(act):
                    def stage(b):
                        if b.from_(4):
                            hold(act, s_mm, b.n - 3)
                        act.copy(sc[:, b.slot, :], scalars_of(b, DP, KS)).then_inc(s_sc, 1)

                    def step(t):
                        if t.back(-1).has():
                            stage(t.back(-1))
                        b = t.back(2)
                        if b.has():
                            hold(act, s_mm, b.n + 1)
                            act.copy(scalars_of(b, DI, DI + COLS, parts=BP), acc[0:BP, b.slot, 0:COLS]).then_inc(s_fin, 1)
                    stage(Step(0, 0))
                    run_steps(act, step, ahead=1, drain=2)

                @block.vector
                def _(dve):
                    def step(b):
                        dve.wait_ge(s_sc, b.n + 1)
                        if b.from_(4):
                            dve.wait_ge(s_mm, b.n - 3)
                        for g in range(G):
                            ins = dve.tensor_scalar(oh[:, b.slot, g, :], nodes[:, 0:BP], sc[:, b.slot, g:g + 1], None,
                                                    ALU.is_equal)
                        ins.then_inc(s_oh, 1)
                    run_steps(dve, step)

                @block.tensor
                def _(pe):
                    def step(b):
                        hold(pe, s_oh, b.n + 1)
                        if b.from_(4):
                            hold(pe, s_fin, b.n - 3)
                        for g in range(G):
                            mm = pe.matmul(acc[0:BP, b.slot, 0:COLS], oh[:, b.slot, g, :],
                                           sc[:, b.slot, G + g * COLS:G + (g + 1) * COLS],
                                           start=g == 0, stop=g == G - 1)
                        mm.then_inc(s_mm, 1)
                    run_steps(pe, step)

        with ExitStack() as ph:
            nodes_of = "(b p c) a -> p b (c a)"
            deg_rows = deg_tab[0:N, :].rearrange(nodes_of, p=BP, c=COLS)
            general_path("gd", 1, deg_tab, [(deg_rows, dinv3)], [(dinv3, deg_rows)])
            pos = sb("di_pos", [BP, NB, COLS], F32, ph)
            dinv = sb("di_dinv", [BP, NB, COLS], F32, ph)
            s_d1 = sem("di_dve")
            s_guard = sem("di_guarded")
            s_root = sem("di_root")
            with nc.Block() as block:
                @block.vector
                def _(dve):
                    c = Chain(dve, s_d1)
                    c(dve.tensor_scalar(dinv[:, :, :], dinv3, 2.0, None, ALU.add))
                    c(dve.tensor_scalar(pos[:, :, :], dinv[:, :, :], 0.0, None, ALU.is_gt))
                    c(dve.tensor_tensor(dinv[:, :, :], dinv[:, :, :], pos[:, :, :], ALU.mult))
                    c(dve.tensor_tensor(dinv[:, :, :], dinv[:, :, :], pos[:, :, :], ALU.subtract))
                    dve.tensor_scalar(dinv[:, :, :], dinv[:, :, :], 1.0, None, ALU.add).then_inc(s_guard, 1)
                    dve.wait_ge(s_root, 1)
                    c(dve.reciprocal(dinv[:, :, :], dinv[:, :, :]))
                    c(dve.tensor_tensor(dinv3, dinv[:, :, :], pos[:, :, :], ALU.mult))
                    c(dve.tensor_tensor(dinv_sq, dinv3, dinv3, ALU.mult))

                @block.scalar
                def _(act):
                    act.wait_ge(s_guard, 1)
                    act.activation(dinv[:, :, :], dinv[:, :, :], ACT.Sqrt).then_inc(s_root, 1)

        layer_norm("ln0", yn_tab, dinv3)

        sum_rows = blocks(sum_tab[0:N, :])
        general_path("g0g", C, sum_tab, [(sum_rows, Yb)], [(Yb, sum_rows)], tab=yn_tab)

        def narrow_layer(name, first):
            CUT = 3
            DN, QN, PN, WNC = 0, COLS, 2 * COLS, 2 * COLS + G
            with ExitStack() as ph:
                rows = sb(name + "_rows", [P, 4, G, C], F32, ph)
                idx = sb(name + "_idx", [P, 4, G], I32, ph)
                sc = sb(name + "_scalars", [P, 4, KS - DI], F32, ph)
                oh = sb(name + "_oh", [P, 2, G, BP], F32, ph)
                rowx = sb(name + "_rowx", [P, 2, G, BC], F32, ph)
                s1 = sb(name + "_s1", [BP, 2, BC], F32, ph)
                s2 = sb(name + "_s2", [BP, 4, BC + COLS], F32, ph)
                acc = ps(name + "_acc", [P, 2, 512], ph)
                s_ix = sem(name + "_index_ready")
                s_g = [sem(f"{name}_rows_gathered{u}") for u in range(4)]
                s_sc = sem(name + "_scalars_staged")
                s_oh = sem(name + "_operands_ready")
                s_mm = sem(name + "_block_summed")
                s_f = sem(name + "_own_added")
                s_s = sem(name + "_sums_ready")
                s_b = sem(name + "_bias_added")
                if first:
                    sumT = sb(name + "_sumT", [BC + COLS, 2, BP], F32, ph)
                    post = sb(name + "_post", [BP, 2, COLS * H], F32, ph)
                    p_t = ps(name + "_p_t", [P, 2, 512], ph)
                    p_z = ps(name + "_p_z", [P, 2, 2, 512], ph)
                    s_dv = sem(name + "_dinv_placed")
                    s_t = sem(name + "_turned")
                    s_tc = sem(name + "_turned_copied")
                    s_z = sem(name + "_product")
                    s_y = [sem(name + "_result_vector"), sem(name + "_result_scalar")]
                    s_st = [sem(f"{name}_stored{u}") for u in range(2)]
                with nc.Block() as block:
                    @block.gpsimd
                    def _(pool):
                        gather_blocks(pool, yn_tab, rows, idx, s_ix, s_g, s_oh)

                    @block.vector
                    def _(dve):
                        def operands(b):
                            dve.wait_ge(s_sc, b.n + 1)
                            if b.from_(2):
                                dve.wait_ge(s_mm, b.n - 1)
                            for g in range(G):
                                dve.tensor_scalar(oh[:, b.par, g, :], nodes[:, 0:BP], sc[:, b.slot, PN + g:PN + g + 1],
                                                  None, ALU.is_equal)
                            dve.wait_ge(s_g[b.slot], (b.round + 1) * 16 * G)
                            dve.tensor_tensor(
                                rowx[:, b.par, :, :].rearrange("p g (c f) -> p g c f", f=C),
                                rows[:, b.slot, :, :].rearrange("p g (a f) -> p g a f", a=1).broadcast_to([P, G, COLS, C]),
                                sc[:, b.slot, WNC:WNC + G * COLS].rearrange("p (g c a) -> p g c a", g=G, a=1)
                                .broadcast_to([P, G, COLS, C]), ALU.mult).then_inc(s_oh, 1)

                        def step(t):
                            if t.has():
                                operands(t)
                            b = t.back(1)
                            if b.has():
                                dve.wait_ge(s_mm, b.n + 1)
                                dve.scalar_tensor_tensor(out=s1[:, b.par, :], in0=Y[:, bass.ds(b.n * BC, BC)], scalar=2.0,
                                                         in1=acc[0:BP, b.par, 0:BC], op0=ALU.mult, op1=ALU.add
                                                         ).then_inc(s_f, 1)
                                if first and b.from_(4):
                                    dve.wait_ge(s_t, b.n - 3)
                                dve.wait_ge(s_f, b.n + 1)
                                by = QN if first else DN
                                dve.tensor_tensor(s2[:, b.slot, 0:BC].rearrange("p (c f) -> p c f", f=C),
                                                  s1[:, b.par, :].rearrange("p (c f) -> p c f", f=C),
                                                  spread(sc[0:BP, b.slot, by:by + COLS], BP, COLS, C), ALU.mult
                                                  ).then_inc(s_s, 1)
                                if not first:
                                    x_ = X[:, bass.ds(b.n * BC, BC)]
                                    x3 = x_.rearrange("p (c f) -> p c f", f=C)
                                    dve.tensor_tensor(x3, x3, bias3[0:BP, :].rearrange("p (a f) -> p a f", a=1)
                                                      .broadcast_to([BP, COLS, C]), ALU.add).then_inc(s_b, 1)
                                    dve.wait_ge(s_s, b.n + 1)
                                    dve.wait_ge(s_b, b.n + 1)
                                    dve.tensor_tensor(x_, x_, s2[:, b.slot, 0:BC], ALU.add)
                            b = t.back(4)
                            if first and b.has():
                                dve.wait_ge(s_z, b.n + 1)
                                if b.from_(2):
                                    dve.wait_ge(s_st[b.par], 16 * b.round2)
                                dve.tensor_scalar(post[:, b.par, 0:CUT * H], p_z[0:BP, b.par, 0, 0:CUT * H],
                                                  0.0, None, ALU.max).then_inc(s_y[0], 1)
                        run_steps(dve, step, drain=4 if first else 1)

                    @block.tensor
                    def _(pe):
                        def step(t):
                            if t.has():
                                hold(pe, s_oh, t.n + 1)
                                if t.from_(2):
                                    hold(pe, s_f, t.n - 1)
                                for g in range(G):
                                    mm = pe.matmul(acc[0:BP, t.par, 0:BC], oh[:, t.par, g, :], rowx[:, t.par, g, :],
                                                   start=g == 0, stop=g == G - 1)
                                mm.then_inc(s_mm, 1)
                            b = t.back(2)
                            if first and b.has():
                                hold(pe, s_s, b.n + 1)
                                hold(pe, s_dv, b.n + 1)
                                if b.from_(2):
                                    hold(pe, s_tc, b.n - 1)
                                pe.transpose(p_t[0:BC + COLS, b.par, 0:BP], s2[:, b.slot, :], ident[0:BP, 0:BP]
                                             ).then_inc(s_t, 1)
                            b = t.back(3)
                            if first and b.has():
                                hold(pe, s_tc, b.n + 1)
                                if b.from_(2):
                                    hold(pe, s_y[0], b.n - 1)
                                    hold(pe, s_y[1], b.n - 1)
                                pe.matmul(p_z[0:BP, b.par, 0, 0:CUT * H], sumT[:, b.par, :], W0x[:, 0:CUT * H],
                                          start=True, stop=True)
                                pe.matmul(p_z[0:BP, b.par, 1, 0:(COLS - CUT) * H], sumT[:, b.par, :],
                                          W0x[:, CUT * H:], start=True, stop=True).then_inc(s_z, 1)
                        run_steps(pe, step, drain=3 if first else 0)

                    @block.scalar
                    def _(act):
                        def stage(b):
                            if b.from_(4):
                                hold(act, s_s, b.n - 3)
                            act.copy(sc[:, b.slot, :], scalars_of(b, DI, KS)).then_inc(s_sc, 1)

                        def step(t):
                            if t.back(-1).has():
                                stage(t.back(-1))
                            if first and t.has():
                                if t.from_(4):
                                    hold(act, s_t, t.n - 3)
                                hold(act, s_sc, t.n + 1)
                                act.copy(s2[:, t.slot, BC:BC + COLS], sc[0:BP, t.slot, DN:DN + COLS]).then_inc(s_dv, 1)
                            b = t.back(2)
                            if first and b.has():
                                hold(act, s_t, b.n + 1)
                                if b.from_(2):
                                    hold(act, s_z, b.n - 1)
                                act.copy(sumT[:, b.par, :], p_t[0:BC + COLS, b.par, 0:BP]).then_inc(s_tc, 1)
                            b = t.back(4)
                            if first and b.has():
                                hold(act, s_z, b.n + 1)
                                if b.from_(2):
                                    hold(act, s_st[b.par], 16 * b.round2)
                                act.activation(post[:, b.par, CUT * H:COLS * H], p_z[0:BP, b.par, 1, 0:(COLS - CUT) * H],
                                               ACT.Relu).then_inc(s_y[1], 1)
                        stage(Step(0, 0))
                        run_steps(act, step, ahead=1, drain=4 if first else 0)

                    if first:
                        @block.sync
                        def _(sp):
                            def step(b):
                                sp.wait_ge(s_y[0], b.n + 1)
                                sp.wait_ge(s_y[1], b.n + 1)
                                sp.dma_start(rows_of(y1_tab, b), post[:, b.par, :]).then_inc(s_st[b.par], 16)
                            run_steps(sp, step)
                            for u in range(2):
                                sp.wait_ge(s_st[u], 16 * (NB // 2))

        narrow_layer("l0", True)

        def wide_layer(name, tab, Wt, y_out):
            narrow = y_out is None
            KW = DQ
            at = [sum(hi - lo for lo, hi in SPAN[:g]) for g in range(G + 1)]
            with ExitStack() as ph:
                rows = sb(name + "_rows", [P, 4, G, H], F32, ph)
                idx = sb(name + "_idx", [P, 4, G], I32, ph)
                sc = sb(name + "_scalars", [P, 4, KW], F32, ph)
                oh = sb(name + "_oh", [P, 2, at[G]], F32, ph)
                own = sb(name + "_own", [BP, 2, COLS * H], F32, ph)
                ownT = sb(name + "_ownT2", [P, 2, COLS, BP], F32, ph)
                sumT = sb(name + "_sumT", [P, 2, COLS, BP], F32, ph)
                pre = sb(name + "_pre", [BP, 2, COLS * H], F32, ph)
                post = sb(name + "_post", [P, 2, COLS, BP] if narrow else [BP, 2, COLS, H], F32, ph)
                p_sum = ps(name + "_p_sum", [P, 1024], ph)
                p_own = ps(name + "_p_own", [P, 1024], ph)
                p_z = ps(name + "_p_z", [P, 1024], ph)
                p_h = ps(name + "_p_h", [P, 1024], ph) if narrow else None
                s_ix = sem(name + "_index_ready")
                s_g = [sem(f"{name}_rows_gathered{u}") for u in range(4)]
                s_sc = sem(name + "_scalars_staged")
                s_own = [sem(f"{name}_own_loaded{u}") for u in range(2)]
                s_oh = sem(name + "_onehot_ready")
                s_mm = sem(name + "_block_summed")
                s_turn = sem(name + "_own_turned")
                s_twice = sem(name + "_own_copied")
                s_T = sem(name + "_sums_ready")
                s_z = sem(name + "_product")
                s_e = sem(name + "_preactivation")
                s_post = sem(name + "_activated")
                if narrow:
                    s_h = sem(name + "_hidden_turned")
                    s_y = sem(name + "_narrow_product")
                    s_p = sem(name + "_narrow_rows")
                else:
                    s_st = [sem(f"{name}_stored{u}") for u in range(2)]

                def chunks(ap):
                    return ap[:, 0:COLS * P].rearrange("f (c p) -> f c p", c=COLS)[:, :, 0:BP]

                with nc.Block() as block:
                    @block.gpsimd
                    def _(pool):
                        gather_blocks(pool, tab, rows, idx, s_ix, s_g, s_mm)

                    @block.sync
                    def _(sp):
                        def load(b, own_tab):
                            if b.from_(2):
                                sp.wait_ge(s_turn, b.n - 1)
                            sp.dma_start(own[:, b.par, :], rows_of(own_tab, b)).then_inc(s_own[b.par], 16)
                        with sp.If(uncovered(sp)):
                            run_steps(sp, lambda b: load(b, u_tab))
                        with sp.Else():
                            run_steps(sp, lambda b: load(b, tab))

                    @block.vector
                    def _(dve):
                        def onehot(b):
                            dve.wait_ge(s_sc, b.n + 1)
                            if b.from_(2):
                                dve.wait_ge(s_mm, b.n - 1)
                            for g, (lo, hi) in enumerate(SPAN):
                                ins = dve.tensor_scalar(oh[:, b.par, at[g]:at[g + 1]], nodes[:, lo:hi],
                                                        sc[:, b.slot, D0 + g:D0 + g + 1], sc[:, b.slot, W0_ + g:W0_ + g + 1],
                                                        ALU.is_equal, ALU.mult)
                            ins.then_inc(s_oh, 1)

                        def step(t):
                            if t.has():
                                dve.wait_ge(s_mm, t.n + 1)
                                dve.wait_ge(s_twice, t.n + 1)
                                if t.from_(2):
                                    dve.wait_ge(s_z, t.n - 1)
                                for lo, hi, bank in ((0, HALF // COLS, 0), (HALF // COLS, BP, 512)):
                                    ins = dve.tensor_tensor(
                                        sumT[:, t.par, :, lo:hi],
                                        p_sum[:, bank:bank + (hi - lo) * COLS].rearrange("f (p c) -> f c p", c=COLS),
                                        ownT[:, t.par, :, lo:hi], ALU.add)
                                ins.then_inc(s_T, 1)
                            b = t.back(3)
                            if narrow and b.has():
                                dve.wait_ge(s_y, b.n + 1)
                                dve.tensor_tensor(
                                    Y[:, bass.ds(b.n * BC, BC)].rearrange("p (c f) -> p c f", f=C),
                                    p_h[0:BP, COLS * P:COLS * P + BC].rearrange("p (c f) -> p c f", f=C),
                                    spread(scalars_of(b, DI, DI + COLS, parts=BP), BP, COLS, C), ALU.mult
                                    ).then_inc(s_p, 1)
                            b = t.back(1)
                            if b.has():
                                dve.wait_ge(s_z, b.n + 1)
                                if b.from_(2):
                                    dve.wait_ge(s_h if narrow else s_post, b.n - 1)
                                if narrow:
                                    dve.tensor_tensor(
                                        pre[:, b.par, :].rearrange("p (c f) -> p c f", f=H),
                                        p_z[0:BP, 0:COLS * H].rearrange("p (c f) -> p c f", f=H),
                                        spread(sc[0:BP, b.slot, DI:DI + COLS], BP, COLS, H), ALU.mult).then_inc(s_e, 1)
                                else:
                                    for c in range(COLS):
                                        ins = dve.scalar_tensor_tensor(
                                            out=pre[:, b.par, c * H:(c + 1) * H], in0=p_z[0:BP, c * H:(c + 1) * H],
                                            scalar=sc[0:BP, b.slot, DI + c:DI + c + 1], in1=bias1[0:BP, :],
                                            op0=ALU.mult, op1=ALU.add)
                                    ins.then_inc(s_e, 1)
                            if t.back(-2).has():
                                onehot(t.back(-2))
                        onehot(Step(0, 0))
                        onehot(Step(0, 1))
                        run_steps(dve, step, ahead=1, drain=3)

                    @block.tensor
                    def _(pe):
                        def sums(b):
                            hold(pe, s_own[b.par], (b.round2 + 1) * 16)
                            if b.from_(1):
                                hold(pe, s_twice, b.n)
                            for c in range(COLS):
                                mm = pe.transpose(p_own[:, c * P:c * P + BP], own[:, b.par, c * H:(c + 1) * H],
                                                  ident[0:BP, 0:BP])
                            mm.then_inc(s_turn, 1)
                            hold(pe, s_oh, b.n + 1)
                            hold(pe, s_g[b.slot], (b.round + 1) * 16 * G)
                            if b.from_(1):
                                hold(pe, s_T, b.n)
                            parts = ((1, 1, HALF, BN), (0, 0, 0, HALF), (1, 0, HALF, SPAN[0][1]),
                                     (0, 1, SPAN[1][0], HALF), (1, 2, SPAN[2][0], BN))
                            for k, (bank, g, lo, hi) in enumerate(parts):
                                out_at = 512 * bank + lo - HALF * bank
                                oh_at = at[g] + lo - SPAN[g][0]
                                mm = pe.matmul(p_sum[:, out_at:out_at + hi - lo], rows[:, b.slot, g, :],
                                               oh[:, b.par, oh_at:oh_at + hi - lo], start=k < 2, stop=k > 2)
                            mm.then_inc(s_mm, 1)

                        def step(t):
                            if t.back(-1).has():
                                sums(t.back(-1))
                            b = t.back(2)
                            if narrow and b.has():
                                hold(pe, s_post, b.n + 1)
                                for c in range(COLS):
                                    mm = pe.matmul(p_h[0:BP, COLS * P + c * C:COLS * P + (c + 1) * C],
                                                   post[:, b.par, c, :], W3[:, :], start=True, stop=True)
                                mm.then_inc(s_y, 1)
                            if t.has():
                                hold(pe, s_T, t.n + 1)
                                if t.from_(1):
                                    hold(pe, s_e, t.n)
                                for c in range(COLS):
                                    mm = pe.matmul(p_z[0:BP, c * H:(c + 1) * H], sumT[:, t.par, c, :], Wt[:, :],
                                                   start=True, stop=True)
                                mm.then_inc(s_z, 1)
                            b = t.back(1)
                            if narrow and b.has():
                                hold(pe, s_e, b.n + 1)
                                if b.from_(1):
                                    hold(pe, s_p, b.n)
                                for c in range(COLS):
                                    mm = pe.transpose(p_h[:, c * P:c * P + BP], pre[:, b.par, c * H:(c + 1) * H],
                                                      ident[0:BP, 0:BP])
                                mm.then_inc(s_h, 1)
                        sums(Step(0, 0))
                        run_steps(pe, step, ahead=1, drain=2)

                    @block.scalar
                    def _(act):
                        def stage(b):
                            if b.from_(4):
                                hold(act, s_e, b.n - 3)
                            act.copy(sc[:, b.slot, :], scalars_of(b, 0, KW)).then_inc(s_sc, 1)

                        def twice(b):
                            hold(act, s_turn, b.n + 1)
                            if b.from_(2):
                                hold(act, s_T, b.n - 1)
                            act.mul(ownT[:, b.par, :, :], chunks(p_own), 2.0).then_inc(s_twice, 1)

                        def step(t):
                            if not narrow and t.back(-2).has():
                                stage(t.back(-2))
                            if t.back(-1).has():
                                twice(t.back(-1))
                            if narrow and t.back(-3).has():
                                stage(t.back(-3))
                            b = t.back(1)
                            if not b.has():
                                return
                            if narrow:
                                hold(act, s_h, b.n + 1)
                                if b.from_(2):
                                    hold(act, s_y, b.n - 1)
                                act.activation(post[:, b.par, :, :], chunks(p_h), ACT.Relu,
                                               bias=bias2[:, 0:1]).then_inc(s_post, 1)
                                return
                            hold(act, s_e, b.n + 1)
                            hold(act, s_sc, b.n + 1)
                            if b.from_(2):
                                hold(act, s_st[b.par], 16 * b.round2)
                            for c in range(COLS):
                                ins = act.activation(post[:, b.par, c, :], pre[:, b.par, c * H:(c + 1) * H], ACT.Relu,
                                                     scale=sc[0:BP, b.slot, DI + c:DI + c + 1])
                            ins.then_inc(s_post, 1)
                            act.wait_ge(s_post, b.n + 1)
                            act.dma_start(rows_of(y_out, b), post[:, b.par, :, :].rearrange("p c f -> p (c f)")
                                          ).then_inc(s_st[b.par], 16)
                        stage(Step(0, 0))
                        stage(Step(0, 1))
                        if narrow:
                            stage(Step(0, 2))
                        twice(Step(0, 0))
                        run_steps(act, step, ahead=1, drain=1)
                        if not narrow:
                            for u in range(2):
                                act.wait_ge(s_st[u], 16 * (NB // 2))

        own_wide = u_tab[0:N, :]
        general_path("g1g", H, u_tab, [(own_wide, y1_tab)], [], tab=y1_tab)
        wide_layer("l1", y1_tab, W1, y2_tab)
        general_path("g2g", H, u_tab, [(own_wide, y2_tab)], [], tab=y2_tab)
        wide_layer("l2", y2_tab, W2, None)

        s_y3 = sem("y3_stored")
        with nc.Block() as block:
            @block.sync
            def _(sp):
                sp.dma_start(blocks(yn_tab), Yb).then_inc(s_y3, 16)
                sp.wait_ge(s_y3, 16)
        general_path("g3g", C, sum_tab, [(sum_rows, Yb)], [(Yb, sum_rows)], tab=yn_tab)
        narrow_layer("l3", False)

        layer_norm("ln1", yn_tab, None)
        with ExitStack() as ph:
            dtmp = sb("rd_tmp", [BP, 20 * BC], F32, ph)
            s_dr = sem("rd_dst_dots")
            with nc.Block() as block:
                @block.vector
                def _(dve):
                    c = Chain(dve, s_dr)
                    for lo in range(0, NB, 20):
                        d4 = dtmp[:, :].rearrange("p (b c f) -> p b c f", c=COLS, f=C)
                        d3 = dtmp[:, :].rearrange("p (n f) -> p n f", f=C)
                        c(dve.tensor_tensor(d3, Y[:, lo * BC:(lo + 20) * BC].rearrange("p (n f) -> p n f", f=C),
                                            v_rel[0:BP, 2 * C:3 * C].rearrange("p (a f) -> p a f", a=1)
                                            .broadcast_to([BP, 20 * COLS, C]), ALU.mult))
                        c(dve.tensor_reduce(drow3[:, lo:lo + 20, :], d4, AX.X, ALU.add))

        general_path("grg", C, sum_tab, [(sum_rows, Xb), (dot_tab.rearrange(nodes_of, p=BP, c=COLS), drow3)],
                     [(Xb, sum_rows)], tab=yn_tab, dots=True)
        with ExitStack() as ph:
            rows = sb("rl_rows", [P, 4, G, C], F32, ph)
            idx = sb("rl_idx", [P, 4, G], I32, ph)
            sc = sb("rl_scalars", [P, 4, RD], F32, ph)
            oh = sb("rl_oh", [P, 4, G, BP], F32, ph)
            typ = sb("rl_type", [P, 2, G, R], F32, ph)
            typT = sb("rl_typeT", [R, 2, G * P], F32, ph)
            prod = sb("rl_prod", [P, G, C, C], F32, ph)
            dots = sb("rl_dots", [P, G, C], F32, ph)
            s_src = sb("rl_src_dot", [P, G], F32, ph)
            coef = sb("rl_coef", [P, G], F32, ph)
            msg = sb("rl_msg", [P, G, 2, C], F32, ph)
            msgx = sb("rl_msgx", [P, 2, G, COLS, 2 * C], F32, ph)
            d_u = sb("rl_d_times_sum", [BP, 2, COLS, C], F32, ph)
            p_t = ps("rl_p_t", [P, 2, 512], ph)
            p_w = ps("rl_p_w", [P, 2, 1024], ph)
            acc = ps("rl_acc", [P, 2, 512], ph)
            s_ix = sem("rl_index_ready")
            s_g = [sem(f"rl_rows_gathered{k}") for k in range(4)]
            s_sc = sem("rl_scalars_staged")
            s_ty = sem("rl_types_compared")
            s_tt = sem("rl_types_turned")
            s_tc = sem("rl_types_copied")
            s_w = sem("rl_matrices_selected")
            s_pr = sem("rl_products")
            s_do = sem("rl_dots")
            s_sd = sem("rl_source_dots")
            s_co = sem("rl_coefficients")
            s_u = sem("rl_rows_times_matrix")
            s_ue = sem("rl_rows_weighted")
            s_m = sem("rl_messages_ready")
            s_mm = sem("rl_block_summed")
            s_f = sem("rl_block_read")
            with nc.Block() as block:
                @block.gpsimd
                def _(pool):
                    gather_blocks(pool, yn_tab, rows, idx, s_ix, s_g, s_m)

                @block.scalar
                def _(act):
                    def stage(b):
                        if b.from_(4):
                            hold(act, s_m, b.n - 3)
                        act.copy(sc[:, b.slot, :], scalars_of(b, 0, RD, tab=scal_rel)).then_inc(s_sc, 1)

                    def step(t):
                        if t.back(-1).has():
                            stage(t.back(-1))
                        if t.has():
                            hold(act, s_tt, t.n + 1)
                            if t.from_(2):
                                hold(act, s_w, t.n - 1)
                            act.copy(typT[:, t.par, :], p_t[0:R, t.par, 0:G * P]).then_inc(s_tc, 1)
                    stage(Step(0, 0))
                    run_steps(act, step, ahead=1)

                @block.vector
                def _(dve):
                    def operands(b):
                        dve.wait_ge(s_sc, b.n + 1)
                        if b.from_(2):
                            dve.wait_ge(s_tt, b.n - 1)
                        dve.tensor_tensor(
                            typ[:, b.par, :, :], nodes[:, 0:R].rearrange("p (a r) -> p a r", a=1).broadcast_to([P, G, R]),
                            spread(sc[:, b.slot, RT:RT + G], P, G, R), ALU.is_equal).then_inc(s_ty, 1)
                        if b.from_(4):
                            dve.wait_ge(s_mm, b.n - 3)
                        for g in range(G):
                            dve.tensor_scalar(oh[:, b.slot, g, :], nodes[:, 0:BP], sc[:, b.slot, RP + g:RP + g + 1], None,
                                              ALU.is_equal)

                    def step(t):
                        if t.has():
                            operands(t)
                        b = t.back(2)
                        if b.has():
                            products(b)
                        if t.back(3).has():
                            add_sums(t.back(3))
                        if b.has():
                            messages(b)
                        if t.back(3).has():
                            finish(t.back(3))

                    def products(b):
                        dve.wait_ge(s_g[b.slot], (b.round + 1) * 16 * G)
                        dve.tensor_tensor(dots[:, :, :], rows[:, b.slot, :, :],
                                          v_rel[:, 0:C].rearrange("p (a f) -> p a f", a=1).broadcast_to([P, G, C]),
                                          ALU.mult).then_inc(s_do, 1)
                        dve.wait_ge(s_w, b.n + 1)
                        dve.tensor_tensor(
                            prod[:, :, :, :], p_w[:, b.par, 0:G * C * C].rearrange("p (g o i) -> p g o i", g=G, o=C),
                            rows[:, b.slot, :, :].rearrange("p g (a i) -> p g a i", a=1).broadcast_to([P, G, C, C]),
                            ALU.mult).then_inc(s_pr, 1)
                        dve.wait_ge(s_do, b.n + 1)
                        dve.tensor_reduce(s_src[:, :], dots[:, :, :], AX.X, ALU.add).then_inc(s_sd, 1)
                        dve.wait_ge(s_pr, b.n + 1)
                        dve.tensor_reduce(msg[:, :, 1, :], prod[:, :, :, :], AX.X, ALU.add).then_inc(s_u, 1)

                    def messages(b):
                        dve.wait_ge(s_sd, b.n + 1)
                        dve.tensor_tensor(coef[:, :], s_src[:, :], sc[:, b.slot, RE:RE + G], ALU.add).then_inc(s_co, 1)
                        dve.wait_ge(s_u, b.n + 1)
                        dve.wait_ge(s_co, b.n + 1)
                        dve.tensor_tensor(msg[:, :, 0, :], msg[:, :, 1, :], spread(coef[:, :], P, G, C), ALU.mult
                                          ).then_inc(s_ue, 1)
                        if b.from_(2):
                            dve.wait_ge(s_mm, b.n - 1)
                        dve.wait_ge(s_ue, b.n + 1)
                        dve.tensor_tensor(
                            msgx[:, b.par, :, :, :],
                            msg[:, :, :, :].rearrange("p g (a k) f -> p g a (k f)", a=1).broadcast_to([P, G, COLS, 2 * C]),
                            sc[:, b.slot, RC:RC + G * COLS].rearrange("p (g c a) -> p g c a", g=G, a=1)
                            .broadcast_to([P, G, COLS, 2 * C]), ALU.mult).then_inc(s_m, 1)

                    def add_sums(b):
                        x3 = X[:, bass.ds(b.n * BC, BC)].rearrange("p (c f) -> p c f", f=C)
                        a4 = acc[0:BP, b.par, 0:2 * BC].rearrange("p (c k f) -> p c k f", c=COLS, k=2)
                        dve.wait_ge(s_mm, b.n + 1)
                        dve.tensor_tensor(d_u[:, b.par, :, :], a4[:, :, 1, :], spread(drow3[:, bass.ds(b.n, 1), :].rearrange("p b c -> p (b c)"), BP, COLS, C),
                                          ALU.mult)
                        dve.tensor_tensor(x3, x3, a4[:, :, 0, :], ALU.add).then_inc(s_f, 1)

                    def finish(b):
                        x3 = X[:, bass.ds(b.n * BC, BC)].rearrange("p (c f) -> p c f", f=C)
                        dve.wait_ge(s_f, b.n + 1)
                        dve.tensor_tensor(x3, x3, d_u[:, b.par, :, :], ALU.add)

                    run_steps(dve, step, drain=3)

                @block.tensor
                def _(pe):
                    def step(t):
                        b = t.back(3)
                        if b.has():
                            hold(pe, s_m, b.n + 1)
                            if b.from_(2):
                                hold(pe, s_f, b.n - 1)
                            for g in range(G):
                                mm = pe.matmul(acc[0:BP, b.par, 0:2 * BC], oh[:, b.slot, g, :],
                                               msgx[:, b.par, g, :, :].rearrange("p c f -> p (c f)"),
                                               start=g == 0, stop=g == G - 1)
                            mm.then_inc(s_mm, 1)
                        if t.has():
                            hold(pe, s_ty, t.n + 1)
                            if t.from_(2):
                                hold(pe, s_tc, t.n - 1)
                            for g in range(G):
                                mm = pe.transpose(p_t[0:R, t.par, g * P:(g + 1) * P], typ[:, t.par, g, :], ident[:, :])
                            mm.then_inc(s_tt, 1)
                        b = t.back(1)
                        if b.has():
                            hold(pe, s_tc, b.n + 1)
                            if b.from_(2):
                                hold(pe, s_pr, b.n - 1)
                            for g in range(G):
                                mm = pe.matmul(p_w[:, b.par, g * C * C:(g + 1) * C * C],
                                               typT[:, b.par, g * P:(g + 1) * P], Wr[:, :], start=True, stop=True)
                            mm.then_inc(s_w, 1)
                    run_steps(pe, step, drain=3)

        s_out = sem("out_stored")
        with nc.Block() as block:
            @block.sync
            def _(sp):
                sp.dma_start(blocks(out), Xb).then_inc(s_out, 16)
                sp.wait_ge(s_out, 16)


_INS = ["x", "src", "dst", "edge_attr_16", "edge_type_90", "edge_weight", "L0_gnn_w0", "L0_gnn_b0", "L0_gnn_w1",
        "L0_gnn_b1", "L0_gnn_w2", "L0_gnn_b2", "L0_gnn_w3", "L0_gnn_b3", "L1_gnn_Ws", "L1_gnn_Wa", "L1_gnn_weight",
        "L1_gnn_w_comp"]


def kernel(**inputs):
    import concourse.bacc as bacc
    from concourse.bass_utils import run_bass_kernel_spmd as run

    nc = bacc.Bacc("TRN2", target_bir_lowering=False, num_devices=1)
    arrays, args = {}, []
    for name in _INS:
        a = np.ascontiguousarray(inputs[name])
        arrays["in_" + name] = a
        args.append(nc.dram_tensor("in_" + name, a.shape, mybir.dt.from_np(a.dtype), kind="ExternalInput").ap())
    o = nc.dram_tensor("out_0", (N, C), F32, kind="ExternalOutput").ap()
    build(nc, *args, o)
    return run(nc, [arrays], core_ids=[0]).results[0]["out_0"]
```

```python
from contextlib import ExitStack

import numpy as np
import concourse.bass as bass
from concourse import mybir

F32 = mybir.dt.float32
I32 = mybir.dt.int32
BF16 = mybir.dt.bfloat16
ALU = mybir.AluOpType
ACT = mybir.ActivationFunctionType
AX = mybir.AxisListType

P = 128
N = 100000
E = 50000
C = 16
H = 128
R = 90
B = 30
COLS = 5
BP = 125
BN = BP * COLS
NB = N // BN
G = 3
BC = COLS * C
NT = N + P
TAIL = P * G
NQ = -(-NB // P)
EP = 125
ET = E // EP
SKIP = 1 << 21
UNROLL = 4
HEAD = 2 * UNROLL
SPAN = ((0, 360), (150, BN), (365, BN))
HALF = 310

D0, W0_, DI, DQ = 0, G, 2 * G, 2 * G + COLS
DP, WC, KS = DQ + COLS, DQ + COLS + G, DQ + COLS + G + G * COLS
RP, RC, RT, RE, RD, KR = 0, G, G + G * COLS, 2 * G + G * COLS, 3 * G + G * COLS, 3 * G + G * COLS + COLS


class Step:

    def __init__(self, i, c=0):
        self.static = isinstance(i, int)
        self.i, self.c = divmod(UNROLL * i + c, UNROLL) if self.static else (i, c)

    @property
    def n(self):
        return self.i * UNROLL + self.c

    @property
    def par(self):
        return self.c % 2

    @property
    def slot(self):
        return self.c % UNROLL

    @property
    def round(self):
        return self.i + self.c // UNROLL

    @property
    def round2(self):
        return self.i * 2 + self.c // 2

    def back(self, k):
        return Step(self.i, self.c - k)

    def has(self):
        return not self.static or 0 <= self.n < NB

    def from_(self, k):
        return not self.static or self.n >= k


def run_steps(eng, step, ahead=0, drain=0, head=HEAD):
    for t in range(head):
        step(Step(0, t))
    with eng.Fori(head // UNROLL, NB // UNROLL - (1 if ahead else 0)) as i:
        for c in range(UNROLL):
            step(Step(i, c))
    for t in range(NB - (UNROLL if ahead else 0), NB + drain):
        step(Step(0, t))


def hold(eng, sem, value):
    eng.wait_ge(sem, value)
    eng.nop(nofuse=True)


class Chain:

    def __init__(self, eng, sem, n=0):
        self.eng, self.sem, self.n = eng, sem, n

    def __call__(self, ins):
        self.n += 1
        ins.then_inc(self.sem, 1)
        self.eng.wait_ge(self.sem, self.n)


def spread(ap, parts, n, m):
    return ap.rearrange("p (n a) -> p n a", a=1).broadcast_to([parts, n, m])


def build(nc, x, src, dst, edge_attr, edge_type, edge_weight, w0, b0, w1, b1, w2, b2, w3, b3,
          Ws, Wa, weight, w_comp, out):
    top = ExitStack()
    with top:
        def sb(name, shape, dt=F32, ctx=top):
            return ctx.enter_context(nc.sbuf_tensor(name, shape, dt))

        def ps(name, shape, ctx):
            return ctx.enter_context(nc.psum_tensor(name, shape, F32))

        def sem(name):
            return top.enter_context(nc.semaphore(name))

        yn_tab = nc.dram_tensor("y_narrow", (N, C), F32).ap()
        h_tab = nc.dram_tensor("h_and_dot", (N, C + 1), F32).ap()
        y1_tab = nc.dram_tensor("y1", (N, H), F32).ap()
        y2_tab = nc.dram_tensor("y2", (N, H), F32).ap()
        te_tab = nc.dram_tensor("edge_dot", (E + TAIL,), F32).ap()
        dst_tab = nc.dram_tensor("dst_tailed", (E + TAIL,), I32).ap()
        src_tab = nc.dram_tensor("src_tailed", (E + TAIL,), I32).ap()
        type_tab = nc.dram_tensor("type_tailed", (E + TAIL,), I32).ap()
        w_tab = nc.dram_tensor("weight_tailed", (E + TAIL,), F32).ap()
        rel_tab = nc.dram_tensor("rel_w", (C * R, C), F32).ap()
        deg_tab = nc.dram_tensor("deg", (NT, 1), F32).ap()
        dot_tab = nc.dram_tensor("dst_dot", (N, 1), F32).ap()
        sum_tab = nc.dram_tensor("sum_narrow", (NT, C), F32).ap()
        u_tab = nc.dram_tensor("own_wide", (NT, H), F32).ap()

        X = sb("X", [BP, NB * BC])
        Y = sb("Y", [BP, NB * BC])
        ident = sb("ident", [P, P])
        nodes = sb("nodes", [P, BN])
        ones = sb("ones", [P, P])
        part = sb("part", [P, 1])
        src_slot = sb("src_slot", [P, NB, G], I32)
        scal = sb("scal", [P, NB, KS])
        scal_rel = sb("scal_rel", [P, NB, KR])
        covered = sb("covered", [P, 1])
        covered_i = sb("covered_i", [P, 1], I32)
        W1 = sb("W1", [H, H])
        W2 = sb("W2", [H, H])
        W3 = sb("W3", [H, C])
        bias1 = sb("bias1", [P, H])
        bias2 = sb("bias2", [H, 1])
        bias3 = sb("bias3", [P, C])
        W0x = sb("W0x", [BC + COLS, COLS * H])
        v_rel = sb("v_rel", [P, 3 * C])
        Wr = sb("Wr", [R, C * C])

        def blocks(tab):
            return tab.rearrange("(b p c) f -> p b (c f)", p=BP, c=COLS)

        def rows_of(tab, b):
            return tab[bass.ds(b.n * BN, BN), :].rearrange("(p c) f -> p (c f)", c=COLS)

        Xb = X[:, :].rearrange("p (b g) -> p b g", g=BC)
        Yb = Y[:, :].rearrange("p (b g) -> p b g", g=BC)
        dinv3 = scal[0:BP, :, DI:DI + COLS]
        dinv_sq = scal[0:BP, :, DQ:DQ + COLS]
        drow3 = scal_rel[0:BP, :, RD:RD + COLS]

        with ExitStack() as ph:
            def t(name, shape, dt=F32):
                return sb("su_" + name, shape, dt, ph)
            nodes_i = t("nodes_i", [P, BN], I32)
            part_i = t("part_i", [P, 1], I32)
            first = t("first", [P, NQ])
            base_i = t("base_i", [P, NB], I32)
            head_i = t("head_i", [1, ET], I32)
            head = t("head", [1, ET])
            below = t("below", [P, ET])
            cnt = t("cnt", [P, NQ])
            row_i = t("row_i", [P, NQ], I32)
            row = t("row", [P, NQ])
            runs = t("runs", [P, NQ, EP], I32)
            runs_f = t("runs_f", [P, NQ, EP])
            begin = t("begin", [P, NQ])
            begin_i = t("begin_i", [P, NQ], I32)
            lanes = [t("lanes_" + k, [P, NQ, TAIL], dt) for k, dt in
                     (("dst", I32), ("src", I32), ("type", I32), ("w", F32), ("te", F32))]
            lanes_f = [t("lanes_f_" + k, [P, NQ, TAIL]) for k in ("dst", "src", "type")]
            slots = [t("slots_" + k, [P, G, NB]) for k in ("dst", "src", "type", "w", "te")]
            d, s, typ, w, te = slots
            valid = t("valid", [P, G, NB])
            tmp = t("tmp", [P, G, NB])
            dp = t("dp", [P, G, NB])
            dp_i = t("dp_i", [P, G, NB], I32)
            dc = t("dc", [P, G, NB])
            total = t("total", [P, 1])
            tail_i = t("tail_i", [3, P], I32)
            bases = t("bases", [B, C * C])
            comp = t("comp", [B, R])
            comp_r = t("comp_r", [R, B])
            wa = t("wa", [C, 3])
            wa_b = t("wa_b", [C, 3, P])
            ws = t("ws", [C, C])
            p_head = ps("p_head", [P, 512], ph)
            p_win = ps("p_win", [P, 5, 512], ph)
            p_misc = ps("p_misc", [P, 512], ph)
            attr = Y[:, 0:ET * C]
            rel_mix = Y[0:R, ET * C:ET * C + C * C]
            te_e = Y[:, ET * C + 2 * C * C:ET * C + 2 * C * C + ET]
            rel_in = Y[0:R, ET * C + C * C:ET * C + 2 * C * C]

            s_load = sem("su_loaded")
            s_heads = sem("su_heads_loaded")
            s_relw = sem("su_relation_inputs_loaded")
            s_attr = sem("su_attributes_loaded")
            s_tail = sem("su_lists_tailed")
            s_te = sem("su_edge_dots")
            s_tes = sem("su_edge_dots_stored")
            s_iota = sem("su_iota")
            s_d = sem("su_dve")
            s_id = sem("su_identity_ready")
            s_hf = sem("su_heads_float")
            s_hb = sem("su_heads_broadcast")
            s_row = sem("su_rows_ready")
            s_runs = sem("su_runs_gathered")
            s_beg = sem("su_begins_ready")
            s_lanes = sem("su_lanes_gathered")
            s_lf = sem("su_lanes_float")
            s_tr = sem("su_slots_turned")
            s_tc = sem("su_slots_copied")
            s_tot = sem("su_valid_counted")
            s_sum = sem("su_valid_summed")
            s_rm = sem("su_relation_matrix")
            s_rst = sem("su_relation_stored")
            s_rld = sem("su_relation_loaded")
            s_rc = sem("su_relation_copied")
            s_cT = sem("su_comp_turned")

            LOADS = 6 + 4 + 2 * COLS
            XB = NB // 4
            TAILS = 4 * 2 + 1
            dst_rows = dst.rearrange("(t p) -> t p", p=EP)
            with nc.Block() as block:
                @block.sync
                def _(sp):
                    sp.dma_start(head_i[:, :], dst.rearrange("(t p) -> p t", p=EP)[0:1, :],
                                 allow_slow_non_contiguous=True).then_inc(s_heads, 16)
                    sp.dma_start(bases[:, :].rearrange("b (i o) -> b i o", i=C),
                                 weight.rearrange("b i o -> (b i o)").rearrange("(i b o) -> b i o", i=C, b=B)
                                 ).then_inc(s_relw, 16)
                    sp.dma_start(comp_r[:, :], w_comp).then_inc(s_relw, 16)
                    sp.dma_start(wa[:, :], Wa.rearrange("a (k o) -> o (a k)", k=3),
                                 allow_slow_non_contiguous=True).then_inc(s_relw, 16)
                    sp.dma_start(ws[:, :], Ws).then_inc(s_relw, 16)
                    sp.dma_start(attr, edge_attr.rearrange("(p t) f -> p (t f)", t=ET)).then_inc(s_attr, 16)
                    sp.dma_start(W1[:, :], w1).then_inc(s_load, 16)
                    sp.dma_start(W2[:, :], w2).then_inc(s_load, 16)
                    sp.dma_start(W3[:, :], w3).then_inc(s_load, 16)
                    for tile, vec in ((bias1, b1), (bias3, b3)):
                        sp.dma_start(tile[:, :], vec.rearrange("(a f) -> a f", a=1).broadcast_to([P, vec.shape[0]])
                                     ).then_inc(s_load, 16)
                    sp.dma_start(bias2[:, :], b2.rearrange("(f a) -> f a", a=1)).then_inc(s_load, 16)
                    sp.wait_ge(s_iota, 4)
                    for c in range(COLS):
                        sp.dma_start(W0x[c * C:(c + 1) * C, c * H:(c + 1) * H], w0).then_inc(s_load, 16)
                        sp.dma_start(W0x[BC + c:BC + c + 1, c * H:(c + 1) * H],
                                     b0.rearrange("(a f) -> a f", a=1)).then_inc(s_load, 16)
                    sp.wait_ge(s_rm, 1)
                    sp.dma_start(rel_tab.rearrange("(i r) o -> r i o", r=R),
                                 rel_mix[:, :].rearrange("r (i o) -> r i o", i=C)).then_inc(s_rst, 16)
                    sp.wait_ge(s_rst, 16)
                    sp.dma_start(rel_in[:, :], rel_tab.rearrange("(r i) o -> r (i o)", i=C)).then_inc(s_rld, 16)
                    sp.wait_ge(s_load, 16 * LOADS)
                    sp.wait_ge(s_rld, 16)

                @block.scalar
                def _(act):
                    act.wait_ge(s_iota, 3)
                    for tab, vec in ((dst_tab, dst), (src_tab, src), (type_tab, edge_type), (w_tab, edge_weight)):
                        act.dma_start(tab[0:E].rearrange("(a e) -> a e", a=16),
                                      vec.rearrange("(a e) -> a e", a=16)).then_inc(s_tail, 16)
                    for tab in (dst_tab, src_tab, type_tab):
                        act.dma_start(tab[E:E + TAIL].rearrange("(a e) -> a e", a=G), tail_i[:, :]).then_inc(s_tail, 16)
                    act.wait_ge(s_iota, 8)
                    act.dma_start(w_tab[E:E + TAIL].rearrange("(a e) -> a e", a=G), ones[0:G, :]).then_inc(s_tail, 16)
                    act.dma_start(te_tab[E:E + TAIL].rearrange("(a e) -> a e", a=G), ones[0:G, :]).then_inc(s_tail, 16)
                    act.wait_ge(s_beg, 1)
                    for k in range(2):
                        act.dma_start(Xb[:, k * XB:(k + 1) * XB, :], blocks(x[k * XB * BN:(k + 1) * XB * BN, :])
                                      ).then_inc(s_load, 16)
                    act.wait_ge(s_te, 1)
                    act.dma_start(te_tab[0:E].rearrange("(p t) -> p t", t=ET), te_e).then_inc(s_tes, 16)
                    act.wait_ge(s_lanes, 16 * 5 * NQ)
                    for k in range(2, 4):
                        act.dma_start(Xb[:, k * XB:(k + 1) * XB, :], blocks(x[k * XB * BN:(k + 1) * XB * BN, :])
                                      ).then_inc(s_load, 16)
                    for k in range(5):
                        act.wait_ge(s_tr, k + 1)
                        act.copy(slots[k][:, :, :].rearrange("p g b -> p (g b)"), p_win[:, k, 0:G * NB]).then_inc(s_tc, 1)
                    act.wait_ge(s_load, 16 * LOADS)
                    act.wait_ge(s_tes, 16)
                    act.wait_ge(s_tail, 16 * TAILS)

                @block.gpsimd
                def _(pool):
                    pool.iota(nodes_i[:, :], pattern=[[1, BN]], base=0, channel_multiplier=0).then_inc(s_iota, 1)
                    pool.iota(part_i[:, :], pattern=[[0, 1]], base=0, channel_multiplier=1).then_inc(s_iota, 1)
                    pool.iota(tail_i[:, :], pattern=[[0, P]], base=1 << 20, channel_multiplier=0).then_inc(s_iota, 1)
                    pool.memset(W0x[:, :], 0.0).then_inc(s_iota, 1)
                    pool.iota(base_i[:, :], pattern=[[BN, NB]], base=0, channel_multiplier=0).then_inc(s_iota, 1)
                    pool.memset(scal[:, :, DI:DI + 2 * COLS], 0.0).then_inc(s_iota, 1)
                    pool.memset(scal_rel[:, :, RD:RD + COLS], 0.0).then_inc(s_iota, 1)
                    pool.memset(ones[:, :], 1.0).then_inc(s_iota, 1)
                    pool.wait_ge(s_row, 1)
                    for q in range(NQ):
                        pool.indirect_dma_start(
                            out=runs[:, q, :], out_offset=None, in_=dst_rows,
                            in_offset=bass.IndirectOffsetOnAxis(ap=row_i[:, q:q + 1], axis=0)).then_inc(s_runs, 16)
                    hold(pool, s_tail, 16 * TAILS)
                    pool.wait_ge(s_beg, 1)
                    for tile, tab in zip(lanes, (dst_tab, src_tab, type_tab, w_tab, te_tab)):
                        if tab is te_tab:
                            hold(pool, s_tes, 16)
                        for q in range(NQ):
                            pool.indirect_dma_start(
                                out=tile[:, q, :], out_offset=None, in_=tab.rearrange("(a e) -> a e", a=1),
                                in_offset=bass.IndirectOffsetOnAxis(ap=begin_i[:, q:q + 1], axis=1)
                                ).then_inc(s_lanes, 16)
                    pool.wait_ge(s_lanes, 16 * 5 * NQ)

                @block.vector
                def _(dve):
                    c = Chain(dve, s_d)
                    dve.wait_ge(s_iota, 8)
                    c(dve.tensor_copy(nodes[:, :], nodes_i[:, :]))
                    c(dve.tensor_copy(part[:, :], part_i[:, :]))
                    dve.tensor_scalar(ident[:, :], nodes[:, 0:P], part[:, 0:1], None, ALU.is_equal).then_inc(s_id, 1)
                    dve.wait_ge(s_heads, 16)
                    dve.tensor_copy(head[:, :], head_i[:, :]).then_inc(s_hf, 1)
                    for q in range(NQ):
                        c(dve.tensor_scalar(first[:, q:q + 1], part[:, :], float(BN), float(BN * P * q), ALU.mult, ALU.add))
                    dve.wait_ge(s_hb, 1)
                    for q in range(NQ):
                        c(dve.tensor_scalar(below[:, :], p_head[:, 0:ET], first[:, q:q + 1], None, ALU.is_lt))
                        c(dve.tensor_reduce(cnt[:, q:q + 1], below[:, :], AX.X, ALU.add))
                    c(dve.tensor_scalar(row[:, :], cnt[:, :], -1.0, 0.0, ALU.add, ALU.max))
                    dve.tensor_copy(row_i[:, :], row[:, :]).then_inc(s_row, 1)
                    dve.wait_ge(s_cT, 1)
                    dve.tensor_copy(comp[:, :], p_misc[0:B, 0:R]).then_inc(s_rc, 1)
                    dve.tensor_copy(wa_b[:, :, :], spread(wa[:, :], C, 3, P)).then_inc(s_rc, 1)
                    dve.wait_ge(s_runs, 16 * NQ)
                    c(dve.tensor_copy(runs_f[:, :, :], runs[:, :, :]))
                    for q in range(NQ):
                        c(dve.tensor_scalar(below[:, 0:EP], runs_f[:, q, :], first[:, q:q + 1], None, ALU.is_lt))
                        c(dve.tensor_reduce(cnt[:, q:q + 1], below[:, 0:EP], AX.X, ALU.add))
                    c(dve.scalar_tensor_tensor(out=begin[:, :], in0=row[:, :], scalar=float(EP), in1=cnt[:, :],
                                               op0=ALU.mult, op1=ALU.add))
                    dve.tensor_copy(begin_i[:, :], begin[:, :]).then_inc(s_beg, 1)
                    dve.wait_ge(s_cT, 2)
                    dve.tensor_copy(rel_mix[:, :], p_misc[0:R, 0:C * C]).then_inc(s_rm, 1)
                    c(dve.tensor_copy(v_rel[:, :], p_misc[:, C * C:C * C + 3 * C]))
                    dve.wait_ge(s_attr, 16)
                    a3 = attr.rearrange("p (t f) -> p t f", f=C)
                    c(dve.tensor_tensor(a3, a3, v_rel[0:EP, C:2 * C].rearrange("p (a f) -> p a f", a=1)
                                        .broadcast_to([EP, ET, C]), ALU.mult))
                    dve.tensor_reduce(te_e, a3, AX.X, ALU.add).then_inc(s_te, 1)
                    dve.wait_ge(s_lanes, 16 * 5 * NQ)
                    for k in range(3):
                        dve.tensor_copy(lanes_f[k][:, :, :], lanes[k][:, :, :]).then_inc(s_lf, 1)
                    dve.wait_ge(s_tc, 5)
                    c(dve.tensor_copy(tmp[:, 0, :], base_i[:, :]))
                    c(dve.tensor_tensor(d[:, :, :], d[:, :, :], tmp[:, 0, :].rearrange("p (a b) -> p a b", a=1)
                                        .broadcast_to([P, G, NB]), ALU.subtract))
                    for g, (lo, hi) in enumerate(SPAN):
                        c(dve.tensor_scalar(valid[:, g, :], d[:, g, :], float(lo), None, ALU.is_ge))
                        c(dve.scalar_tensor_tensor(out=valid[:, g, :], in0=d[:, g, :], scalar=float(hi),
                                                   in1=valid[:, g, :], op0=ALU.is_lt, op1=ALU.mult))
                    dve.tensor_reduce(total[:, :], valid[:, :, :].rearrange("p g b -> p (g b)"), AX.X, ALU.add
                                      ).then_inc(s_tot, 1)
                    c(dve.scalar_tensor_tensor(out=d[:, :, :], in0=d[:, :, :], scalar=10000.0, in1=valid[:, :, :],
                                               op0=ALU.add, op1=ALU.mult))
                    c(dve.tensor_scalar(d[:, :, :], d[:, :, :], -10000.0, None, ALU.add))
                    c(dve.tensor_scalar(valid[:, :, :], valid[:, :, :], -float(SKIP), float(SKIP), ALU.mult, ALU.add))
                    c(dve.tensor_tensor(s[:, :, :], s[:, :, :], valid[:, :, :], ALU.add))
                    c(dve.tensor_copy(src_slot[:, :, :].rearrange("p b g -> p g b"), s[:, :, :]))
                    c(dve.tensor_scalar(dp[:, :, :], d[:, :, :], 0.2, None, ALU.mult))
                    c(dve.tensor_copy(dp_i[:, :, :], dp[:, :, :]))
                    c(dve.tensor_copy(dp[:, :, :], dp_i[:, :, :]))
                    c(dve.scalar_tensor_tensor(out=dc[:, :, :], in0=dp[:, :, :], scalar=-float(COLS), in1=d[:, :, :],
                                               op0=ALU.mult, op1=ALU.add))
                    c(dve.tensor_scalar(tmp[:, :, :], dc[:, :, :], 0.0, None, ALU.is_lt))
                    c(dve.tensor_tensor(dp[:, :, :], dp[:, :, :], tmp[:, :, :], ALU.subtract))
                    c(dve.tensor_scalar(tmp[:, :, :], dc[:, :, :], float(COLS), None, ALU.is_ge))
                    c(dve.tensor_tensor(dp[:, :, :], dp[:, :, :], tmp[:, :, :], ALU.add))
                    c(dve.scalar_tensor_tensor(out=dc[:, :, :], in0=dp[:, :, :], scalar=-float(COLS), in1=d[:, :, :],
                                               op0=ALU.mult, op1=ALU.add))
                    dve.wait_ge(s_sum, 1)
                    c(dve.tensor_scalar(covered[:, :], p_head[:, 0:1], float(E), None, ALU.is_equal))
                    c(dve.tensor_copy(covered_i[:, :], covered[:, :]))
                    c(dve.tensor_scalar(w[:, :, :], w[:, :, :], covered[:, 0:1], None, ALU.mult))
                    c(dve.tensor_scalar(scal_rel[:, :, RP:RP + G].rearrange("p b g -> p g b"), dp[:, :, :], -1.0, None,
                                        ALU.mult))
                    for dest, k, source in ((scal, D0, d), (scal, W0_, w), (scal, DP, dp),
                                            (scal_rel, RT, typ), (scal_rel, RE, te)):
                        dve.tensor_copy(dest[:, :, k:k + G].rearrange("p b g -> p g b"), source[:, :, :]).then_inc(s_rc, 1)
                    for j in range(COLS):
                        c(dve.tensor_scalar(tmp[:, :, :], dc[:, :, :], float(j), None, ALU.is_equal))
                        c(dve.tensor_tensor(scal[:, :, WC + j:WC + G * COLS:COLS].rearrange("p b g -> p g b"),
                                            tmp[:, :, :], w[:, :, :], ALU.mult))
                        c(dve.tensor_scalar(scal_rel[:, :, RC + j:RC + G * COLS:COLS].rearrange("p b g -> p g b"),
                                            tmp[:, :, :], covered[:, 0:1], None, ALU.mult))
                    dve.wait_ge(s_rld, 16)
                    c(dve.tensor_copy(Wr[:, :].rearrange("r (o i) -> r o i", o=C),
                                      rel_in[:, :].rearrange("r (i o) -> r o i", i=C)))

                @block.tensor
                def _(pe):
                    pe.wait_ge(s_id, 1)
                    pe.wait_ge(s_hf, 1)
                    pe.matmul(p_head[:, 0:ET], ones[0:1, :], head[:, :], start=True, stop=True).then_inc(s_hb, 1)
                    pe.wait_ge(s_relw, 64)
                    pe.transpose(p_misc[0:B, 0:R], comp_r[:, :], ident[0:R, 0:R]).then_inc(s_cT, 1)
                    pe.wait_ge(s_rc, 2)
                    pe.matmul(p_misc[0:R, 0:C * C], comp[:, :], bases[:, :], start=True, stop=True)
                    for k in range(3):
                        mm = pe.matmul(p_misc[:, C * C + k * C:C * C + (k + 1) * C], wa_b[:, k, :], ws[:, :],
                                       start=True, stop=True)
                    mm.then_inc(s_cT, 1)
                    for k, tile in enumerate(lanes_f + lanes[3:]):
                        pe.wait_ge(s_lf, min(k + 1, 3))
                        for g in range(G):
                            for q in range(NQ):
                                n = min(P, NB - q * P)
                                mm = pe.transpose(p_win[:, k, g * NB + q * P:g * NB + q * P + n],
                                                  tile[0:n, q, g * P:(g + 1) * P], ident[0:n, 0:n])
                        mm.then_inc(s_tr, 1)
                    pe.wait_ge(s_tot, 1)
                    pe.matmul(p_head[:, 0:1], ones[:, :], total[:, :], start=True, stop=True).then_inc(s_sum, 1)

        TN = UNROLL * COLS

        def norm_tiles(name, ph):
            return [sb(f"{name}_{k}", [BP, TN], F32, ph) for k in ("mean", "var", "inv")] + [
                sb(f"{name}_{k}", [BP, TN, C], F32, ph) for k in ("centred", "sq")]

        def four_blocks(tile, j):
            return tile[:, bass.ds(j * UNROLL * BC, UNROLL * BC)].rearrange("p (n f) -> p n f", f=C)

        def centre(dve, link, j, tiles):
            mean, var, inv, cen, sq = tiles
            link(dve.tensor_reduce(mean[:, :], four_blocks(X, j), AX.X, ALU.add), j, 1)
            link(dve.tensor_scalar(mean[:, :], mean[:, :], 1.0 / C, None, ALU.mult), j, 2)
            link(dve.tensor_tensor(cen[:, :, :], four_blocks(X, j), spread(mean[:, :], BP, TN, C), ALU.subtract), j, 3)

        def variance(dve, link, j, tiles):
            mean, var, inv, cen, sq = tiles
            link(dve.tensor_tensor(sq[:, :, :], cen[:, :, :], cen[:, :, :], ALU.mult), j, 4)
            link(dve.tensor_reduce(var[:, :], sq[:, :, :], AX.X, ALU.add), j, 5)
            link(dve.tensor_scalar(var[:, :], var[:, :], 1.0 / C, 1e-5, ALU.mult, ALU.add), j, 6)

        def uncovered(eng):
            return eng.value_load(covered_i[0:1, 0:1], min_val=0, max_val=1) < 1

        s_in = sem("gp_inputs_loaded")
        s_before = sem("gp_target_prepared")
        s_link = sem("gp_chain")
        s_dg = sem("gp_diagonal_ready")
        s_row = sem("gp_targets_spread")
        s_same = sem("gp_index_ready")
        s_from = sem("gp_source_ready")
        s_rows = sem("gp_rows_gathered")
        s_rowmsg = sem("gp_messages_ready")
        s_comb = sem("gp_sums_ready")
        s_sum_out = sem("gp_sums_copied")
        s_add = sem("gp_sums_added")
        s_after = sem("gp_result_loaded")
        s_is_type = sem("gp_types_compared")
        s_type_turned = sem("gp_types_turned")
        s_type_copied = sem("gp_types_copied")
        s_mat = sem("gp_matrices_selected")
        general_count = {"visits": 0, "in": 0, "before": 0, "after": 0, "from": 0, "rows": 0, "chain": 0}

        def general_path(name, width, target, before, after, tab=None, dots=False):
            before = before + [(target[N:N + EP, :], X[:, 0:width])]
            with ExitStack() as ph:
                dst_i = sb(name + "_dst_i", [EP, ET], I32, ph)
                dst_e = sb(name + "_dst", [EP, ET], F32, ph)
                w_e = sb(name + "_w", [EP, ET], F32, ph)
                src_e = sb(name + "_src", [EP, ET], I32, ph)
                tri = sb(name + "_tri", [EP, EP], F32, ph)
                spare = sb(name + "_spare", [EP, 1], F32, ph)
                diag = sb(name + "_diag", [EP, EP], F32, ph)
                same = sb(name + "_same", [EP, EP], F32, ph)
                low = sb(name + "_low", [EP, EP], F32, ph)
                earlier = sb(name + "_earlier", [EP, 1], F32, ph)
                firsts = sb(name + "_firsts", [EP, 1], F32, ph)
                off = sb(name + "_off", [EP, 1], F32, ph)
                at_f = sb(name + "_at_f", [EP, 1], F32, ph)
                at = sb(name + "_at", [EP, 1], I32, ph)
                from_ = sb(name + "_from", [EP, 1], I32, ph)
                rows = sb(name + "_rows", [EP, tab.shape[1] if tab is not None else 1], F32, ph)
                scaled = sb(name + "_scaled", [EP, width], F32, ph)
                dot = sb(name + "_dot", [EP, 1], F32, ph)
                msg = sb(name + "_msg", [EP, width], F32, ph)
                comb = sb(name + "_comb", [EP, width], F32, ph)
                if dots:
                    type_i = sb(name + "_type_i", [EP, ET], I32, ph)
                    type_e = sb(name + "_type", [EP, ET], F32, ph)
                    te_e = sb(name + "_edge_dot", [EP, ET], F32, ph)
                    is_type = sb(name + "_is_type", [EP, R], F32, ph)
                    is_typeT = sb(name + "_is_typeT", [R, EP], F32, ph)
                    prod = sb(name + "_prod", [EP, C, C], F32, ph)
                    u = sb(name + "_u", [EP, C], F32, ph)
                    coef = sb(name + "_coef", [EP, 2], F32, ph)
                    p_type = ps(name + "_p_type", [P, 512], ph)
                    p_mat = ps(name + "_p_mat", [P, 512], ph)
                p_row = ps(name + "_p_row", [EP, 512], ph)
                p_comb = ps(name + "_p_comb", [EP, 512], ph)
                was = dict(general_count)
                visit = was["visits"]
                tiles = visit * ET
                per = 2 if dots else 1
                K = 11 if dots else 7
                loads = 5 if dots else 3
                with nc.Block() as block:
                    @block.sync
                    def _(sp):
                        with sp.If(uncovered(sp)):
                            sp.dma_start(dst_i[:, :], dst.rearrange("(p t) -> p t", t=ET)).then_inc(s_in, 16)
                            sp.dma_start(w_e[:, :], edge_weight.rearrange("(p t) -> p t", t=ET)).then_inc(s_in, 16)
                            sp.dma_start(src_e[:, :], src.rearrange("(p t) -> p t", t=ET)).then_inc(s_in, 16)
                            if dots:
                                sp.dma_start(type_i[:, :], edge_type.rearrange("(p t) -> p t", t=ET)).then_inc(s_in, 16)
                                sp.dma_start(te_e[:, :], te_tab[0:E].rearrange("(p t) -> p t", t=ET)).then_inc(s_in, 16)
                            for o, i in before:
                                sp.dma_start(o, i).then_inc(s_before, 16)
                            sp.wait_ge(s_add, 16 * (tiles + ET))
                            for o, i in after:
                                sp.dma_start(o, i).then_inc(s_after, 16)
                            if after:
                                sp.wait_ge(s_after, 16 * (was["after"] + len(after)))
                            sp.nop()

                    @block.gpsimd
                    def _(pool):
                        with pool.If(uncovered(pool)):
                            hold(pool, s_before, 16 * (was["before"] + len(before)))
                            hold(pool, s_in, 16 * (was["in"] + loads))
                            with pool.Fori(0, ET) as t:
                                if tab is not None:
                                    pool.tensor_copy(from_[:, :], src_e[:, bass.ds(t, 1)]).then_inc(s_from, 1)
                                    hold(pool, s_from, t * per + (was["from"] + 1))
                                    pool.indirect_dma_start(
                                        out=rows[:, :], out_offset=None, in_=tab,
                                        in_offset=bass.IndirectOffsetOnAxis(ap=from_[:, 0:1], axis=0)
                                        ).then_inc(s_rows, 16)
                                if dots:
                                    hold(pool, s_rows, t * 32 + (was["rows"] + 16))
                                    pool.tensor_copy(from_[:, :], dst_i[:, bass.ds(t, 1)]).then_inc(s_from, 1)
                                    hold(pool, s_from, t * 2 + (was["from"] + 2))
                                    pool.indirect_dma_start(
                                        out=dot[:, :], out_offset=None, in_=dot_tab,
                                        in_offset=bass.IndirectOffsetOnAxis(ap=from_[:, 0:1], axis=0)
                                        ).then_inc(s_rows, 16)
                                hold(pool, s_same, t + (tiles + 1))
                                hold(pool, s_sum_out, t + (tiles + 1))
                                pool.indirect_dma_start(
                                    out=target, out_offset=bass.IndirectOffsetOnAxis(ap=at[:, 0:1], axis=0),
                                    in_=comb[:, :], in_offset=None, compute_op=ALU.add).then_inc(s_add, 16)
                                hold(pool, s_add, (t + (tiles + 1)) * 16)
                            pool.nop()

                    @block.tensor
                    def _(pe):
                        with pe.If(uncovered(pe)):
                            with pe.Fori(0, ET) as t:
                                hold(pe, s_dg, t + (tiles + 1))
                                pe.matmul(p_row[:, 0:EP], ones[0:EP, 0:EP], diag[:, :], start=True, stop=True
                                          ).then_inc(s_row, 1)
                                if dots:
                                    hold(pe, s_is_type, t + 1)
                                    pe.transpose(p_type[0:R, 0:EP], is_type[:, :], ident[0:EP, 0:EP]
                                                 ).then_inc(s_type_turned, 1)
                                    hold(pe, s_type_copied, t + 1)
                                    pe.matmul(p_mat[0:EP, 0:C * C], is_typeT[:, :], Wr[:, :], start=True, stop=True
                                              ).then_inc(s_mat, 1)
                                hold(pe, s_same, t + (tiles + 1))
                                hold(pe, s_rowmsg, t + (tiles + 1))
                                pe.matmul(p_comb[:, 0:width], same[:, :], msg[:, :], start=True, stop=True
                                          ).then_inc(s_comb, 1)
                            pe.nop()

                    @block.vector
                    def _(dve):
                        with dve.If(uncovered(dve)):
                            c = Chain(dve, s_link, was["chain"])
                            dve.wait_ge(s_in, 16 * (was["in"] + loads))
                            c(dve.tensor_copy(dst_e[:, :], dst_i[:, :]))
                            c(dve.tensor_scalar(tri[:, :], nodes[0:EP, 0:EP], part[0:EP, 0:1], None, ALU.is_lt))
                            c(dve.tensor_scalar(spare[:, :], part[0:EP, :], float(N), None, ALU.add))
                            if dots:
                                c(dve.tensor_copy(type_e[:, :], type_i[:, :]))
                            n0 = c.n
                            general_count["chain"] = n0 + ET * K
                            with dve.Fori(0, ET) as t:
                                def link(ins, k):
                                    ins.then_inc(s_link, 1)
                                    hold(dve, s_link, t * K + n0 + k)
                                col = dst_e[:, bass.ds(t, 1)]
                                dve.tensor_scalar(diag[:, :], ident[0:EP, 0:EP], col, None, ALU.mult).then_inc(s_dg, 1)
                                hold(dve, s_row, t + (tiles + 1))
                                link(dve.tensor_scalar(same[:, :], p_row[:, 0:EP], col, None, ALU.is_equal), 1)
                                link(dve.tensor_tensor(low[:, :], same[:, :], tri[:, :], ALU.mult), 2)
                                link(dve.tensor_reduce(earlier[:, :], low[:, :], AX.X, ALU.add), 3)
                                link(dve.tensor_scalar(firsts[:, :], earlier[:, :], 0.0, None, ALU.is_equal), 4)
                                link(dve.tensor_tensor(off[:, :], col, spare[:, :], ALU.subtract), 5)
                                link(dve.scalar_tensor_tensor(out=at_f[:, :], in0=off[:, :], scalar=firsts[:, 0:1],
                                                              in1=spare[:, :], op0=ALU.mult, op1=ALU.add), 6)
                                dve.tensor_copy(at[:, :], at_f[:, :]).then_inc(s_same, 1)
                                w_col = w_e[:, bass.ds(t, 1)]
                                if dots:
                                    dve.tensor_scalar(is_type[:, :], nodes[0:EP, 0:R], type_e[:, bass.ds(t, 1)], None,
                                                      ALU.is_equal).then_inc(s_is_type, 1)
                                    hold(dve, s_type_turned, t + 1)
                                    dve.tensor_copy(is_typeT[:, :], p_type[0:R, 0:EP]).then_inc(s_type_copied, 1)
                                    hold(dve, s_rows, t * 32 + (was["rows"] + 32))
                                    hold(dve, s_mat, t + 1)
                                    link(dve.tensor_tensor(
                                        prod[:, :, :], p_mat[0:EP, 0:C * C].rearrange("p (o i) -> p o i", i=C),
                                        rows[:, 0:C].rearrange("p (a i) -> p a i", a=1).broadcast_to([EP, C, C]),
                                        ALU.mult), 7)
                                    link(dve.tensor_reduce(u[:, :], prod[:, :, :], AX.X, ALU.add), 8)
                                    link(dve.tensor_tensor(coef[:, 1:2], rows[:, C:C + 1], te_e[:, bass.ds(t, 1)],
                                                           ALU.add), 9)
                                    link(dve.tensor_tensor(coef[:, 0:1], coef[:, 1:2], dot[:, :], ALU.add), 10)
                                    link(dve.tensor_scalar(scaled[:, :], u[:, :], coef[:, 0:1], None, ALU.mult), 11)
                                    dve.tensor_copy(msg[:, :], scaled[:, :]).then_inc(s_rowmsg, 1)
                                elif tab is not None:
                                    hold(dve, s_rows, t * 16 + (was["rows"] + 16))
                                    link(dve.tensor_scalar(scaled[:, :], rows[:, :], w_col, None, ALU.mult), 7)
                                    dve.tensor_scalar(msg[:, :], scaled[:, :], 0.5, None, ALU.mult).then_inc(s_rowmsg, 1)
                                else:
                                    link(dve.tensor_copy(low[:, 0:1], w_col), 7)
                                    dve.tensor_copy(msg[:, :], low[:, 0:1]).then_inc(s_rowmsg, 1)
                                hold(dve, s_comb, t + (tiles + 1))
                                dve.tensor_copy(comb[:, :], p_comb[:, 0:width]).then_inc(s_sum_out, 1)
                                hold(dve, s_add, (t + (tiles + 1)) * 16)
                            dve.nop()
            general_count["visits"] += 1
            general_count["before"] += len(before)
            general_count["after"] += len(after)
            general_count["in"] += loads
            general_count["from"] += per * ET if tab is not None else 0
            general_count["rows"] += 16 * per * ET if tab is not None else 0

        s_clr = sem("ring_cleared")
        cleared = {"times": 0}

        def gather_blocks(pool, tab, rows, idx, s_ix, s_g, s_used):
            cleared["times"] += 1
            pool.memset(rows[:, :, :, :], 0.0).then_inc(s_clr, 1)
            hold(pool, s_clr, cleared["times"])
            limit = pool.to_reg(N - 1)

            def step(b):
                hold(pool, s_ix, b.n + 1)
                if b.from_(UNROLL):
                    hold(pool, s_used, b.n - (UNROLL - 1))
                for g in range(G):
                    pool.indirect_dma_start(
                        out=rows[:, b.slot, g, :], out_offset=None, in_=tab,
                        in_offset=bass.IndirectOffsetOnAxis(ap=idx[:, b.slot, g:g + 1], axis=0),
                        bounds_check=limit, oob_is_err=False).then_inc(s_g[b.slot], 16)
            run_steps(pool, step)

        def place_indices(act, b, idx, s_ix, s_g):
            if not b.has():
                return
            if b.from_(UNROLL):
                hold(act, s_g[b.slot], b.round * 16 * G)
            act.copy(idx[:, b.slot, :], src_slot[:, bass.ds(b.n, 1), :].rearrange("p b g -> p (b g)")
                     ).then_inc(s_ix, 1)

        def scalars_of(b, lo, hi, tab=scal, parts=P):
            return tab[0:parts, bass.ds(b.n, 1), lo:hi].rearrange("p b k -> p (b k)")

        TINY = float(np.finfo(np.float32).tiny)
        with ExitStack() as ph:
            deg_parts = sb("dg_parts", [BP, NB, 3 * COLS], F32, ph)
            nodes_h = sb("dg_nodes", [P, BP], BF16, ph)
            cut = sb("dg_cut", [P, NB, G, 3, COLS], BF16, ph)
            left = sb("dg_left", [P, NB, G, COLS], F32, ph)
            sc = sb("dg_scalars", [P, 4, G], F32, ph)
            oh = sb("dg_oh", [P, 4, G, BP], BF16, ph)
            acc = ps("dg_acc", [P, 4, 512], ph)
            mean = sb("dg_mean", [BP, TN], F32, ph)
            cen = sb("dg_centred", [BP, TN, C], F32, ph)
            sq = sb("dg_sq", [BP, TN, C], F32, ph)
            deg = sb("dg_deg", [BP, TN], F32, ph)
            pos = sb("dg_pos", [BP, TN], F32, ph)
            both = sb("dg_both", [BP, 2, TN], F32, ph)
            inv = sb("dg_inv", [BP, 2, TN], F32, ph)
            dinv = sb("dg_dinv", [BP, TN], F32, ph)
            by = sb("dg_by", [BP, TN], F32, ph)
            s_cut = sem("dg_weights_cut")
            s_sc = sem("dg_scalars_staged")
            s_oh = sem("dg_onehot_ready")
            s_mm = sem("dg_block_summed")
            s_fin = sem("dg_block_finished")
            s_ln = sem("dg_norm_chain")
            s_sq = sem("dg_squared")
            s_root = sem("dg_root_ready")
            s_y0 = sem("dg_rows_stored")
            LINKS = 15
            with nc.Block() as block:
                @block.scalar
                def _(act):
                    def stage(b):
                        if b.from_(4):
                            hold(act, s_oh, b.n - 3)
                        act.copy(sc[:, b.slot, :], scalars_of(b, DP, WC)).then_inc(s_sc, 1)

                    def step(t):
                        if t.back(-3).has():
                            stage(t.back(-3))
                        b = t.back(2)
                        if b.has():
                            hold(act, s_mm, b.n + 1)
                            act.copy(deg_parts[:, bass.ds(b.n, 1), :].rearrange("p b k -> p (b k)"),
                                     acc[0:BP, b.slot, 0:3 * COLS]).then_inc(s_fin, 1)
                        if t.slot == 0 and t.back(8).has():
                            act.wait_ge(s_ln, t.back(8).round * LINKS + 3)
                            act.activation(sq[:, :, :], cen[:, :, :], ACT.Square).then_inc(s_sq, 1)
                        if t.slot == 2 and t.back(10).has():
                            act.wait_ge(s_ln, t.back(10).round * LINKS + 9)
                            act.activation(inv[:, :, :], both[:, :, :], ACT.Sqrt).then_inc(s_root, 1)
                    for b in range(3):
                        stage(Step(0, b))
                    run_steps(act, step, ahead=1, drain=8, head=HEAD + UNROLL)

                @block.vector
                def _(dve):
                    c = Chain(dve, s_cut)
                    wcol = scal[:, :, WC:KS].rearrange("p b (g c) -> p b g c", g=G)
                    c(dve.tensor_copy(nodes_h[:, :], nodes[:, 0:BP]))
                    c(dve.tensor_copy(cut[:, :, :, 0, :], wcol))
                    c(dve.tensor_tensor(left[:, :, :, :], wcol, cut[:, :, :, 0, :], ALU.subtract))
                    c(dve.tensor_copy(cut[:, :, :, 1, :], left[:, :, :, :]))
                    c(dve.tensor_tensor(left[:, :, :, :], left[:, :, :, :], cut[:, :, :, 1, :], ALU.subtract))
                    c(dve.tensor_copy(cut[:, :, :, 2, :], left[:, :, :, :]))

                    def after(j, k, by_register=False):
                        if by_register and (not isinstance(j, int) or j * LINKS + k > 0):
                            hold(dve, s_ln, j * LINKS + k)
                        elif not by_register:
                            dve.wait_ge(s_ln, j * LINKS + k)

                    def part_of(j, k):
                        return deg_parts[:, bass.ds(j * UNROLL, UNROLL), k * COLS:(k + 1) * COLS]

                    def per_block(tile):
                        return tile.rearrange("p (b c) -> p b c", c=COLS)

                    def norm(t, g):
                        if t.slot == 0 and t.back(8).has():
                            j = t.back(8).round
                            after(j, g, by_register=g != 1)
                            if g == 0:
                                ins = dve.tensor_reduce(mean[:, :], four_blocks(X, j), AX.X, ALU.add)
                            elif g == 1:
                                ins = dve.tensor_scalar(mean[:, :], mean[:, :], 1.0 / C, None, ALU.mult)
                            else:
                                ins = dve.tensor_tensor(cen[:, :, :], four_blocks(X, j), spread(mean[:, :], BP, TN, C),
                                                        ALU.subtract)
                            ins.then_inc(s_ln, 1)
                        if t.slot == 1 and t.back(9).has():
                            j = t.back(9).round
                            after(j, 3 + g, by_register=g != 2)
                            if g == 0:
                                hold(dve, s_fin, j * UNROLL + UNROLL)
                                ins = dve.tensor_tensor(per_block(deg[:, :]), part_of(j, 2), part_of(j, 1), ALU.add)
                            elif g == 1:
                                ins = dve.scalar_tensor_tensor(out=per_block(deg[:, :]), in0=per_block(deg[:, :]), scalar=2.0,
                                                               in1=part_of(j, 0), op0=ALU.add, op1=ALU.add)
                            else:
                                ins = dve.tensor_scalar(pos[:, :], deg[:, :], 0.0, None, ALU.is_gt)
                            ins.then_inc(s_ln, 1)
                        if t.slot == 2 and t.back(10).has():
                            j = t.back(10).round
                            after(j, 6 + g)
                            if g == 0:
                                ins = dve.tensor_scalar(both[:, 1, :], deg[:, :], TINY, None, ALU.max)
                            elif g == 1:
                                dve.wait_ge(s_sq, j + 1)
                                ins = dve.tensor_reduce(both[:, 0, :], sq[:, :, :], AX.X, ALU.add)
                            else:
                                ins = dve.tensor_scalar(both[:, 0, :], both[:, 0, :], 1.0 / C, 1e-5, ALU.mult, ALU.add)
                            ins.then_inc(s_ln, 1)
                        if t.slot == 3 and t.back(11).has():
                            j = t.back(11).round
                            after(j, 9 + g)
                            if g == 0:
                                dve.wait_ge(s_root, j + 1)
                                ins = dve.reciprocal(inv[:, :, :], inv[:, :, :])
                            elif g == 1:
                                ins = dve.tensor_tensor(dinv[:, :], inv[:, 1, :], pos[:, :], ALU.mult)
                            else:
                                ins = dve.tensor_tensor(by[:, :], inv[:, 0, :], dinv[:, :], ALU.mult)
                            ins.then_inc(s_ln, 1)
                            if g == 2:
                                place = scal[0:BP, bass.ds(j * UNROLL, UNROLL), DI:DI + COLS]
                                place_sq = scal[0:BP, bass.ds(j * UNROLL, UNROLL), DQ:DQ + COLS]
                                after(j, 12, by_register=True)
                                dve.scalar_tensor_tensor(out=four_blocks(Y, j), in0=cen[:, :, :], scalar=0.0,
                                                         in1=spread(by[:, :], BP, TN, C), op0=ALU.max, op1=ALU.mult
                                                         ).then_inc(s_ln, 1)
                                dve.tensor_copy(place, per_block(dinv[:, :])).then_inc(s_ln, 1)
                                dve.tensor_tensor(place_sq, per_block(dinv[:, :]), per_block(dinv[:, :]), ALU.mult
                                                  ).then_inc(s_ln, 1)

                    def step(b):
                        if b.has():
                            dve.wait_ge(s_sc, b.n + 1)
                            if b.from_(4):
                                dve.wait_ge(s_mm, b.n - 3)
                        for g in range(G):
                            if b.has():
                                ins = dve.tensor_scalar(oh[:, b.slot, g, :], nodes_h[:, :], sc[:, b.slot, g:g + 1], None,
                                                        ALU.is_equal)
                                if g == G - 1:
                                    ins.then_inc(s_oh, 1)
                            norm(b, g)
                    run_steps(dve, step, drain=8, head=HEAD + UNROLL)

                @block.tensor
                def _(pe):
                    def step(b):
                        hold(pe, s_oh, b.n + 1)
                        if b.from_(4):
                            hold(pe, s_fin, b.n - 3)
                        for g in range(G):
                            mm = pe.matmul(acc[0:BP, b.slot, 0:3 * COLS], oh[:, b.slot, g, :],
                                           cut[:, bass.ds(b.n, 1), g, :, :].rearrange("p b k c -> p (b k c)"),
                                           start=g == 0, stop=g == G - 1)
                        mm.then_inc(s_mm, 1)
                    run_steps(pe, step)

                @block.sync
                def _(sp):
                    with sp.Fori(0, NB // UNROLL) as j:
                        sp.wait_ge(s_ln, j * LINKS + 13)
                        sp.dma_start(blocks(yn_tab[bass.ds(j * UNROLL * BN, UNROLL * BN), :]),
                                     Y[:, bass.ds(j * UNROLL * BC, UNROLL * BC)].rearrange("p (b g) -> p b g", g=BC)
                                     ).then_inc(s_y0, 16)
                    sp.wait_ge(s_y0, 16 * (NB // UNROLL))

        with ExitStack() as ph:
            nodes_of = "(b p c) a -> p b (c a)"
            deg_rows = deg_tab[0:N, :].rearrange(nodes_of, p=BP, c=COLS)
            general_path("gd", 1, deg_tab, [(deg_rows, drow3)], [(dinv3, deg_rows)])
            pos = sb("di_pos", [BP, NB, COLS], F32, ph)
            dinv = sb("di_dinv", [BP, NB, COLS], F32, ph)
            s_d1 = sem("di_dve")
            s_guard = sem("di_guarded")
            s_sqrt = sem("di_root")
            s_y0 = sem("di_rows_scaled")
            s_y0st = sem("di_rows_stored")
            with nc.Block() as block:
                @block.vector
                def _(dve):
                    with dve.If(uncovered(dve)):
                        c = Chain(dve, s_d1)
                        c(dve.tensor_scalar(dinv[:, :, :], dinv3, 2.0, None, ALU.add))
                        c(dve.tensor_scalar(pos[:, :, :], dinv[:, :, :], 0.0, None, ALU.is_gt))
                        dve.tensor_scalar(dinv[:, :, :], dinv[:, :, :], TINY, None, ALU.max).then_inc(s_guard, 1)
                        dve.wait_ge(s_sqrt, 1)
                        c(dve.reciprocal(dinv[:, :, :], dinv[:, :, :]))
                        c(dve.tensor_tensor(dinv[:, :, :], dinv[:, :, :], pos[:, :, :], ALU.mult))
                        c(dve.tensor_copy(dinv3, dinv[:, :, :]))
                        c(dve.tensor_tensor(dinv_sq, dinv[:, :, :], dinv[:, :, :], ALU.mult))
                        y3 = Y[:, :].rearrange("p (n f) -> p n f", f=C)
                        dve.scalar_tensor_tensor(out=y3, in0=y3, scalar=float(np.sqrt(2.0)), op0=ALU.mult, op1=ALU.mult,
                                                 in1=spread(dinv[:, :, :].rearrange("p b c -> p (b c)"), BP, NB * COLS, C)
                                                 ).then_inc(s_y0, 1)
                        dve.nop()

                @block.scalar
                def _(act):
                    with act.If(uncovered(act)):
                        act.wait_ge(s_guard, 1)
                        act.activation(dinv[:, :, :], dinv[:, :, :], ACT.Sqrt).then_inc(s_sqrt, 1)
                        act.nop()

                @block.sync
                def _(sp):
                    with sp.If(uncovered(sp)):
                        sp.wait_ge(s_y0, 1)
                        sp.dma_start(blocks(yn_tab), Yb).then_inc(s_y0st, 16)
                        sp.wait_ge(s_y0st, 16)
                        sp.nop()

        sum_rows = blocks(sum_tab[0:N, :])
        general_path("g0g", C, sum_tab, [(sum_rows, Yb)], [(Yb, sum_rows)], tab=yn_tab)

        def narrow_layer(name, first):
            CUT = 3
            DN, QN, PN, WNC = 0, COLS, 2 * COLS, 2 * COLS + G
            with ExitStack() as ph:
                rows = sb(name + "_rows", [P, 4, G, C], F32, ph)
                idx = sb(name + "_idx", [P, 4, G], I32, ph)
                sc = sb(name + "_scalars", [P, 4, KS - DI], F32, ph)
                oh = sb(name + "_oh", [P, 4, G, BP], F32, ph)
                rowx = sb(name + "_rowx", [P, 2, G, BC], F32, ph)
                s1 = sb(name + "_s1", [BP, 2, BC], F32, ph)
                s2 = sb(name + "_s2", [BP, 4, BC + COLS], F32, ph)
                acc = ps(name + "_acc", [P, 2, 512], ph)
                s_ix = sem(name + "_index_ready")
                s_g = [sem(f"{name}_rows_gathered{u}") for u in range(4)]
                s_sc = sem(name + "_scalars_staged")
                s_oh = sem(name + "_operands_ready")
                s_mm = sem(name + "_block_summed")
                s_f = sem(name + "_own_added")
                s_s = sem(name + "_sums_ready")
                if not first:
                    LN = 12
                    tiles = norm_tiles(name, ph)
                    mean, var, inv, cen, sq = tiles
                    hs = sb(name + "_h", [BP, TN, C + 1], F32, ph)
                    far = sb(name + "_far", [P, 2, G, BP], F32, ph)
                    s_far = sem(name + "_distances")
                    s_hot = sem(name + "_onehot_ready")
                    s_ln = sem(name + "_norm_chain")
                    s_root = sem(name + "_root_ready")
                    s_hst = sem(name + "_h_stored")
                if first:
                    sumT = sb(name + "_sumT", [BC + COLS, 2, BP], F32, ph)
                    post = sb(name + "_post", [BP, 2, COLS * H], F32, ph)
                    p_t = ps(name + "_p_t", [P, 2, 512], ph)
                    p_z = ps(name + "_p_z", [P, 2, 2, 512], ph)
                    s_dv = sem(name + "_dinv_placed")
                    s_t = sem(name + "_turned")
                    s_tc = sem(name + "_turned_copied")
                    s_z = sem(name + "_product")
                    s_y = [sem(name + "_result_vector"), sem(name + "_result_scalar")]
                    s_st = [sem(f"{name}_stored{u}") for u in range(2)]
                with nc.Block() as block:
                    @block.gpsimd
                    def _(pool):
                        gather_blocks(pool, yn_tab, rows, idx, s_ix, s_g, s_oh)

                    @block.vector
                    def _(dve):
                        def operands(b):
                            dve.wait_ge(s_sc, b.n + 1)
                            if b.from_(2):
                                dve.wait_ge(s_mm, b.n - 1)
                            if first:
                                dve.tensor_tensor(
                                    oh[:, b.slot, :, :], nodes[:, 0:BP].rearrange("p (a n) -> p a n", a=1)
                                    .broadcast_to([P, G, BP]), spread(sc[:, b.slot, PN:PN + G], P, G, BP), ALU.is_equal)
                            dve.wait_ge(s_g[b.slot], (b.round + 1) * 16 * G)
                            dve.tensor_tensor(
                                rowx[:, b.par, :, :].rearrange("p g (c f) -> p g c f", f=C),
                                rows[:, b.slot, :, :].rearrange("p g (a f) -> p g a f", a=1).broadcast_to([P, G, COLS, C]),
                                sc[:, b.slot, WNC:WNC + G * COLS].rearrange("p (g c a) -> p g c a", g=G, a=1)
                                .broadcast_to([P, G, COLS, C]), ALU.mult).then_inc(s_oh, 1)

                        def link(ins, j, k):
                            ins.then_inc(s_ln, 1)
                            if k < 11:
                                dve.wait_ge(s_ln, j * LN + k)
                            else:
                                hold(dve, s_ln, j * LN + k)

                        def hidden(j):
                            def vec(k):
                                return v_rel[0:BP, k * C:(k + 1) * C].rearrange("p (a f) -> p a f", a=1
                                                                               ).broadcast_to([BP, TN, C])
                            dve.wait_ge(s_root, j + 1)
                            if not isinstance(j, int) or j >= 1:
                                dve.wait_ge(s_hst, 16 * j)
                            link(dve.reciprocal(inv[:, :], inv[:, :]), j, 7)
                            link(dve.scalar_tensor_tensor(out=hs[:, :, 0:C], in0=cen[:, :, :], scalar=0.0,
                                                          in1=spread(inv[:, :], BP, TN, C), op0=ALU.max, op1=ALU.mult),
                                 j, 8)
                            link(dve.tensor_tensor(sq[:, :, :], hs[:, :, 0:C], vec(0), ALU.mult), j, 9)
                            link(dve.tensor_reduce(hs[:, :, C], sq[:, :, :], AX.X, ALU.add), j, 10)
                            link(dve.tensor_tensor(sq[:, :, :], hs[:, :, 0:C], vec(2), ALU.mult), j, 11)
                            link(dve.tensor_reduce(drow3[:, bass.ds(j * UNROLL, UNROLL), :],
                                                   sq[:, :, :].rearrange("p (b c) f -> p b c f", c=COLS),
                                                   AX.X, ALU.add), j, 12)

                        def step(t):
                            if t.has():
                                operands(t)
                            b = t.back(1)
                            if b.has():
                                dve.wait_ge(s_mm, b.n + 1)
                                dve.scalar_tensor_tensor(out=s1[:, b.par, :], in0=Y[:, bass.ds(b.n * BC, BC)], scalar=2.0,
                                                         in1=acc[0:BP, b.par, 0:BC], op0=ALU.mult, op1=ALU.add
                                                         ).then_inc(s_f, 1)
                                if first and b.from_(4):
                                    dve.wait_ge(s_t, b.n - 3)
                                dve.wait_ge(s_f, b.n + 1)
                                by = QN if first else DN
                                dve.tensor_tensor(s2[:, b.slot, 0:BC].rearrange("p (c f) -> p c f", f=C),
                                                  s1[:, b.par, :].rearrange("p (c f) -> p c f", f=C),
                                                  spread(sc[0:BP, b.slot, by:by + COLS], BP, COLS, C), ALU.mult
                                                  ).then_inc(s_s, 1)
                                if first:
                                    x3 = X[:, bass.ds(b.n * BC, BC)].rearrange("p (c f) -> p c f", f=C)
                                    dve.tensor_tensor(x3, x3, bias3[0:BP, :].rearrange("p (a f) -> p a f", a=1)
                                                      .broadcast_to([BP, COLS, C]), ALU.add)
                                else:
                                    x_ = X[:, bass.ds(b.n * BC, BC)]
                                    dve.wait_ge(s_s, b.n + 1)
                                    dve.tensor_tensor(x_, x_, s2[:, b.slot, 0:BC], ALU.add)
                            if not first:
                                if t.slot == 3 and t.back(11).has():
                                    hidden(t.back(11).round)
                                if t.slot == 0 and t.back(8).has():
                                    centre(dve, link, t.back(8).round, tiles)
                                if t.slot == 1 and t.back(9).has():
                                    variance(dve, link, t.back(9).round, tiles)
                            b = t.back(4)
                            if first and b.has():
                                dve.wait_ge(s_z, b.n + 1)
                                if b.from_(2):
                                    dve.wait_ge(s_st[b.par], 16 * b.round2)
                                dve.tensor_scalar(post[:, b.par, 0:CUT * H], p_z[0:BP, b.par, 0, 0:CUT * H],
                                                  0.0, None, ALU.max).then_inc(s_y[0], 1)
                        run_steps(dve, step, drain=4 if first else 8, head=HEAD if first else HEAD + UNROLL)

                    @block.tensor
                    def _(pe):
                        def step(t):
                            if t.has():
                                hold(pe, s_oh, t.n + 1)
                                if not first:
                                    hold(pe, s_hot, t.n + 1)
                                if t.from_(2):
                                    hold(pe, s_f, t.n - 1)
                                for g in range(G):
                                    mm = pe.matmul(acc[0:BP, t.par, 0:BC], oh[:, t.slot, g, :], rowx[:, t.par, g, :],
                                                   start=g == 0, stop=g == G - 1)
                                mm.then_inc(s_mm, 1)
                            b = t.back(2)
                            if first and b.has():
                                hold(pe, s_s, b.n + 1)
                                hold(pe, s_dv, b.n + 1)
                                if b.from_(2):
                                    hold(pe, s_tc, b.n - 1)
                                pe.transpose(p_t[0:BC + COLS, b.par, 0:BP], s2[:, b.slot, :], ident[0:BP, 0:BP]
                                             ).then_inc(s_t, 1)
                            b = t.back(3)
                            if first and b.has():
                                hold(pe, s_tc, b.n + 1)
                                if b.from_(2):
                                    hold(pe, s_y[0], b.n - 1)
                                    hold(pe, s_y[1], b.n - 1)
                                pe.matmul(p_z[0:BP, b.par, 0, 0:CUT * H], sumT[:, b.par, :], W0x[:, 0:CUT * H],
                                          start=True, stop=True)
                                pe.matmul(p_z[0:BP, b.par, 1, 0:(COLS - CUT) * H], sumT[:, b.par, :],
                                          W0x[:, CUT * H:], start=True, stop=True).then_inc(s_z, 1)
                        run_steps(pe, step, drain=3 if first else 0)

                    @block.scalar
                    def _(act):
                        def stage(b):
                            if b.from_(4):
                                hold(act, s_s, b.n - 3)
                                if not first:
                                    hold(act, s_hot, b.n - 3)
                            act.copy(sc[:, b.slot, :], scalars_of(b, DI, KS)).then_inc(s_sc, 1)

                        def onehot(b):
                            hold(act, s_sc, b.n + 1)
                            if b.from_(2):
                                hold(act, s_hot, b.n - 1)
                            for g in range(G):
                                ins = act.activation(far[:, b.par, g, :], nodes[:, 0:BP], ACT.Abs, scale=-1.0,
                                                     bias=sc[:, b.slot, PN + g:PN + g + 1])
                            ins.then_inc(s_far, 1)
                            if b.from_(4):
                                hold(act, s_mm, b.n - 3)
                            hold(act, s_far, b.n + 1)
                            act.activation(oh[:, b.slot, :, :], far[:, b.par, :, :], ACT.Relu, scale=-1.0,
                                           bias=ones[:, 0:1]).then_inc(s_hot, 1)

                        def step(t):
                            place_indices(act, t.back(-3), idx, s_ix, s_g)
                            if t.back(-1).has():
                                stage(t.back(-1))
                                if not first:
                                    onehot(t.back(-1))
                            if first and t.has():
                                if t.from_(4):
                                    hold(act, s_t, t.n - 3)
                                hold(act, s_sc, t.n + 1)
                                act.copy(s2[:, t.slot, BC:BC + COLS], sc[0:BP, t.slot, DN:DN + COLS]).then_inc(s_dv, 1)
                            b = t.back(2)
                            if first and b.has():
                                hold(act, s_t, b.n + 1)
                                if b.from_(2):
                                    hold(act, s_z, b.n - 1)
                                act.copy(sumT[:, b.par, :], p_t[0:BC + COLS, b.par, 0:BP]).then_inc(s_tc, 1)
                            b = t.back(4)
                            if first and b.has():
                                hold(act, s_z, b.n + 1)
                                if b.from_(2):
                                    hold(act, s_st[b.par], 16 * b.round2)
                                act.activation(post[:, b.par, CUT * H:COLS * H], p_z[0:BP, b.par, 1, 0:(COLS - CUT) * H],
                                               ACT.Relu).then_inc(s_y[1], 1)
                            if not first:
                                if t.slot == 3 and t.back(11).has():
                                    act.wait_ge(s_ln, t.back(11).round * LN + 6)
                                    act.activation(inv[:, :], var[:, :], ACT.Sqrt).then_inc(s_root, 1)
                        for b in range(3):
                            place_indices(act, Step(0, b), idx, s_ix, s_g)
                        stage(Step(0, 0))
                        if not first:
                            onehot(Step(0, 0))
                        run_steps(act, step, ahead=1, drain=4 if first else 8, head=HEAD if first else HEAD + UNROLL)

                    if not first:
                        @block.sync
                        def _(sp):
                            with sp.Fori(0, NB // UNROLL) as j:
                                sp.wait_ge(s_ln, j * LN + 10)
                                sp.dma_start(blocks(h_tab[bass.ds(j * UNROLL * BN, UNROLL * BN), :]),
                                             hs[:, :, :].rearrange("p (b c) f -> p b (c f)", c=COLS)).then_inc(s_hst, 16)
                            sp.wait_ge(s_hst, 16 * (NB // UNROLL))

                    if first:
                        @block.sync
                        def _(sp):
                            def step(b):
                                sp.wait_ge(s_y[0], b.n + 1)
                                sp.wait_ge(s_y[1], b.n + 1)
                                sp.dma_start(rows_of(y1_tab, b), post[:, b.par, :]).then_inc(s_st[b.par], 16)
                            run_steps(sp, step)
                            for u in range(2):
                                sp.wait_ge(s_st[u], 16 * (NB // 2))

        narrow_layer("l0", True)

        def wide_layer(name, tab, Wt, y_out):
            narrow = y_out is None
            KW = DQ
            at = [sum(hi - lo for lo, hi in SPAN[:g]) for g in range(G + 1)]
            with ExitStack() as ph:
                rows = sb(name + "_rows", [P, 4, G, H], F32, ph)
                idx = sb(name + "_idx", [P, 4, G], I32, ph)
                sc = sb(name + "_scalars", [P, 4, KW], F32, ph)
                oh = sb(name + "_oh", [P, 2, at[G]], F32, ph)
                own = sb(name + "_own", [BP, 2, COLS * H], F32, ph)
                ownT = sb(name + "_ownT2", [P, 2, COLS, BP], F32, ph)
                sumT = sb(name + "_sumT", [P, 2, COLS, BP], F32, ph)
                pre = sb(name + "_pre", [BP, 2, COLS * H], F32, ph)
                post = sb(name + "_post", [P, 2, COLS, BP] if narrow else [BP, 2, COLS, H], F32, ph)
                p_sum = ps(name + "_p_sum", [P, 1024], ph)
                p_own = ps(name + "_p_own", [P, 1024], ph)
                p_z = ps(name + "_p_z", [P, 1024], ph)
                p_h = ps(name + "_p_h", [P, 1024], ph) if narrow else None
                s_ix = sem(name + "_index_ready")
                s_g = [sem(f"{name}_rows_gathered{u}") for u in range(4)]
                s_sc = sem(name + "_scalars_staged")
                s_own = [sem(f"{name}_own_loaded{u}") for u in range(2)]
                s_oh = sem(name + "_onehot_ready")
                s_mm = sem(name + "_block_summed")
                s_turn = sem(name + "_own_turned")
                s_twice = sem(name + "_own_copied")
                s_T = sem(name + "_sums_ready")
                s_z = sem(name + "_product")
                s_e = sem(name + "_preactivation")
                s_post = sem(name + "_activated")
                if narrow:
                    s_h = sem(name + "_hidden_turned")
                    s_y = sem(name + "_narrow_product")
                    s_p = sem(name + "_narrow_rows")
                    s_y3 = sem(name + "_narrow_rows_stored")
                else:
                    s_st = [sem(f"{name}_stored{u}") for u in range(2)]

                def chunks(ap):
                    return ap[:, 0:COLS * P].rearrange("f (c p) -> f c p", c=COLS)[:, :, 0:BP]

                with nc.Block() as block:
                    @block.gpsimd
                    def _(pool):
                        gather_blocks(pool, tab, rows, idx, s_ix, s_g, s_mm)

                    @block.sync
                    def _(sp):
                        def load(b, own_tab):
                            if b.from_(2):
                                sp.wait_ge(s_turn, b.n - 1)
                            sp.dma_start(own[:, b.par, :], rows_of(own_tab, b)).then_inc(s_own[b.par], 16)
                            if narrow and b.slot == 3 and b.back(11).has():
                                store(b.back(11))

                        def store(b):
                            sp.wait_ge(s_p, b.n + UNROLL)
                            sp.dma_start(blocks(yn_tab[bass.ds(b.n * BN, UNROLL * BN), :]),
                                         Y[:, bass.ds(b.n * BC, UNROLL * BC)].rearrange("p (b g) -> p b g", g=BC)
                                         ).then_inc(s_y3, 16)
                        with sp.If(uncovered(sp)):
                            run_steps(sp, lambda b: load(b, u_tab))
                        with sp.Else():
                            run_steps(sp, lambda b: load(b, tab))
                        if narrow:
                            for n in range(NB - HEAD, NB, UNROLL):
                                store(Step(0, n))
                            sp.wait_ge(s_y3, 16 * (NB // UNROLL))

                    @block.vector
                    def _(dve):
                        def onehot(b):
                            dve.wait_ge(s_sc, b.n + 1)
                            if b.from_(2):
                                dve.wait_ge(s_mm, b.n - 1)
                            for g, (lo, hi) in enumerate(SPAN):
                                ins = dve.tensor_scalar(oh[:, b.par, at[g]:at[g + 1]], nodes[:, lo:hi],
                                                        sc[:, b.slot, D0 + g:D0 + g + 1], sc[:, b.slot, W0_ + g:W0_ + g + 1],
                                                        ALU.is_equal, ALU.mult)
                            ins.then_inc(s_oh, 1)

                        def step(t):
                            if t.has():
                                dve.wait_ge(s_mm, t.n + 1)
                                dve.wait_ge(s_twice, t.n + 1)
                                if t.from_(2):
                                    dve.wait_ge(s_z, t.n - 1)
                                for lo, hi, bank in ((0, HALF // COLS, 0), (HALF // COLS, BP, 512)):
                                    ins = dve.tensor_tensor(
                                        sumT[:, t.par, :, lo:hi],
                                        p_sum[:, bank:bank + (hi - lo) * COLS].rearrange("f (p c) -> f c p", c=COLS),
                                        ownT[:, t.par, :, lo:hi], ALU.add)
                                ins.then_inc(s_T, 1)
                            b = t.back(3)
                            if narrow and b.has():
                                dve.wait_ge(s_y, b.n + 1)
                                dve.tensor_tensor(
                                    Y[:, bass.ds(b.n * BC, BC)].rearrange("p (c f) -> p c f", f=C),
                                    p_h[0:BP, COLS * P:COLS * P + BC].rearrange("p (c f) -> p c f", f=C),
                                    spread(scalars_of(b, DI, DI + COLS, parts=BP), BP, COLS, C), ALU.mult
                                    ).then_inc(s_p, 1)
                            b = t.back(1)
                            if b.has():
                                dve.wait_ge(s_z, b.n + 1)
                                if b.from_(2):
                                    dve.wait_ge(s_h if narrow else s_post, b.n - 1)
                                if narrow:
                                    dve.tensor_tensor(
                                        pre[:, b.par, :].rearrange("p (c f) -> p c f", f=H),
                                        p_z[0:BP, 0:COLS * H].rearrange("p (c f) -> p c f", f=H),
                                        spread(sc[0:BP, b.slot, DI:DI + COLS], BP, COLS, H), ALU.mult).then_inc(s_e, 1)
                                else:
                                    for c in range(COLS):
                                        ins = dve.scalar_tensor_tensor(
                                            out=pre[:, b.par, c * H:(c + 1) * H], in0=p_z[0:BP, c * H:(c + 1) * H],
                                            scalar=sc[0:BP, b.slot, DI + c:DI + c + 1], in1=bias1[0:BP, :],
                                            op0=ALU.mult, op1=ALU.add)
                                    ins.then_inc(s_e, 1)
                            if t.back(-2).has():
                                onehot(t.back(-2))
                        onehot(Step(0, 0))
                        onehot(Step(0, 1))
                        run_steps(dve, step, ahead=1, drain=3)

                    @block.tensor
                    def _(pe):
                        def sums(b):
                            hold(pe, s_own[b.par], (b.round2 + 1) * 16)
                            if b.from_(1):
                                hold(pe, s_twice, b.n)
                            for c in range(COLS):
                                mm = pe.transpose(p_own[:, c * P:c * P + BP], own[:, b.par, c * H:(c + 1) * H],
                                                  ident[0:BP, 0:BP])
                            mm.then_inc(s_turn, 1)
                            hold(pe, s_oh, b.n + 1)
                            hold(pe, s_g[b.slot], (b.round + 1) * 16 * G)
                            if b.from_(1):
                                hold(pe, s_T, b.n)
                            parts = ((1, 1, HALF, BN), (0, 0, 0, HALF), (1, 0, HALF, SPAN[0][1]),
                                     (0, 1, SPAN[1][0], HALF), (1, 2, SPAN[2][0], BN))
                            for k, (bank, g, lo, hi) in enumerate(parts):
                                out_at = 512 * bank + lo - HALF * bank
                                oh_at = at[g] + lo - SPAN[g][0]
                                mm = pe.matmul(p_sum[:, out_at:out_at + hi - lo], rows[:, b.slot, g, :],
                                               oh[:, b.par, oh_at:oh_at + hi - lo], start=k < 2, stop=k > 2)
                            mm.then_inc(s_mm, 1)

                        def step(t):
                            if t.back(-1).has():
                                sums(t.back(-1))
                            b = t.back(2)
                            if narrow and b.has():
                                hold(pe, s_post, b.n + 1)
                                for c in range(COLS):
                                    mm = pe.matmul(p_h[0:BP, COLS * P + c * C:COLS * P + (c + 1) * C],
                                                   post[:, b.par, c, :], W3[:, :], start=True, stop=True)
                                mm.then_inc(s_y, 1)
                            if t.has():
                                hold(pe, s_T, t.n + 1)
                                if t.from_(1):
                                    hold(pe, s_e, t.n)
                                for c in range(COLS):
                                    mm = pe.matmul(p_z[0:BP, c * H:(c + 1) * H], sumT[:, t.par, c, :], Wt[:, :],
                                                   start=True, stop=True)
                                mm.then_inc(s_z, 1)
                            b = t.back(1)
                            if narrow and b.has():
                                hold(pe, s_e, b.n + 1)
                                if b.from_(1):
                                    hold(pe, s_p, b.n)
                                for c in range(COLS):
                                    mm = pe.transpose(p_h[:, c * P:c * P + BP], pre[:, b.par, c * H:(c + 1) * H],
                                                      ident[0:BP, 0:BP])
                                mm.then_inc(s_h, 1)
                        sums(Step(0, 0))
                        run_steps(pe, step, ahead=1, drain=2)

                    @block.scalar
                    def _(act):
                        def stage(b):
                            if b.from_(4):
                                hold(act, s_e, b.n - 3)
                            act.copy(sc[:, b.slot, :], scalars_of(b, 0, KW)).then_inc(s_sc, 1)

                        def twice(b):
                            hold(act, s_turn, b.n + 1)
                            if b.from_(2):
                                hold(act, s_T, b.n - 1)
                            act.mul(ownT[:, b.par, :, :], chunks(p_own), 2.0).then_inc(s_twice, 1)

                        def step(t):
                            place_indices(act, t.back(-3), idx, s_ix, s_g)
                            if not narrow and t.back(-2).has():
                                stage(t.back(-2))
                            if t.back(-1).has():
                                twice(t.back(-1))
                            if narrow and t.back(-3).has():
                                stage(t.back(-3))
                            b = t.back(1)
                            if not b.has():
                                return
                            if narrow:
                                hold(act, s_h, b.n + 1)
                                if b.from_(2):
                                    hold(act, s_y, b.n - 1)
                                act.activation(post[:, b.par, :, :], chunks(p_h), ACT.Relu,
                                               bias=bias2[:, 0:1]).then_inc(s_post, 1)
                                return
                            hold(act, s_e, b.n + 1)
                            hold(act, s_sc, b.n + 1)
                            if b.from_(2):
                                hold(act, s_st[b.par], 16 * b.round2)
                            for c in range(COLS):
                                ins = act.activation(post[:, b.par, c, :], pre[:, b.par, c * H:(c + 1) * H], ACT.Relu,
                                                     scale=sc[0:BP, b.slot, DI + c:DI + c + 1])
                            ins.then_inc(s_post, 1)
                            act.wait_ge(s_post, b.n + 1)
                            act.dma_start(rows_of(y_out, b), post[:, b.par, :, :].rearrange("p c f -> p (c f)")
                                          ).then_inc(s_st[b.par], 16)
                        for b in range(3):
                            place_indices(act, Step(0, b), idx, s_ix, s_g)
                        stage(Step(0, 0))
                        stage(Step(0, 1))
                        if narrow:
                            stage(Step(0, 2))
                        twice(Step(0, 0))
                        run_steps(act, step, ahead=1, drain=1)
                        if not narrow:
                            for u in range(2):
                                act.wait_ge(s_st[u], 16 * (NB // 2))

        own_wide = u_tab[0:N, :]
        general_path("g1g", H, u_tab, [(own_wide, y1_tab)], [], tab=y1_tab)
        wide_layer("l1", y1_tab, W1, y2_tab)
        general_path("g2g", H, u_tab, [(own_wide, y2_tab)], [], tab=y2_tab)
        wide_layer("l2", y2_tab, W2, None)

        general_path("g3g", C, sum_tab, [(sum_rows, Yb)], [(Yb, sum_rows)], tab=yn_tab)
        narrow_layer("l3", False)

        general_path("grg", C, sum_tab, [(sum_rows, Xb), (dot_tab.rearrange(nodes_of, p=BP, c=COLS), drow3)],
                     [(Xb, sum_rows)], tab=h_tab, dots=True)
        with ExitStack() as ph:
            rows = sb("rl_rows", [P, 4, G, C + 1], F32, ph)
            idx = sb("rl_idx", [P, 4, G], I32, ph)
            sc = sb("rl_scalars", [P, 4, RD], F32, ph)
            oh = sb("rl_oh", [P, 4, G, BP], F32, ph)
            far = sb("rl_far", [P, 2, G, BP], F32, ph)
            typ = sb("rl_type", [P, 2, G, R], F32, ph)
            typT = sb("rl_typeT", [R, 2, G * P], F32, ph)
            prod = sb("rl_prod", [P, G, C, C], F32, ph)
            coef = sb("rl_coef", [P, G], F32, ph)
            msg = sb("rl_msg", [P, G, 2, C], F32, ph)
            msgx = sb("rl_msgx", [P, 2, G, COLS, 2 * C], F32, ph)
            d_u = sb("rl_d_times_sum", [BP, 2, COLS, C], F32, ph)
            p_t = ps("rl_p_t", [P, 2, 512], ph)
            p_w = ps("rl_p_w", [P, 2, 1024], ph)
            acc = ps("rl_acc", [P, 2, 512], ph)
            s_ix = sem("rl_index_ready")
            s_g = [sem(f"rl_rows_gathered{k}") for k in range(4)]
            s_sc = sem("rl_scalars_staged")
            s_far = sem("rl_distances")
            s_oh = sem("rl_onehot_ready")
            s_ty = sem("rl_types_compared")
            s_tt = sem("rl_types_turned")
            s_tc = sem("rl_types_copied")
            s_w = sem("rl_matrices_selected")
            s_pr = sem("rl_products")
            s_co = sem("rl_coefficients")
            s_u = sem("rl_rows_times_matrix")
            s_ue = sem("rl_rows_weighted")
            s_m = sem("rl_messages_ready")
            s_mm = sem("rl_block_summed")
            s_du = sem("rl_dst_part")
            s_out = sem("out_stored")
            s_f = sem("rl_result_ready")
            with nc.Block() as block:
                @block.gpsimd
                def _(pool):
                    gather_blocks(pool, h_tab, rows, idx, s_ix, s_g, s_m)

                @block.sync
                def _(sp):
                    with sp.Fori(0, NB // UNROLL) as j:
                        sp.wait_ge(s_f, j * UNROLL + UNROLL)
                        sp.dma_start(blocks(out[bass.ds(j * UNROLL * BN, UNROLL * BN), :]),
                                     X[:, bass.ds(j * UNROLL * BC, UNROLL * BC)].rearrange("p (b g) -> p b g", g=BC)
                                     ).then_inc(s_out, 16)
                    sp.wait_ge(s_out, 16 * (NB // UNROLL))

                @block.scalar
                def _(act):
                    def stage(b):
                        if b.from_(4):
                            hold(act, s_m, b.n - 3)
                            hold(act, s_oh, b.n - 3)
                        act.copy(sc[:, b.slot, :], scalars_of(b, 0, RD, tab=scal_rel)).then_inc(s_sc, 1)

                    def step(t):
                        place_indices(act, t.back(-3), idx, s_ix, s_g)
                        if t.back(-1).has():
                            stage(t.back(-1))
                        if t.has():
                            hold(act, s_tt, t.n + 1)
                            if t.from_(2):
                                hold(act, s_w, t.n - 1)
                            act.copy(typT[:, t.par, :], p_t[0:R, t.par, 0:G * P]).then_inc(s_tc, 1)
                        b = t.back(1)
                        if b.has():
                            hold(act, s_sc, b.n + 1)
                            if b.from_(2):
                                hold(act, s_oh, b.n - 1)
                            for g in range(G):
                                ins = act.activation(far[:, b.par, g, :], nodes[:, 0:BP], ACT.Abs,
                                                     bias=sc[:, b.slot, RP + g:RP + g + 1])
                            ins.then_inc(s_far, 1)
                            if b.from_(4):
                                hold(act, s_mm, b.n - 3)
                            hold(act, s_far, b.n + 1)
                            act.activation(oh[:, b.slot, :, :], far[:, b.par, :, :], ACT.Relu, scale=-1.0,
                                           bias=ones[:, 0:1]).then_inc(s_oh, 1)
                    for b in range(3):
                        place_indices(act, Step(0, b), idx, s_ix, s_g)
                    stage(Step(0, 0))
                    run_steps(act, step, ahead=1, drain=1)

                @block.vector
                def _(dve):
                    def operands(b):
                        dve.wait_ge(s_sc, b.n + 1)
                        if b.from_(2):
                            dve.wait_ge(s_tt, b.n - 1)
                        dve.tensor_tensor(
                            typ[:, b.par, :, :], nodes[:, 0:R].rearrange("p (a r) -> p a r", a=1).broadcast_to([P, G, R]),
                            spread(sc[:, b.slot, RT:RT + G], P, G, R), ALU.is_equal).then_inc(s_ty, 1)

                    def step(t):
                        if t.has():
                            operands(t)
                        b = t.back(2)
                        if b.has():
                            products(b)
                        if t.back(3).has():
                            add_sums(t.back(3))
                        if b.has():
                            messages(b)
                        if t.back(3).has():
                            finish(t.back(3))
                        if b.has():
                            place(b)

                    def products(b):
                        dve.wait_ge(s_g[b.slot], (b.round + 1) * 16 * G)
                        dve.wait_ge(s_w, b.n + 1)
                        dve.tensor_tensor(
                            prod[:, :, :, :], p_w[:, b.par, 0:G * C * C].rearrange("p (g o i) -> p g o i", g=G, o=C),
                            rows[:, b.slot, :, 0:C].rearrange("p g (a i) -> p g a i", a=1).broadcast_to([P, G, C, C]),
                            ALU.mult).then_inc(s_pr, 1)
                        dve.tensor_tensor(coef[:, :], rows[:, b.slot, :, C], sc[:, b.slot, RE:RE + G], ALU.add).then_inc(s_co, 1)
                        dve.wait_ge(s_pr, b.n + 1)
                        dve.tensor_reduce(msg[:, :, 1, :], prod[:, :, :, :], AX.X, ALU.add).then_inc(s_u, 1)

                    def messages(b):
                        dve.wait_ge(s_u, b.n + 1)
                        dve.wait_ge(s_co, b.n + 1)
                        dve.tensor_tensor(msg[:, :, 0, :], msg[:, :, 1, :], spread(coef[:, :], P, G, C), ALU.mult
                                          ).then_inc(s_ue, 1)

                    def place(b):
                        if b.from_(2):
                            dve.wait_ge(s_mm, b.n - 1)
                        dve.wait_ge(s_ue, b.n + 1)
                        dve.tensor_tensor(
                            msgx[:, b.par, :, :, :],
                            msg[:, :, :, :].rearrange("p g (a k) f -> p g a (k f)", a=1).broadcast_to([P, G, COLS, 2 * C]),
                            sc[:, b.slot, RC:RC + G * COLS].rearrange("p (g c a) -> p g c a", g=G, a=1)
                            .broadcast_to([P, G, COLS, 2 * C]), ALU.mult).then_inc(s_m, 1)

                    def add_sums(b):
                        a4 = acc[0:BP, b.par, 0:2 * BC].rearrange("p (c k f) -> p c k f", c=COLS, k=2)
                        dve.wait_ge(s_mm, b.n + 1)
                        dve.tensor_tensor(d_u[:, b.par, :, :], a4[:, :, 1, :], spread(drow3[:, bass.ds(b.n, 1), :].rearrange("p b c -> p (b c)"), BP, COLS, C),
                                          ALU.mult).then_inc(s_du, 1)

                    def finish(b):
                        x3 = X[:, bass.ds(b.n * BC, BC)].rearrange("p (c f) -> p c f", f=C)
                        a4 = acc[0:BP, b.par, 0:2 * BC].rearrange("p (c k f) -> p c k f", c=COLS, k=2)
                        dve.wait_ge(s_du, b.n + 1)
                        dve.tensor_tensor(x3, a4[:, :, 0, :], d_u[:, b.par, :, :], ALU.add).then_inc(s_f, 1)

                    run_steps(dve, step, drain=3)

                @block.tensor
                def _(pe):
                    def step(t):
                        b = t.back(3)
                        if b.has():
                            hold(pe, s_m, b.n + 1)
                            hold(pe, s_oh, b.n + 1)
                            if b.from_(2):
                                hold(pe, s_f, b.n - 1)
                            for g in range(G):
                                mm = pe.matmul(acc[0:BP, b.par, 0:2 * BC], oh[:, b.slot, g, :],
                                               msgx[:, b.par, g, :, :].rearrange("p c f -> p (c f)"),
                                               start=g == 0, stop=g == G - 1)
                                if g == 0:
                                    pe.matmul(acc[0:BP, b.par, 0:2 * BC]
                                              .rearrange("p (c k f) -> p c k f", c=COLS, k=2)[:, :, 0, :],
                                              ident[0:BP, 0:BP], X[:, bass.ds(b.n * BC, BC)]
                                              .rearrange("p (c f) -> p c f", f=C), start=False, stop=False)
                            mm.then_inc(s_mm, 1)
                        if t.has():
                            hold(pe, s_ty, t.n + 1)
                            if t.from_(2):
                                hold(pe, s_tc, t.n - 1)
                            for g in range(G):
                                mm = pe.transpose(p_t[0:R, t.par, g * P:(g + 1) * P], typ[:, t.par, g, :], ident[:, :])
                            mm.then_inc(s_tt, 1)
                        b = t.back(1)
                        if b.has():
                            hold(pe, s_tc, b.n + 1)
                            if b.from_(2):
                                hold(pe, s_pr, b.n - 1)
                            for g in range(G):
                                mm = pe.matmul(p_w[:, b.par, g * C * C:(g + 1) * C * C],
                                               typT[:, b.par, g * P:(g + 1) * P], Wr[:, :], start=True, stop=True)
                            mm.then_inc(s_w, 1)
                    run_steps(pe, step, drain=3)


_INS = ["x", "src", "dst", "edge_attr_16", "edge_type_90", "edge_weight", "L0_gnn_w0", "L0_gnn_b0", "L0_gnn_w1",
        "L0_gnn_b1", "L0_gnn_w2", "L0_gnn_b2", "L0_gnn_w3", "L0_gnn_b3", "L1_gnn_Ws", "L1_gnn_Wa", "L1_gnn_weight",
        "L1_gnn_w_comp"]


def kernel(**inputs):
    import concourse.bacc as bacc
    from concourse.bass_utils import run_bass_kernel_spmd as run

    nc = bacc.Bacc("TRN2", target_bir_lowering=False, num_devices=1)
    arrays, args = {}, []
    for name in _INS:
        a = np.ascontiguousarray(inputs[name])
        arrays["in_" + name] = a
        args.append(nc.dram_tensor("in_" + name, a.shape, mybir.dt.from_np(a.dtype), kind="ExternalInput").ap())
    o = nc.dram_tensor("out_0", (N, C), F32, kind="ExternalOutput").ap()
    build(nc, *args, o)
    return run(nc, [arrays], core_ids=[0]).results[0]["out_0"]
```
